# Optimizing a Trainium2 kernel written in Bass

```python
import numpy as np
import jax
import jax.numpy as jnp

def _softmax(x, axis=-1):
    return jax.nn.softmax(x, axis=axis)

def _gelu(x):
    return jax.nn.gelu(x, approximate=True)

def _silu(x):
    return jax.nn.silu(x)

def _sigmoid(x):
    return jax.nn.sigmoid(x)

def _layernorm(x, axis=-1, eps=1e-05):
    m = jnp.mean(x, axis=axis, keepdims=True)
    v = jnp.var(x, axis=axis, keepdims=True)
    return (x - m) / jnp.sqrt(v + eps)

def _scatter_add(tgt, idx, src, axis=0):
    return tgt.at[idx].add(src)

def _segment_sum(src, seg, n):
    return jax.ops.segment_sum(src, seg, n)
kernel_name = 'mk_gps_d1_gnn_r8_ada6f0'

def setup_inputs(seed: int=0):
    np.random.seed(seed)
    _w = jnp.asarray

    def _rec_inputs():
        import jax
        import jax.numpy as jnp
        _gk = jax.random.key(seed)
        x = -0.0002117 + 1 * jax.random.normal(jax.random.fold_in(_gk, 1), (6250, 256), jnp.float32)
        _s = jax.random.randint(jax.random.fold_in(_gk, 2), (100000,), 0, 6250, jnp.int32)
        _d = jax.random.randint(jax.random.fold_in(_gk, 3), (100000,), 0, 6250, jnp.int32)
        _loop = jnp.arange(6250, dtype=jnp.int32)
        src = jnp.concatenate([_s, _d, _loop])
        dst = jnp.concatenate([_d, _s, _loop])
        _o = jnp.argsort(dst, stable=True)
        src = src[_o]
        dst = dst[_o]
        return (x, src, dst)
    x, src, dst = _rec_inputs()

    def _L0_gnn_setup():
        import jax, jax.numpy as jnp
        import numpy as np
        V = 12500
        E = 37500
        D = 256
        BN_EPS = 1e-05
        key = jax.random.key(seed)
        ks = jax.random.split(key, 8)
        features = jax.random.normal(ks[0], (V, D), dtype=jnp.float32)
        edges = jax.random.randint(ks[1], (E, 2), 0, V, dtype=jnp.int64)
        s = 1.0 / np.sqrt(D)
        W0 = jax.random.normal(ks[2], (D, D), dtype=jnp.float32) * s
        b0 = jax.random.normal(ks[3], (D,), dtype=jnp.float32) * s
        W1 = jax.random.normal(ks[4], (D, D), dtype=jnp.float32) * s
        b1 = jax.random.normal(ks[5], (D,), dtype=jnp.float32) * s
        gamma = jnp.ones((D,), dtype=jnp.float32)
        beta = jnp.zeros((D,), dtype=jnp.float32)
        return {'features': features, 'edges': edges, 'W0': W0, 'b0': b0, 'W1': W1, 'b1': b1, 'gamma': gamma, 'beta': beta}
    _L0_gnn_all = _L0_gnn_setup()
    _L0_gnn_in = {k: v for k, v in _L0_gnn_all.items() if k in ('W0', 'b0', 'W1', 'b1', 'gamma', 'beta')}
    del _L0_gnn_all

    def _L0_mix_setup():
        import jax, jax.numpy as jnp
        import numpy as np
        EMB, HEADS, DEPTH, SEQ, BATCH = (256, 8, 4, 1024, 4)
        DH = EMB // HEADS
        FF = 4 * EMB
        EPS = 1e-05

        def _layernorm(x, g, b):
            mu = x.mean(-1, keepdims=True)
            var = ((x - mu) ** 2).mean(-1, keepdims=True)
            return (x - mu) * jax.lax.rsqrt(var + EPS) * g + b

        def _linear_attn(x, Wq, Wk, Wv, Wo, bo):
            b, n, dm = x.shape
            split = lambda t: t.reshape(b, n, HEADS, DH).transpose(0, 2, 1, 3)
            scale = DH ** (-0.25)
            q = jax.nn.softmax(split(x @ Wq) * scale, axis=-1)
            k = jax.nn.softmax(split(x @ Wk) * scale, axis=-2)
            v = split(x @ Wv)
            context = jnp.einsum('bhnd,bhne->bhde', k, v)
            out = jnp.einsum('bhnd,bhde->bhne', q, context)
            out = out.transpose(0, 2, 1, 3).reshape(b, n, dm)
            return out @ Wo + bo

        def _forward(x, Wq, Wk, Wv, Wo, bo, ln1_g, ln1_b, W1, b1, W2, b2, ln2_g, ln2_b):
            for i in range(DEPTH):
                h = _layernorm(x, ln1_g[i], ln1_b[i])
                x = x + _linear_attn(h, Wq[i], Wk[i], Wv[i], Wo[i], bo[i])
                h = _layernorm(x, ln2_g[i], ln2_b[i])
                x = x + (jax.nn.gelu(h @ W1[i] + b1[i], approximate=False) @ W2[i] + b2[i])
            return x
        key = jax.random.key(seed)
        ks = jax.random.split(key, 8)
        w = lambda k, shape: jax.random.normal(k, shape, dtype=jnp.float32) * 0.02
        D = DEPTH
        return {'x': jax.random.normal(ks[0], (BATCH, SEQ, EMB), dtype=jnp.float32), 'Wq': w(ks[1], (D, EMB, EMB)), 'Wk': w(ks[2], (D, EMB, EMB)), 'Wv': w(ks[3], (D, EMB, EMB)), 'Wo': w(ks[4], (D, EMB, EMB)), 'bo': jnp.zeros((D, EMB), jnp.float32), 'ln1_g': jnp.ones((D, EMB), jnp.float32), 'ln1_b': jnp.zeros((D, EMB), jnp.float32), 'W1': w(ks[5], (D, EMB, FF)), 'b1': jnp.zeros((D, FF), jnp.float32), 'W2': w(ks[6], (D, FF, EMB)), 'b2': jnp.zeros((D, EMB), jnp.float32), 'ln2_g': jnp.ones((D, EMB), jnp.float32), 'ln2_b': jnp.zeros((D, EMB), jnp.float32)}
    _L0_mix_all = _L0_mix_setup()
    _L0_mix_in = {k: v for k, v in _L0_mix_all.items() if k in ('Wq', 'Wk', 'Wv', 'Wo', 'bo', 'ln1_g', 'ln1_b', 'W1', 'b1', 'W2', 'b2', 'ln2_g', 'ln2_b')}
    del _L0_mix_all

    def _L0_ffn_setup():
        import jax, jax.numpy as jnp
        import numpy as np
        B, N, D = (16, 512, 256)
        NUM_EXPERTS, TOP_K, HEADS = (4, 2, 4)
        N_EDGES = 131072
        LN_EPS = 1e-05

        def _layernorm(x, g, b):
            mu = x.mean(-1, keepdims=True)
            var = ((x - mu) ** 2).mean(-1, keepdims=True)
            return (x - mu) * jax.lax.rsqrt(var + LN_EPS) * g + b

        def _forward(x, edge_index, W_gat, att_src, att_dst, b_gat, ln_gamma, ln_beta, W1, b1, W2, b2):
            Bc, Nc, Dc = x.shape
            M = Bc * Nc
            x_flat = x.reshape(M, Dc)
            h = (x_flat @ W_gat).reshape(M, HEADS, NUM_EXPERTS)
            loops = jnp.arange(M, dtype=edge_index.dtype)
            src = jnp.concatenate([edge_index[0], loops])
            dst = jnp.concatenate([edge_index[1], loops])
            a_src = (h * att_src).sum(-1)
            a_dst = (h * att_dst).sum(-1)
            e = jax.nn.leaky_relu(a_src[src] + a_dst[dst], negative_slope=0.2)
            e_max = jax.ops.segment_max(e, dst, num_segments=M)
            ee = jnp.exp(e - e_max[dst])
            denom = jax.ops.segment_sum(ee, dst, num_segments=M)
            alpha = ee / (denom[dst] + 1e-16)
            msg = h[src] * alpha[:, :, None]
            agg = jax.ops.segment_sum(msg, dst, num_segments=M).reshape(M, HEADS * NUM_EXPERTS) + b_gat
            scores = _layernorm(agg, ln_gamma, ln_beta).reshape(M, HEADS, NUM_EXPERTS).mean(1)
            scores = scores.reshape(Bc, Nc, NUM_EXPERTS)
            topk_s, topk_i = jax.lax.top_k(scores, TOP_K)
            w = jax.nn.softmax(topk_s, axis=-1)
            out = jnp.zeros_like(x)
            for ei in range(NUM_EXPERTS):
                g = jnp.where(topk_i == ei, w, 0.0).sum(-1)
                hh = jax.nn.gelu(x @ W1[ei] + b1[ei], approximate=False)
                out = out + g[..., None] * (hh @ W2[ei] + b2[ei])
            return out
        key = jax.random.key(seed)
        ks = jax.random.split(key, 8)
        s = 0.05
        return {'x': jax.random.normal(ks[0], (B, N, D), jnp.float32), 'W_gat': jax.random.normal(ks[1], (D, HEADS * NUM_EXPERTS), jnp.float32) * s, 'att_src': jax.random.normal(ks[2], (HEADS, NUM_EXPERTS), jnp.float32) * s, 'att_dst': jax.random.normal(ks[3], (HEADS, NUM_EXPERTS), jnp.float32) * s, 'b_gat': jnp.zeros((HEADS * NUM_EXPERTS,), jnp.float32), 'ln_gamma': jnp.ones((HEADS * NUM_EXPERTS,), jnp.float32), 'ln_beta': jnp.zeros((HEADS * NUM_EXPERTS,), jnp.float32), 'W1': jax.random.normal(ks[4], (NUM_EXPERTS, D, 2 * D), jnp.float32) * s, 'b1': jnp.zeros((NUM_EXPERTS, 2 * D), jnp.float32), 'W2': jax.random.normal(ks[5], (NUM_EXPERTS, 2 * D, D), jnp.float32) * s, 'b2': jnp.zeros((NUM_EXPERTS, D), jnp.float32), 'edge_index': jax.random.randint(ks[6], (2, N_EDGES), 0, B * N, jnp.int32)}
    _L0_ffn_all = _L0_ffn_setup()
    _L0_ffn_in = {k: v for k, v in _L0_ffn_all.items() if k in ('W_gat', 'att_src', 'att_dst', 'b_gat', 'ln_gamma', 'ln_beta', 'W1', 'b1', 'W2', 'b2', 'edge_index')}
    del _L0_ffn_all
    return {'x': x, 'src': src, 'dst': dst, 'L0_gnn_W0': _L0_gnn_in['W0'], 'L0_gnn_b0': _L0_gnn_in['b0'], 'L0_gnn_W1': _L0_gnn_in['W1'], 'L0_gnn_b1': _L0_gnn_in['b1'], 'L0_gnn_gamma': _L0_gnn_in['gamma'], 'L0_gnn_beta': _L0_gnn_in['beta'], 'L0_mix_Wq': _L0_mix_in['Wq'], 'L0_mix_Wk': _L0_mix_in['Wk'], 'L0_mix_Wv': _L0_mix_in['Wv'], 'L0_mix_Wo': _L0_mix_in['Wo'], 'L0_mix_bo': _L0_mix_in['bo'], 'L0_mix_ln1_g': _L0_mix_in['ln1_g'], 'L0_mix_ln1_b': _L0_mix_in['ln1_b'], 'L0_mix_W1': _L0_mix_in['W1'], 'L0_mix_b1': _L0_mix_in['b1'], 'L0_mix_W2': _L0_mix_in['W2'], 'L0_mix_b2': _L0_mix_in['b2'], 'L0_mix_ln2_g': _L0_mix_in['ln2_g'], 'L0_mix_ln2_b': _L0_mix_in['ln2_b'], 'L0_ffn_W_gat': _L0_ffn_in['W_gat'], 'L0_ffn_att_src': _L0_ffn_in['att_src'], 'L0_ffn_att_dst': _L0_ffn_in['att_dst'], 'L0_ffn_b_gat': _L0_ffn_in['b_gat'], 'L0_ffn_ln_gamma': _L0_ffn_in['ln_gamma'], 'L0_ffn_ln_beta': _L0_ffn_in['ln_beta'], 'L0_ffn_W1': _L0_ffn_in['W1'], 'L0_ffn_b1': _L0_ffn_in['b1'], 'L0_ffn_W2': _L0_ffn_in['W2'], 'L0_ffn_b2': _L0_ffn_in['b2'], 'L0_ffn_edge_index': _L0_ffn_in['edge_index']}

def reference(x, src, dst, L0_gnn_W0, L0_gnn_b0, L0_gnn_W1, L0_gnn_b1, L0_gnn_gamma, L0_gnn_beta, L0_mix_Wq, L0_mix_Wk, L0_mix_Wv, L0_mix_Wo, L0_mix_bo, L0_mix_ln1_g, L0_mix_ln1_b, L0_mix_W1, L0_mix_b1, L0_mix_W2, L0_mix_b2, L0_mix_ln2_g, L0_mix_ln2_b, L0_ffn_W_gat, L0_ffn_att_src, L0_ffn_att_dst, L0_ffn_b_gat, L0_ffn_ln_gamma, L0_ffn_ln_beta, L0_ffn_W1, L0_ffn_b1, L0_ffn_W2, L0_ffn_b2, L0_ffn_edge_index):
    import jax
    import jax.numpy as jnp

    def _L0_gnn_ref(features, edges, W0, b0, W1, b1, gamma, beta):
        import jax, jax.numpy as jnp
        import numpy as np
        V = 12500
        E = 37500
        D = 256
        BN_EPS = 1e-05
        num_verts = features.shape[0]
        h_self = jnp.einsum('vd,od->vo', features, W0) + b0
        h_nbr = jnp.einsum('vd,od->vo', features, W1) + b1
        src = jnp.concatenate([edges[:, 0], edges[:, 1]])
        dst = jnp.concatenate([edges[:, 1], edges[:, 0]])
        agg = jax.ops.segment_sum(h_nbr[src], dst, num_segments=num_verts)
        y = h_self + agg
        mean = jnp.mean(y, axis=0)
        var = jnp.var(y, axis=0)
        y_hat = (y - mean) * jax.lax.rsqrt(var + BN_EPS) * gamma + beta
        return jax.nn.relu(y_hat)

    def _L0_mix_ref(x, Wq, Wk, Wv, Wo, bo, ln1_g, ln1_b, W1, b1, W2, b2, ln2_g, ln2_b):
        import jax, jax.numpy as jnp
        import numpy as np
        EMB, HEADS, DEPTH, SEQ, BATCH = (256, 8, 4, 1024, 4)
        DH = EMB // HEADS
        FF = 4 * EMB
        EPS = 1e-05

        def _layernorm(x, g, b):
            mu = x.mean(-1, keepdims=True)
            var = ((x - mu) ** 2).mean(-1, keepdims=True)
            return (x - mu) * jax.lax.rsqrt(var + EPS) * g + b

        def _linear_attn(x, Wq, Wk, Wv, Wo, bo):
            b, n, dm = x.shape
            split = lambda t: t.reshape(b, n, HEADS, DH).transpose(0, 2, 1, 3)
            scale = DH ** (-0.25)
            q = jax.nn.softmax(split(x @ Wq) * scale, axis=-1)
            k = jax.nn.softmax(split(x @ Wk) * scale, axis=-2)
            v = split(x @ Wv)
            context = jnp.einsum('bhnd,bhne->bhde', k, v)
            out = jnp.einsum('bhnd,bhde->bhne', q, context)
            out = out.transpose(0, 2, 1, 3).reshape(b, n, dm)
            return out @ Wo + bo

        def _forward(x, Wq, Wk, Wv, Wo, bo, ln1_g, ln1_b, W1, b1, W2, b2, ln2_g, ln2_b):
            for i in range(DEPTH):
                h = _layernorm(x, ln1_g[i], ln1_b[i])
                x = x + _linear_attn(h, Wq[i], Wk[i], Wv[i], Wo[i], bo[i])
                h = _layernorm(x, ln2_g[i], ln2_b[i])
                x = x + (jax.nn.gelu(h @ W1[i] + b1[i], approximate=False) @ W2[i] + b2[i])
            return x
        return _forward(x, Wq, Wk, Wv, Wo, bo, ln1_g, ln1_b, W1, b1, W2, b2, ln2_g, ln2_b)

    def _L0_ffn_ref(x, W_gat, att_src, att_dst, b_gat, ln_gamma, ln_beta, W1, b1, W2, b2, edge_index):
        import jax, jax.numpy as jnp
        import numpy as np
        B, N, D = (16, 512, 256)
        NUM_EXPERTS, TOP_K, HEADS = (4, 2, 4)
        N_EDGES = 131072
        LN_EPS = 1e-05

        def _layernorm(x, g, b):
            mu = x.mean(-1, keepdims=True)
            var = ((x - mu) ** 2).mean(-1, keepdims=True)
            return (x - mu) * jax.lax.rsqrt(var + LN_EPS) * g + b

        def _forward(x, edge_index, W_gat, att_src, att_dst, b_gat, ln_gamma, ln_beta, W1, b1, W2, b2):
            Bc, Nc, Dc = x.shape
            M = Bc * Nc
            x_flat = x.reshape(M, Dc)
            h = (x_flat @ W_gat).reshape(M, HEADS, NUM_EXPERTS)
            loops = jnp.arange(M, dtype=edge_index.dtype)
            src = jnp.concatenate([edge_index[0], loops])
            dst = jnp.concatenate([edge_index[1], loops])
            a_src = (h * att_src).sum(-1)
            a_dst = (h * att_dst).sum(-1)
            e = jax.nn.leaky_relu(a_src[src] + a_dst[dst], negative_slope=0.2)
            e_max = jax.ops.segment_max(e, dst, num_segments=M)
            ee = jnp.exp(e - e_max[dst])
            denom = jax.ops.segment_sum(ee, dst, num_segments=M)
            alpha = ee / (denom[dst] + 1e-16)
            msg = h[src] * alpha[:, :, None]
            agg = jax.ops.segment_sum(msg, dst, num_segments=M).reshape(M, HEADS * NUM_EXPERTS) + b_gat
            scores = _layernorm(agg, ln_gamma, ln_beta).reshape(M, HEADS, NUM_EXPERTS).mean(1)
            scores = scores.reshape(Bc, Nc, NUM_EXPERTS)
            topk_s, topk_i = jax.lax.top_k(scores, TOP_K)
            w = jax.nn.softmax(topk_s, axis=-1)
            out = jnp.zeros_like(x)
            for ei in range(NUM_EXPERTS):
                g = jnp.where(topk_i == ei, w, 0.0).sum(-1)
                hh = jax.nn.gelu(x @ W1[ei] + b1[ei], approximate=False)
                out = out + g[..., None] * (hh @ W2[ei] + b2[ei])
            return out
        return _forward(x, edge_index, W_gat, att_src, att_dst, b_gat, ln_gamma, ln_beta, W1, b1, W2, b2)
    edge_index_t = jnp.stack([src, dst], axis=1)
    xn = _layernorm(x, axis=-1)
    x = x + _L0_gnn_ref(xn, edge_index_t, L0_gnn_W0, L0_gnn_b0, L0_gnn_W1, L0_gnn_b1, L0_gnn_gamma, L0_gnn_beta) + _L0_mix_ref(xn[None], L0_mix_Wq, L0_mix_Wk, L0_mix_Wv, L0_mix_Wo, L0_mix_bo, L0_mix_ln1_g, L0_mix_ln1_b, L0_mix_W1, L0_mix_b1, L0_mix_W2, L0_mix_b2, L0_mix_ln2_g, L0_mix_ln2_b)[0]
    x = x + _L0_ffn_ref(_layernorm(x, axis=-1)[None], L0_ffn_W_gat, L0_ffn_att_src, L0_ffn_att_dst, L0_ffn_b_gat, L0_ffn_ln_gamma, L0_ffn_ln_beta, L0_ffn_W1, L0_ffn_b1, L0_ffn_W2, L0_ffn_b2, L0_ffn_edge_index)[0]
    return x

_drawn_inputs = setup_inputs


def setup_inputs(seed=0):
    import zlib

    import numpy as np

    out = dict(_drawn_inputs(seed))
    spreads = {'L0_gnn_gamma': (1.0, 0.2),
     'L0_gnn_beta': (0.0, 0.1),
     'L0_mix_bo': (0.0, 0.1),
     'L0_mix_ln1_g': (1.0, 0.6),
     'L0_mix_ln1_b': (0.0, 0.311),
     'L0_mix_b1': (0.0, 0.1),
     'L0_mix_b2': (0.0, 0.1),
     'L0_mix_ln2_g': (1.0, 0.6),
     'L0_mix_ln2_b': (0.0, 0.1),
     'L0_ffn_b_gat': (0.0, 0.1),
     'L0_ffn_ln_gamma': (1.0, 0.2),
     'L0_ffn_ln_beta': (0.0, 0.1),
     'L0_ffn_b1': (0.0, 0.327),
     'L0_ffn_b2': (0.0, 0.1)}
    factors = {'L0_gnn_b0': 64.0, 'L0_mix_Wq': 33.233, 'L0_mix_Wk': 31.539, 'L0_ffn_att_dst': 11.879}
    for name, (base, spread) in spreads.items():
        noise = np.random.default_rng([zlib.crc32(name.encode()), seed]).standard_normal(out[name].shape)
        drawn = base * np.exp(spread * noise) if base else spread * noise
        out[name] = jnp.asarray(drawn.astype(out[name].dtype))
    for name, factor in factors.items():
        out[name] = (out[name] * factor).astype(out[name].dtype)
    return out
```

```python
from contextlib import ExitStack

import concourse.bass as bass
from concourse import mybir

f32, f16, i32, i16 = mybir.dt.float32, mybir.dt.float16, mybir.dt.int32, mybir.dt.int16
ALU, ACT, AX = mybir.AluOpType, mybir.ActivationFunctionType, mybir.AxisListType

P = 128
N, D = 6250, 256
BANK = 512
T = -(-N // P)
LAST = N - (T - 1) * P
EVEN, ODD = (T + 1) // 2, T // 2
HALF = D // P
EPS = 1e-5
LAYERS, HEADS, FF = 4, 8, 1024
DH = D // HEADS
MF = FF // P
QK_SCALE = float(DH) ** -0.25
LOWEST = -3.0e38
UB = 4
GNN_E, GAT_E = 206250, 131072
GNN_G, GNN_C = 8, -(-GNN_E // (4 * P))
GAT_G, GAT_C = 3, -(-GAT_E // (3 * P))
GNN_Q = -(-(GNN_C + T) // UB) * UB
GAT_Q = -(-(GAT_C + T) // UB) * UB
MAXC, MAXQ = max(GNN_C, GAT_C), max(GNN_Q, GAT_Q)
GNN_BLOCKS = GNN_G * GNN_Q // UB
GAT_BLOCKS = GAT_G * GAT_Q // UB
PASSES = 4
MIXED = LAYERS * PASSES * (T - 1)
GH, NE = 4, 4
EF = 512
ME = EF // P
HE = GH * NE
TAB = HE + 2 * GH
MSG = HE + GH


class Shared:
    pass


def build(nc, A, out, stop=99, dbg=None):
    ctx = ExitStack()

    def sb(name, shape, dt, where=ctx):
        return where.enter_context(nc.sbuf_tensor(name, shape, dt))

    def pb(name, shape, where, dt=f32):
        return where.enter_context(nc.psum_tensor(name, shape, dt))

    def sem(name):
        return ctx.enter_context(nc.semaphore(name))

    def sem2(name):
        return [sem(name + "0"), sem(name + "1")]

    def dram(name, shape, dt):
        return nc.dram_tensor(name, shape, dt, kind="Internal").ap()

    def tiles(eng, step):
        with eng.Fori(0, (T - 1) // 2) as j:
            for b in range(2):
                step(j * 2 + b, b, P, j)
        step(T - 1, 0, LAST, EVEN - 1)

    def one(t, w=1):
        return bass.ds(t * w, w)

    with ctx:
        hn_d = dram("hn_d", (T * P, D), f32)
        k_d = dram("k_d", (T * P, D), f32)
        v_d = dram("v_d", (T * P, D), f32)
        q_d = dram("q_d", (T * P, D), f32)
        gnn_tile_d = dram("gnn_tile_d", (GNN_G, GNN_Q), i16)
        gat_tile_d = dram("gat_tile_d", (GAT_G, GAT_Q), i16)
        tab_d = dram("tab_d", (T * P, TAB), f32)

        X = sb("X", [P, T, D], f32)
        ident = sb("ident", [P, P], f32)
        ones = sb("ones", [P, P], f32)
        zeros = sb("zeros", [1, D], f32)
        G = []
        node_no = sb("node_no", [P, P], f32)
        MV = sb("MV", [P, T, 2], f32)
        RS = sb("RS", [P, T], f32)
        NM = sb("NM", [P, T], f32)
        sd = sb("sd", [P, 2, T], f32)
        bst = sb("bst", [P, 6], f32)
        bag = sb("bag", [P, 2], f32)
        gat_src = sb("gat_src", [P, GAT_G * GAT_Q], i32)
        gat_node = sb("gat_node", [P, GAT_G * GAT_Q], f16)

        idle = sem("idle")
        var_ready, sd_ready = sem("var_ready"), sem("sd_ready")

        def hold(eng, s, value):
            eng.wait_ge(s, value)
            eng.sem_inc(idle, 1)

        def row_stats(v, t):
            nc.vector.bn_stats(bst[:, :], X[:, t, :])
            v.drain()
            nc.vector.bn_aggr(bag[:, :], bst[:, :])
            v.drain()
            nc.vector.tensor_copy(MV[:, t, :], bag[:, :])

        def rstd_block(k):
            with nc.Block() as block:
                @block.vector
                def _(v):
                    nc.vector.tensor_scalar(sd[:, 0, :], MV[:, :, 1], EPS, None, ALU.add).then_inc(var_ready, 1)
                    hold(v, sd_ready, k + 1)
                    nc.vector.reciprocal(RS[:, :], sd[:, 1, :])
                    v.drain()
                    nc.vector.tensor_tensor(NM[:, :], RS[:, :], RS[:, :], ALU.mult)
                    v.drain()
                    nc.vector.tensor_tensor(NM[:, :], NM[:, :], sd[:, 0, :], ALU.mult)
                    v.drain()
                    nc.vector.tensor_scalar(NM[:, :], NM[:, :], -0.5, 1.5, ALU.mult, ALU.add)
                    v.drain()
                    nc.vector.tensor_tensor(RS[:, :], RS[:, :], NM[:, :], ALU.mult)
                    v.drain()
                    nc.vector.scalar_tensor_tensor(NM[:, :], MV[:, :, 0], -1.0, RS[:, :], ALU.mult, ALU.mult)

                @block.scalar
                def _(act):
                    act.wait_ge(var_ready, k + 1)
                    nc.scalar.activation(sd[:, 1, :], sd[:, 0, :], ACT.Sqrt).then_inc(sd_ready, 1)

        def normalise(t, dst):
            return nc.vector.tensor_scalar(dst, X[:, t, :], RS[:, one(t)], NM[:, one(t)], ALU.mult, ALU.add)

        def transpose_tile(dst, src):
            for c in range(HALF):
                last = nc.tensor.transpose(dst[:, c * P:(c + 1) * P], src[:, c * P:(c + 1) * P], ident[:, :])
            return last

        graph = ctx.enter_context(ExitStack())
        Y = sb("Y", [P, T, D], f32, graph)
        gnn_src = sb("gnn_src", [P, GNN_G * GNN_Q], i32, graph)
        gnn_node = sb("gnn_node", [P, GNN_G * GNN_Q], f16, graph)

        e = Shared()
        e.G, e.X, e.Y, e.ctx = G, X, Y, ctx
        e.gat_node, e.gat_src, e.gat_tile_d, e.gnn_node = gat_node, gat_src, gat_tile_d, gnn_node
        e.gnn_src, e.gnn_tile_d, e.graph, e.hn_d = gnn_src, gnn_tile_d, graph, hn_d
        e.hold, e.ident, e.k_d, e.node_no = hold, ident, k_d, node_no
        e.normalise, e.ones, e.pb, e.q_d = normalise, ones, pb, q_d
        e.row_stats, e.rstd_block, e.sb, e.sem = row_stats, rstd_block, sb, sem
        e.sem2, e.tab_d, e.tiles, e.transpose_tile = sem2, tab_d, tiles, transpose_tile
        e.v_d, e.zeros = v_d, zeros
        first_phase(nc, A, e)
        if stop >= 1:
            sort_phase(nc, A, e)
        if stop >= 2:
            mix_phase(nc, A, e)
        if stop >= 3:
            sum_phase(nc, A, e)
        if stop <= 3 and dbg is not None:
            dn = sem("dbg")
            with nc.Block() as block:
                @block.sync
                def _(sp):
                    sp.dma_start(dbg["X"], X[:, :, :]).then_inc(dn, 16)
                    sp.dma_start(dbg["Y"], Y[:, :, :]).then_inc(dn, 16)
                    sp.dma_start(dbg["hn"], hn_d).then_inc(dn, 16)
                    if stop:
                        sp.dma_start(dbg["src"], gnn_src[:, :]).then_inc(dn, 16)
                        sp.dma_start(dbg["node"], gnn_node[:, :]).then_inc(dn, 16)
                        sp.dma_start(dbg["tile"], gnn_tile_d).then_inc(dn, 16)
                    sp.wait_ge(dn, 96 if stop else 48)
            return
        graph.close()
        expert_phase(nc, A, out, e)


def first_phase(nc, A, e):
    sb, pb, sem, X, Y, ident, ones = e.sb, e.pb, e.sem, e.X, e.Y, e.ident, e.ones
    x_in, zeroed = sem("x_in"), sem("zeroed")
    wt_ready, wt_copied = sem("wt_ready"), sem("wt_copied")
    xn_ready, tp_ready, ht_ready = sem("xn0_ready"), sem("tp0_ready"), sem("ht0_ready")
    mm_ready, hn_ready, hn_out, hn_stored = sem("mm0_ready"), sem("hn_ready"), e.sem2("hn_out"), sem("hn_stored")
    with ExitStack() as own:
        W01 = sb("W01", [P, 2, HALF, D], f32, own)
        WT = sb("WT", [P, HALF, 2 * D], f32, own)
        b01 = sb("b01", [1, 2 * D], f32, own)
        XS = sb("XS0", [P, 2, D], f32, own)
        HT = sb("HT0", [P, 2, D], f32, own)
        HN = sb("HN", [P, 2, D], f32, own)
        psT = pb("psT0", [P, 2, BANK], own)
        psY = pb("psY0", [P, 2, BANK], own)
        psN = pb("psN0", [P, 2, BANK], own)
        with nc.Block() as block:
            @block.sync
            def _(sp):
                sp.dma_start(X[:, 0:T - 1, :], A["x"][0:(T - 1) * P, :].rearrange("(t p) d -> p t d", p=P)).then_inc(x_in, 16)
                sp.wait_ge(zeroed, 1)
                sp.dma_start(X[0:LAST, T - 1, :], A["x"][(T - 1) * P:N, :]).then_inc(x_in, 16)
                sp.dma_start(W01[:, 0, :, :], A["L0_gnn_W0"].rearrange("(c p) d -> p c d", p=P)).then_inc(x_in, 16)
                sp.dma_start(W01[:, 1, :, :], A["L0_gnn_W1"].rearrange("(c p) d -> p c d", p=P)).then_inc(x_in, 16)
                sp.dma_start(b01[:, 0:D], A["L0_gnn_b0"].rearrange("(a n) -> a n", a=1)).then_inc(x_in, 16)
                sp.dma_start(b01[:, D:2 * D], A["L0_gnn_b1"].rearrange("(a n) -> a n", a=1)).then_inc(x_in, 16)
                sp.wait_ge(x_in, 96)

            @block.gpsimd
            def _(pool):
                nc.gpsimd.memset(ident[:, :], 0.0)
                nc.gpsimd.iota(e.node_no[:, :], pattern=[[1, P]], base=1, channel_multiplier=0,
                               allow_small_or_imprecise_dtypes=True)
                pool.drain()
                nc.gpsimd.affine_select(out=ident[:, :], in_=ident[:, :], compare_op=ALU.not_equal, fill=1.0,
                                        base=0, pattern=[[-1, P]], channel_multiplier=1)

            @block.vector
            def _(v):
                nc.vector.memset(X[:, T - 1, :], 0.0).then_inc(zeroed, 1)
                nc.vector.memset(ones[:, :], 1.0)
                nc.vector.memset(e.zeros[:, :], 0.0)
                e.hold(v, x_in, 96)
                e.tiles(v, lambda t, b, n, j: e.row_stats(v, t))
        e.rstd_block(0)

        with nc.Block() as block:
            @block.tensor
            def _(pe):
                for k in range(4):
                    w, c = divmod(k, HALF)
                    if k >= 2:
                        pe.wait_ge(wt_copied, k - 1)
                    for o in range(HALF):
                        last = nc.tensor.transpose(psY[:, k % 2, o * P:(o + 1) * P],
                                                   W01[:, w, o, c * P:(c + 1) * P], ident[:, :])
                    last.then_inc(wt_ready, 1)
                pe.wait_ge(wt_copied, 4)

                def turn(t, b):
                    pe.wait_ge(xn_ready, t + 1)
                    e.transpose_tile(psT[:, b, 0:D], XS[:, b, :]).then_inc(tp_ready, 1)

                def products(t, b, n, j):
                    if n == P:
                        turn(t + 1, 1 - b)
                    pe.wait_ge(ht_ready, t + 1)
                    for w, ps in enumerate((psY, psN)):
                        cols = slice(w * D, (w + 1) * D)
                        nc.tensor.matmul(ps[:, b, 0:D], ones[0:1, :], b01[:, cols], start=True, stop=False)
                        for c in range(HALF):
                            last = nc.tensor.matmul(ps[:, b, 0:D], HT[:, b, c * P:(c + 1) * P], WT[:, c, cols],
                                                    start=False, stop=(c == HALF - 1))
                    last.then_inc(mm_ready, 1)
                turn(0, 0)
                e.tiles(pe, products)

            @block.vector
            def _(v):
                for k in range(4):
                    w, c = divmod(k, HALF)
                    v.wait_ge(wt_ready, k + 1)
                    nc.vector.tensor_copy(WT[:, c, w * D:(w + 1) * D], psY[:, k % 2, 0:D]).then_inc(wt_copied, 1)

                def xn(t, b):
                    e.normalise(t, XS[:, b, :]).then_inc(xn_ready, 1)
                    e.normalise(t, X[:, t, :])

                def own_part(t, b, n, j):
                    if n == P:
                        xn(t + 1, 1 - b)
                    v.wait_ge(mm_ready, t + 1)
                    nc.vector.tensor_copy(Y[:, t, :], psY[:, b, 0:D])
                xn(0, 0)
                e.tiles(v, own_part)

            @block.scalar
            def _(act):
                def ht(t, b):
                    act.wait_ge(tp_ready, t + 1)
                    nc.scalar.activation(HT[:, b, :], psT[:, b, 0:D], ACT.Copy).then_inc(ht_ready, 1)

                def neighbours(t, b, n, j):
                    if n == P:
                        ht(t + 1, 1 - b)
                    e.hold(act, hn_stored, t + 1)
                    act.wait_ge(mm_ready, t + 1)
                    nc.scalar.activation(HN[:, b, :], psN[:, b, 0:D], ACT.Copy).then_inc(hn_ready, 1)
                ht(0, 0)
                e.tiles(act, neighbours)

            @block.sync
            def _(sp):
                def store(t, b, n, j):
                    sp.wait_ge(hn_ready, t + 1)
                    sp.dma_start(e.hn_d[bass.ds(t * P, P), :], HN[:, b, :]).then_inc(hn_out[b], 16)
                    sp.wait_ge(hn_out[b], j * 16 + 16)
                    sp.sem_inc(hn_stored, 1)
                sp.sem_inc(hn_stored, 2)
                e.tiles(sp, store)


def sort_phase(nc, A, e):
    with ExitStack() as own:
        w = Shared()
        w.lane = e.sb("lane", [P, P], f16, own)
        w.chunk_no = e.sb("chunk_no", [P, MAXQ], f16, own)
        w.tile_no = e.sb("tile_no", [P, T], f32, own)
        w.chunk_at = e.sb("chunk_at", [P, -(-MAXQ // P)], f32, own)
        w.before = e.sb("before", [P, P], f32, own)
        w.blank = e.sb("blank", [P, MAXQ], f16, own)
        w.end, w.start, w.t_a, w.t_b = (e.sb(x, [P, MAXQ], i32, own) for x in ("end", "start", "t_a", "t_b"))
        w.place, w.scan, w.lane_of = (e.sb(x, [P, MAXC], f32, own) for x in ("place", "scan", "lane_of"))
        w.chunk_of, w.pay_hi, w.pay_lo = (e.sb(x, [P, MAXC], f32, own) for x in ("chunk_of", "pay_hi", "pay_lo"))
        w.tile_of, w.mask = (e.sb(x, [P, MAXC], f16, own) for x in ("tile_of", "mask"))
        w.tot, w.chunks, w.upto, w.base = (e.sb(x, [P, T], f32, own) for x in ("tot", "chunks", "upto", "base"))
        w.tot_i = e.sb("tot_i", [P, T], i32, own)
        w.hits = e.sb("hits", [P, T], f32, own)
        w.tile_f = e.sb("tile_f", [P, -(-MAXQ // P)], f32, own)
        w.tile_i = e.sb("tile_i", [P, -(-MAXQ // P)], i16, own)
        w.L = e.sb("L", [P, 2, 2, P], f16, own)
        w.R = e.sb("R", [P, 2, MAXQ], f16, own)
        w.psP = e.pb("psP", [P, 2, BANK], own)
        w.psL = e.pb("psL", [P, 2, BANK], own)
        with nc.Block() as block:
            @block.gpsimd
            def _(pool):
                small = dict(allow_small_or_imprecise_dtypes=True)
                nc.gpsimd.iota(w.lane[:, :], pattern=[[1, P]], base=0, channel_multiplier=0, **small)
                nc.gpsimd.iota(w.chunk_no[:, :], pattern=[[1, MAXQ]], base=0, channel_multiplier=0, **small)
                nc.gpsimd.iota(w.tile_no[:, :], pattern=[[1, T]], base=0, channel_multiplier=0, **small)
                nc.gpsimd.iota(w.chunk_at[:, :], pattern=[[P, -(-MAXQ // P)]], base=0, channel_multiplier=1, **small)
                nc.gpsimd.memset(w.blank[:, :], 0.0)
                nc.gpsimd.memset(w.before[:, :], 1.0)
                pool.drain()
                nc.gpsimd.affine_select(out=w.before[:, :], in_=w.before[:, :], compare_op=ALU.is_ge, fill=0.0,
                                        base=-1, pattern=[[1, P]], channel_multiplier=-1)
        sort_groups(nc, e, w, "gnn", GNN_G, GNN_C, GNN_Q, A["gnn_end"], A["gnn_start"], e.gnn_src, e.gnn_node, e.gnn_tile_d)
        sort_groups(nc, e, w, "gat", GAT_G, GAT_C, GAT_Q, A["gat_end"], A["gat_start"], e.gat_src, e.gat_node, e.gat_tile_d)


def sort_groups(nc, e, w, kind, G, C, Q, end_d, start_d, src_list, node_list, tile_d):
    edges_in, tot_ready, prefix_ready = e.sem(kind + "_edges_in"), e.sem(kind + "_tot_ready"), e.sem(kind + "_prefix_ready")
    tile_ready, tile_out = e.sem(kind + "_tile_ready"), e.sem(kind + "_tile_out")
    onehot_ready, onehot_used, list_ready = e.sem(kind + "_onehot_ready"), e.sem(kind + "_onehot_used"), e.sem(kind + "_list_ready")
    V = nc.vector
    QK = -(-Q // P)

    def columns(eng, step):
        with eng.Fori(0, C // 2) as j:
            for b in range(2):
                step(j * 2 + b, b)
        if C % 2:
            step(C - 1, 0)

    with nc.Fori(0, G) as g:
        with nc.Block() as block:
            @block.sync
            def _(sp):
                sp.dma_start(w.end[:, 0:C], end_d[g, :, :]).then_inc(edges_in, 16)
                sp.dma_start(w.start[:, 0:C], start_d[g, :, :]).then_inc(edges_in, 16)
                sp.wait_ge(tile_ready, g + 1)
                for k in range(QK):
                    n = min(P, Q - k * P)
                    sp.dma_start(tile_d[g, k * P:k * P + n].rearrange("(p a) -> p a", a=1), w.tile_i[0:n, k:k + 1]).then_inc(tile_out, 16)
                e.hold(sp, tile_out, g * (16 * QK) + 16 * QK)

            @block.tensor
            def _(pe):
                pe.wait_ge(tot_ready, g + 1)
                nc.tensor.matmul(w.psP[:, 0, 0:T], w.before[:, :], w.tot[:, :], start=True, stop=True)
                nc.tensor.matmul(w.psP[:, 0, T:2 * T], e.ones[:, :], w.tot[:, :], start=True, stop=True).then_inc(prefix_ready, 1)

            @block.vector
            def _(v):
                end, start, t_a, t_b = w.end[:, 0:C], w.start[:, 0:C], w.t_a[:, 0:C], w.t_b[:, 0:C]
                tile_of, mask, place = w.tile_of[:, 0:C], w.mask[:, 0:C], w.place[:, 0:C]
                v.wait_ge(edges_in, g * 32 + 32)
                V.tensor_scalar(t_a, end, 7, None, ALU.arith_shift_right)
                V.tensor_scalar(t_b, end, 127, None, ALU.bitwise_and)
                V.tensor_scalar(start, start, float(N - 1), None, ALU.min)
                V.memset(place, 0.0)
                v.drain()
                V.tensor_copy(tile_of, t_a)
                V.tensor_scalar(w.pay_lo[:, 0:C], t_b, 1.0, None, ALU.add)
                v.drain()
                V.tensor_scalar(t_a, start, 3, None, ALU.bitwise_and)
                V.tensor_scalar(t_b, start, 2, None, ALU.arith_shift_right)
                v.drain()
                V.scalar_tensor_tensor(w.pay_lo[:, 0:C], t_a, 256.0, w.pay_lo[:, 0:C], ALU.mult, ALU.add)
                V.tensor_copy(w.pay_hi[:, 0:C], t_b)
                with v.Fori(0, T) as t:
                    V.tensor_scalar(mask, tile_of, w.tile_no[:, bass.ds(t, 1)], None, ALU.is_equal, ALU.add,
                                    accum_out=w.tot[:, bass.ds(t, 1)])
                    v.drain()
                V.tensor_copy(w.tot[:, 0:1], w.tot[:, 0:1]).then_inc(tot_ready, 1)
                v.wait_ge(prefix_ready, g + 1)
                V.tensor_scalar(w.tot_i[:, :], w.psP[:, 0, T:2 * T], float(P - 1), None, ALU.add)
                v.drain()
                V.tensor_scalar(w.tot_i[:, :], w.tot_i[:, :], 7, None, ALU.arith_shift_right)
                v.drain()
                V.tensor_copy(w.chunks[:, :], w.tot_i[:, :])
                v.drain()
                V.tensor_tensor_scan(w.upto[:, :], w.chunks[:, :], w.blank[:, 0:T], 0.0, ALU.add, ALU.add)
                v.drain()
                V.tensor_tensor(w.base[:, :], w.upto[:, :], w.chunks[:, :], ALU.subtract)
                v.drain()
                V.scalar_tensor_tensor(w.base[:, :], w.base[:, :], float(P), w.psP[:, 0, 0:T], ALU.mult, ALU.add)
                for k in range(QK):
                    V.tensor_scalar(w.hits[:, :], w.upto[:, :], w.chunk_at[:, k:k + 1], None, ALU.is_le, ALU.add,
                                    accum_out=w.tile_f[:, k:k + 1])
                    v.drain()
                V.tensor_scalar(w.tile_i[:, 0:QK], w.tile_f[:, 0:QK], float(T - 1), None, ALU.min).then_inc(tile_ready, 1)
                with v.Fori(0, T) as t:
                    V.tensor_scalar(mask, tile_of, w.tile_no[:, bass.ds(t, 1)], None, ALU.is_equal)
                    v.drain()
                    V.tensor_tensor_scan(w.scan[:, 0:C], mask, w.blank[:, 0:C], w.base[:, bass.ds(t, 1)], ALU.add, ALU.add)
                    v.drain()
                    V.tensor_tensor(w.scan[:, 0:C], w.scan[:, 0:C], mask, ALU.mult)
                    v.drain()
                    V.tensor_tensor(place, place, w.scan[:, 0:C], ALU.add)
                    v.drain()
                V.tensor_scalar(t_a, place, -1.0, None, ALU.add)
                v.drain()
                V.tensor_scalar(t_b, t_a, 7, None, ALU.arith_shift_right)
                V.tensor_scalar(t_a, t_a, 127, None, ALU.bitwise_and)
                v.drain()
                V.tensor_copy(w.chunk_of[:, 0:C], t_b)
                V.tensor_copy(w.lane_of[:, 0:C], t_a)

        with nc.Block() as block:
            @block.vector
            def _(v):
                def onehots(c, b):
                    at = bass.ds(c, 1)
                    v.wait_ge(onehot_used, g * (C + 2) + (c + 1))
                    V.tensor_scalar(w.L[:, b, 0, :], w.lane[:, :], w.lane_of[:, at], w.pay_hi[:, at], ALU.is_equal, ALU.mult)
                    V.tensor_scalar(w.L[:, b, 1, :], w.lane[:, :], w.lane_of[:, at], w.pay_lo[:, at], ALU.is_equal, ALU.mult)
                    V.tensor_scalar(w.R[:, b, 0:Q], w.chunk_no[:, 0:Q], w.chunk_of[:, at], None, ALU.is_equal).then_inc(onehot_ready, 1)
                columns(v, onehots)
                v.wait_ge(list_ready, g + 1)
                t_a, t_b = w.t_a[:, 0:Q], w.t_b[:, 0:Q]
                V.tensor_copy(t_a, w.psL[:, 1, 0:Q])
                v.drain()
                V.tensor_scalar(t_b, t_a, 8, None, ALU.arith_shift_right)
                V.tensor_scalar(t_a, t_a, 255, None, ALU.bitwise_and)
                v.drain()
                V.tensor_copy(node_list[:, bass.ds(g * Q, Q)], t_a)
                V.scalar_tensor_tensor(src_list[:, bass.ds(g * Q, Q)], w.psL[:, 0, 0:Q], 4.0, t_b, ALU.mult, ALU.add)

            @block.tensor
            def _(pe):
                pe.sem_inc(onehot_used, 2)

                def move(c, b):
                    pe.wait_ge(onehot_ready, g * C + (c + 1))
                    nc.tensor.matmul(w.psL[:, 0, 0:Q], w.L[:, b, 0, :], w.R[:, b, 0:Q], start=False, stop=False)
                    nc.tensor.matmul(w.psL[:, 1, 0:Q], w.L[:, b, 1, :], w.R[:, b, 0:Q], start=False, stop=False).then_inc(onehot_used, 1)
                for h in range(2):
                    nc.tensor.matmul(w.psL[:, h, 0:Q], w.blank[:, 0:P], w.blank[:, 0:Q], start=True, stop=False)
                columns(pe, move)
                for h in range(2):
                    last = nc.tensor.matmul(w.psL[:, h, 0:Q], w.blank[:, 0:P], w.blank[:, 0:Q], start=False, stop=True)
                last.then_inc(list_ready, 1)


class Gathers:

    def __init__(self, nc, e, kind, width, rows_d, src_list, node_list, tile_d, blocks, own):
        self.nc, self.e, self.width, self.rows_d, self.blocks = nc, e, width, rows_d, blocks
        self.src_list, self.node_list, self.tile_d = src_list, node_list, tile_d
        self.numbers = e.sb(kind + "_numbers", [P, 2 * UB], i32, own)
        self.onehot = e.sb(kind + "_onehot", [P, 2 * UB, P], f32, own)
        self.rows = e.sb(kind + "_rows", [P, 2 * UB, width], f32, own)
        self.tile_row = e.sb(kind + "_tile_row", [1, blocks * UB], i16, own)
        self.staged, self.summed = e.sem(kind + "_staged"), e.sem(kind + "_summed")
        self.gathered = [e.sem(f"{kind}_gathered{i}") for i in range(2 * UB)]

    def stage(self, q, b):
        V = self.nc.vector
        V.tensor_copy(self.numbers[:, UB * b:UB * b + UB], self.src_list[:, bass.ds(q * UB, UB)])
        for s in range(UB):
            last = V.tensor_scalar(self.onehot[:, UB * b + s, :], self.e.node_no[:, :],
                                   self.node_list[:, bass.ds(q * UB + s, 1)], None, ALU.is_equal)
        last.then_inc(self.staged, 1)

    def gather(self, pool, q, b):
        self.e.hold(pool, self.staged, q + 1)
        for i in range(UB * b, UB * b + UB):
            self.nc.gpsimd.indirect_dma_start(
                out=self.rows[:, i, :], out_offset=None, in_=self.rows_d,
                in_offset=bass.IndirectOffsetOnAxis(ap=self.numbers[:, i:i + 1], axis=0)).then_inc(self.gathered[i], 16)

    def add_up(self, pe, q, b, j, psG):
        pe.wait_ge(self.staged, q + 1)
        for i in range(UB * b, UB * b + UB):
            pe.wait_ge(self.gathered[i], j * 16 + 16)
            last = self.nc.tensor.matmul(psG[:, i, :], self.onehot[:, i, :], self.rows[:, i, :], start=True, stop=True)
        last.then_inc(self.summed, 1)

    def accumulate(self, v, q, b, psG, Y):
        self.e.hold(v, self.summed, q + 1)
        for s in range(UB):
            t = v.value_load(self.tile_row[0:1, bass.ds(q * UB + s, 1)], min_val=0, max_val=T - 1)
            self.nc.vector.tensor_tensor(Y[:, t, :], Y[:, t, :], psG[:, UB * b + s, :], ALU.add)
            v.drain()


def mix_phase(nc, A, e):
    X, Y, ident, ones, tiles, hold = e.X, e.Y, e.ident, e.ones, e.tiles, e.hold
    V, S = nc.vector, nc.scalar
    own = e.graph
    G = Gathers(nc, e, "gnn", D, e.hn_d, e.gnn_src, e.gnn_node, e.gnn_tile_d, GNN_BLOCKS, own)
    psG = e.pb("psG", [P, 2 * UB, D], own)
    head_block = e.sb("head_block", [P, P], f32, own)
    w_in = e.sem("mix_w_in")
    xn_ready, tp_ready, ht_ready = e.sem("xn_ready"), e.sem("tp_ready"), e.sem("ht_ready")
    qkv_ready, kv_ready, qsub_ready, qexp_ready = e.sem("qkv_ready"), e.sem("kv_ready"), e.sem("qsub_ready"), e.sem("qexp_ready")
    qn_ready, qt_ready, qts_ready = e.sem("qn_ready"), e.sem("qt_ready"), e.sem("qts_ready")
    kv_stored, q_stored = e.sem("kv_stored"), e.sem("q_stored")
    kv_out, q_out, kv_in, q_in = e.sem2("kv_out"), e.sem2("q_out"), e.sem2("kv_in"), e.sem2("q_in")
    kmt_ready, diag_ready, kmb_ready = e.sem("kmt_ready"), e.sem("diag_ready"), e.sem("kmb_ready")
    ks_ready, ke_ready, ctx_done = e.sem("ks_ready"), e.sem("ke_ready"), e.sem("ctx_done")
    cn_ready, cnt_ready, cnt_copied, mx_ready = e.sem("cn_ready"), e.sem("cnt_ready"), e.sem("cnt_copied"), e.sem("mx_ready")
    att_ready, att_added, q_used = e.sem("att_ready"), e.sem("att_added"), e.sem("q_used")
    xn2_ready, tp2_ready, ht2_ready = e.sem("xn2_ready"), e.sem("tp2_ready"), e.sem("ht2_ready")
    up_ready, gelu_ready, down_ready, down_added = e.sem("up_ready"), e.sem("gelu_ready"), e.sem("down_ready"), e.sem("down_added")

    with nc.Block() as block:
        @block.sync
        def _(sp):
            sp.dma_start(G.tile_row[:, :], e.gnn_tile_d.rearrange("(a g) q -> a (g q)", a=1)).then_inc(w_in, 16)
            sp.wait_ge(w_in, 16)

        @block.vector
        def _(v):
            V.memset(head_block[:, :], 0.0)
            v.drain()
            for h in range(P // DH):
                V.memset(head_block[h * DH:(h + 1) * DH, h * DH:(h + 1) * DH], 1.0)
            G.stage(0, 0)

    layer = own.enter_context(ExitStack())
    Wqkv = e.sb("Wqkv", [P, HALF, 3 * D], f32, layer)
    Wo = e.sb("Wo", [P, HALF, D], f32, layer)
    W1 = e.sb("W1", [P, HALF, FF], f32, layer)
    W2 = e.sb("W2", [P, MF, D], f32, layer)
    rows = e.sb("bias_rows", [1, 2 * D + FF], f32, layer)
    bo, b2, b1 = rows[:, 0:D], rows[:, D:2 * D], rows[:, 2 * D:]
    ln = e.sb("ln", [P, 4, HALF], f32, layer)
    KM = e.sb("KM", [P, D], f32, layer)
    MX = e.sb("MX", [P, HALF, D], f32, layer)

    def block_q(l, p, t):
        return l * (PASSES * (T - 1)) + (t + p * (T - 1))

    def block_j(l, p, j):
        return l * (PASSES * (T - 1) // 2) + (j + p * (T - 1) // 2)

    def gathers(pool, l, p):
        def step(t, b, n, j):
            if n == P:
                G.gather(pool, block_q(l, p, t), b)
        tiles(pool, step)

    with nc.Fori(0, LAYERS) as l:
        with nc.Block() as block:
            @block.sync
            def _(sp):
                loads = [(Wqkv[:, :, i * D:(i + 1) * D], A["L0_mix_W" + x][l, :, :].rearrange("(c p) n -> p c n", p=P)) for i, x in enumerate("qkv")]
                loads += [(Wo[:, :, :], A["L0_mix_Wo"][l, :, :].rearrange("(c p) n -> p c n", p=P)),
                          (W1[:, :, :], A["L0_mix_W1"][l, :, :].rearrange("(c p) n -> p c n", p=P)),
                          (W2[:, :, :], A["L0_mix_W2"][l, :, :].rearrange("(c p) n -> p c n", p=P)),
                          (bo, A["L0_mix_bo"][bass.ds(l, 1), :]), (b2, A["L0_mix_b2"][bass.ds(l, 1), :]),
                          (b1, A["L0_mix_b1"][bass.ds(l, 1), :])]
                for i, x in enumerate(("ln1_g", "ln1_b", "ln2_g", "ln2_b")):
                    loads.append((ln[:, i, :], A["L0_mix_" + x][l, :].rearrange("(c p) -> p c", p=P)))
                for dst, src in loads:
                    sp.dma_start(dst, src, allow_slow_non_contiguous=True).then_inc(w_in, 16)
                n = 16 * len(loads)
                hold(sp, w_in, l * n + (n + 16))

            @block.vector
            def _(v):
                V.memset(KM[:, :], LOWEST)
                tiles(v, lambda t, b, n, j: e.row_stats(v, t))

        e.rstd_block(l * 2 + 1)

        with ExitStack() as own:
            XS, HT = e.sb("XS", [P, 2, D], f32, own), e.sb("HT", [P, 2, D], f32, own)
            KV, QS = e.sb("KV", [P, 2, 2 * D], f32, own), e.sb("QS", [P, 2, D], f32, own)
            QE, QT = e.sb("QE", [P, 2, D], f32, own), e.sb("QT", [P, 2, D], f32, own)
            QM = e.sb("QM", [P, 2, 2, HEADS], f32, own)
            psT, psQ = e.pb("psT", [P, BANK], own), e.pb("psQ", [P, BANK], own)
            psKV, psQT = e.pb("psKV", [P, BANK], own), e.pb("psQT", [P, BANK], own)

            def heads(ap):
                return ap.rearrange("p (h d) -> p h d", h=HEADS)

            with nc.Block() as block:
                @block.gpsimd
                def _(pool):
                    gathers(pool, l, 0)

                @block.vector
                def _(v):
                    def xn(t, b):
                        e.normalise(t, XS[:, b, :]).then_inc(xn_ready, 1)

                    def step(t, b, n, j):
                        if n == P:
                            xn(t + 1, 1 - b)
                            G.stage(block_q(l, 0, t) + 1, 1 - b)
                        mx, sm = QM[:, b, 0, :], QM[:, b, 1, :]
                        v.wait_ge(qkv_ready, l * T + (t + 1))
                        V.tensor_reduce(mx, heads(psQ[:, 0:D]), AX.X, ALU.max)
                        v.drain()
                        V.tensor_tensor(heads(QS[:, b, :]), heads(psQ[:, 0:D]), mx.unsqueeze(2).to_broadcast([P, HEADS, DH]),
                                        ALU.subtract).then_inc(qsub_ready, 1)
                        hold(v, kv_ready, l * T + (t + 1))
                        V.tensor_tensor(KM[0:n, :], KM[0:n, :], KV[0:n, b, 0:D], ALU.max)
                        if n == P:
                            G.accumulate(v, block_q(l, 0, t), b, psG, Y)
                        v.wait_ge(qexp_ready, l * T + (t + 1))
                        V.tensor_reduce(sm, heads(QE[:, b, :]), AX.X, ALU.add)
                        v.drain()
                        V.reciprocal(sm, sm)
                        v.drain()
                        V.tensor_tensor(heads(QE[:, b, :]), heads(QE[:, b, :]), sm.unsqueeze(2).to_broadcast([P, HEADS, DH]),
                                        ALU.mult).then_inc(qn_ready, 1)
                    xn(0, 0)
                    tiles(v, step)

                @block.tensor
                def _(pe):
                    def turn(t, b):
                        pe.wait_ge(xn_ready, l * T + (t + 1))
                        e.transpose_tile(psT[:, 0:D], XS[:, b, :]).then_inc(tp_ready, 1)

                    def step(t, b, n, j):
                        pe.wait_ge(ht_ready, l * T + (t + 1))
                        if n == P:
                            turn(t + 1, 1 - b)
                        for ps, lo, hi in ((psQ, 0, D), (psKV, D, 3 * D)):
                            for c in range(HALF):
                                last = nc.tensor.matmul(ps[:, 0:hi - lo], HT[:, b, c * P:(c + 1) * P], Wqkv[:, c, lo:hi],
                                                        start=(c == 0), stop=(c == HALF - 1))
                        last.then_inc(qkv_ready, 1)
                        if n == P:
                            G.add_up(pe, block_q(l, 0, t), b, block_j(l, 0, j), psG)
                        pe.wait_ge(qn_ready, l * T + (t + 1))
                        e.transpose_tile(psQT[:, 0:D], QE[:, b, :]).then_inc(qt_ready, 1)
                    turn(0, 0)
                    tiles(pe, step)

                @block.scalar
                def _(act):
                    def ht(t, b):
                        act.wait_ge(tp_ready, l * T + (t + 1))
                        for c in range(HALF):
                            last = S.activation(HT[:, b, c * P:(c + 1) * P], psT[:, c * P:(c + 1) * P], ACT.Identity,
                                                bias=ln[:, 1, c:c + 1], scale=ln[:, 0, c:c + 1])
                        last.then_inc(ht_ready, 1)

                    def step(t, b, n, j):
                        if n == P:
                            ht(t + 1, 1 - b)
                        hold(act, kv_stored, l * (T + 2) + (t + 1))
                        act.wait_ge(qkv_ready, l * T + (t + 1))
                        S.activation(KV[:, b, :], psKV[:, :], ACT.Copy).then_inc(kv_ready, 1)
                        act.wait_ge(qsub_ready, l * T + (t + 1))
                        S.activation(QE[:, b, :], QS[:, b, :], ACT.Exp, scale=QK_SCALE).then_inc(qexp_ready, 1)
                        hold(act, q_stored, l * (T + 2) + (t + 1))
                        act.wait_ge(qt_ready, l * T + (t + 1))
                        S.activation(QT[:, b, :], psQT[:, 0:D], ACT.Copy).then_inc(qts_ready, 1)
                    ht(0, 0)
                    tiles(act, step)

                @block.sync
                def _(sp):
                    for stored in (kv_stored, q_stored):
                        sp.sem_inc(stored, 2)

                    def step(t, b, n, j):
                        uses = l * (ODD if b else EVEN) + j
                        sp.wait_ge(kv_ready, l * T + (t + 1))
                        sp.dma_start(e.k_d[bass.ds(t * P, P), :], KV[:, b, 0:D]).then_inc(kv_out[b], 16)
                        sp.dma_start(e.v_d[bass.ds(t * P, P), :], KV[:, b, D:2 * D]).then_inc(kv_out[b], 16)
                        sp.wait_ge(kv_out[b], uses * 32 + 32)
                        sp.sem_inc(kv_stored, 1)
                        sp.wait_ge(qts_ready, l * T + (t + 1))
                        sp.dma_start(e.q_d[bass.ds(t * P, P), :], QT[:, b, :]).then_inc(q_out[b], 16)
                        sp.wait_ge(q_out[b], uses * 16 + 16)
                        sp.sem_inc(q_stored, 1)
                    tiles(sp, step)

        with ExitStack() as own:
            KIN, KE = e.sb("KIN", [P, 2, D], f32, own), e.sb("KE", [P, 2, D], f32, own)
            VIN = e.sb("VIN", [P, 2, HALF, P + 1], f32, own)
            diag, km2 = e.sb("diag", [P, HALF, P], f32, own), e.sb("km2", [P, HALF], f32, own)
            CN, CNT = e.sb("CN", [P, HALF, P], f32, own), e.sb("CNT", [P, HALF, P], f32, own)
            psC = e.pb("psC", [P, HALF, BANK], own)
            psA, psB = e.pb("psA", [P, BANK], own), e.pb("psB", [P, BANK], own)
            with nc.Block() as block:
                @block.tensor
                def _(pe):
                    e.transpose_tile(psA[:, 0:D], KM[:, :]).then_inc(kmt_ready, 1)
                    pe.wait_ge(diag_ready, l + 1)
                    for c in range(HALF):
                        last = nc.tensor.matmul(psB[:, c * P:(c + 1) * P], ones[:, :], diag[:, c, :], start=True, stop=True)
                    last.then_inc(kmb_ready, 1)

                @block.vector
                def _(v):
                    V.memset(VIN[:, :, :, P:P + 1], 1.0)
                    v.wait_ge(kmt_ready, l + 1)
                    V.tensor_reduce(km2[:, :], psA[:, 0:D].rearrange("p (c n) -> p c n", c=HALF), AX.X, ALU.max)
                    v.drain()
                    for c in range(HALF):
                        last = V.tensor_scalar(diag[:, c, :], ident[:, :], km2[:, c:c + 1], None, ALU.mult)
                    last.then_inc(diag_ready, 1)
                    v.wait_ge(kmb_ready, l + 1)
                    V.tensor_copy(KM[:, :], psB[:, 0:D])

            with nc.Block() as block:
                @block.gpsimd
                def _(pool):
                    gathers(pool, l, 1)

                @block.sync
                def _(sp):
                    def step(t, b, n, j):
                        hold(sp, ctx_done, l * (T + 2) + (t + 1))
                        sp.dma_start(KIN[:, b, :], e.k_d[bass.ds(t * P, P), :]).then_inc(kv_in[b], 16)
                        sp.dma_start(VIN[:, b, :, 0:P], e.v_d[bass.ds(t * P, P), :].rearrange("p (c n) -> p c n", c=HALF)).then_inc(kv_in[b], 16)
                    tiles(sp, step)

                @block.vector
                def _(v):
                    def step(t, b, n, j):
                        if n == P:
                            G.stage(block_q(l, 1, t) + 1, 1 - b)
                        v.wait_ge(kv_in[b], (l * (ODD if b else EVEN) + j) * 32 + 32)
                        V.tensor_tensor(KIN[:, b, :], KIN[:, b, :], KM[:, :], ALU.subtract).then_inc(ks_ready, 1)
                        if n == P:
                            G.accumulate(v, block_q(l, 1, t), b, psG, Y)
                    tiles(v, step)

                @block.scalar
                def _(act):
                    def step(t, b, n, j):
                        act.wait_ge(ks_ready, l * T + (t + 1))
                        S.activation(KE[:, b, :], KIN[:, b, :], ACT.Exp, scale=QK_SCALE).then_inc(ke_ready, 1)
                    tiles(act, step)

                @block.tensor
                def _(pe):
                    pe.sem_inc(ctx_done, 2)

                    def step(t, b, n, j):
                        pe.wait_ge(ke_ready, l * T + (t + 1))
                        for c in range(HALF):
                            last = nc.tensor.matmul(psC[:, c, 0:P + 1], KE[0:n, b, c * P:(c + 1) * P], VIN[0:n, b, c, :],
                                                    start=False, stop=(n != P))
                        last.then_inc(ctx_done, 1)
                        if n == P:
                            G.add_up(pe, block_q(l, 1, t), b, block_j(l, 1, j), psG)
                    for c in range(HALF):
                        nc.tensor.matmul(psC[:, c, 0:P + 1], e.zeros[0:1, 0:P], e.zeros[0:1, 0:P + 1], start=True, stop=False)
                    tiles(pe, step)

            with nc.Block() as block:
                @block.vector
                def _(v):
                    for c in range(HALF):
                        V.reciprocal(km2[:, c:c + 1], psC[:, c, P:P + 1])
                    v.drain()
                    for c in range(HALF):
                        last = V.scalar_tensor_tensor(CN[:, c, :], psC[:, c, 0:P], km2[:, c:c + 1], head_block[:, :], ALU.mult, ALU.mult)
                    last.then_inc(cn_ready, 1)
                    v.wait_ge(cnt_ready, l + 1)
                    V.tensor_copy(CNT[:, :, :], psA[:, 0:D].rearrange("p (c n) -> p c n", c=HALF)).then_inc(cnt_copied, 1)
                    v.wait_ge(mx_ready, l + 1)
                    V.tensor_copy(MX[:, :, :], psB[:, :].rearrange("p (c n) -> p c n", c=HALF))

                @block.tensor
                def _(pe):
                    pe.wait_ge(cn_ready, l + 1)
                    for c in range(HALF):
                        last = nc.tensor.transpose(psA[:, c * P:(c + 1) * P], CN[:, c, :], ident[:, :])
                    last.then_inc(cnt_ready, 1)
                    pe.wait_ge(cnt_copied, l + 1)
                    for c in range(HALF):
                        last = nc.tensor.matmul(psB[:, c * D:(c + 1) * D], CNT[:, c, :], Wo[:, c, :], start=True, stop=True)
                    last.then_inc(mx_ready, 1)

        with ExitStack() as own:
            QIN = e.sb("QIN", [P, 2, D], f32, own)
            psF = e.pb("psF", [P, 2, BANK], own)
            with nc.Block() as block:
                @block.gpsimd
                def _(pool):
                    gathers(pool, l, 2)

                @block.sync
                def _(sp):
                    def step(t, b, n, j):
                        hold(sp, q_used, l * (T + 2) + (t + 1))
                        sp.dma_start(QIN[:, b, :], e.q_d[bass.ds(t * P, P), :]).then_inc(q_in[b], 16)
                    tiles(sp, step)

                @block.tensor
                def _(pe):
                    pe.sem_inc(q_used, 2)

                    def step(t, b, n, j):
                        pe.wait_ge(att_added, l * (T + 2) + (t + 1))
                        nc.tensor.matmul(psF[:, b, 0:D], ones[0:1, :], bo, start=True, stop=False)
                        pe.wait_ge(q_in[b], (l * (ODD if b else EVEN) + j) * 16 + 16)
                        for c in range(HALF):
                            last = nc.tensor.matmul(psF[:, b, 0:D], QIN[:, b, c * P:(c + 1) * P], MX[:, c, :],
                                                    start=False, stop=(c == HALF - 1))
                        last.then_inc(q_used, 1)
                        if n == P:
                            G.add_up(pe, block_q(l, 2, t), b, block_j(l, 2, j), psG)
                    tiles(pe, step)

                @block.vector
                def _(v):
                    v.sem_inc(att_added, 2)

                    def step(t, b, n, j):
                        if n == P:
                            G.stage(block_q(l, 2, t) + 1, 1 - b)
                        hold(v, q_used, l * (T + 2) + (t + 3))
                        V.tensor_tensor(X[:, t, :], X[:, t, :], psF[:, b, 0:D], ALU.add).then_inc(att_added, 1)
                        v.drain()
                        e.row_stats(v, t)
                        if n == P:
                            G.accumulate(v, block_q(l, 2, t), b, psG, Y)
                    tiles(v, step)

        e.rstd_block(l * 2 + 2)

        with ExitStack() as own:
            XS, HT = e.sb("XS3", [P, 2, D], f32, own), e.sb("HT3", [P, 2, D], f32, own)
            GT = e.sb("GT", [P, MF, P], f32, own)
            psT, psF = e.pb("psT3", [P, BANK], own), e.pb("psF3", [P, BANK], own)
            psU = e.pb("psU", [P, MF, P], own)
            with nc.Block() as block:
                @block.gpsimd
                def _(pool):
                    gathers(pool, l, 3)

                @block.vector
                def _(v):
                    v.sem_inc(down_added, 1)

                    def xn(t, b):
                        e.normalise(t, XS[:, b, :]).then_inc(xn2_ready, 1)

                    def step(t, b, n, j):
                        if n == P:
                            xn(t + 1, 1 - b)
                            G.stage(block_q(l, 3, t) + 1, 1 - b)
                            G.accumulate(v, block_q(l, 3, t), b, psG, Y)
                        hold(v, down_ready, l * T + (t + 1))
                        V.tensor_tensor(X[:, t, :], X[:, t, :], psF[:, 0:D], ALU.add).then_inc(down_added, 1)
                    xn(0, 0)
                    tiles(v, step)

                @block.scalar
                def _(act):
                    def ht(t, b):
                        act.wait_ge(tp2_ready, l * T + (t + 1))
                        for c in range(HALF):
                            last = S.activation(HT[:, b, c * P:(c + 1) * P], psT[:, c * P:(c + 1) * P], ACT.Identity,
                                                bias=ln[:, 3, c:c + 1], scale=ln[:, 2, c:c + 1])
                        last.then_inc(ht2_ready, 1)

                    def step(t, b, n, j):
                        if n == P:
                            ht(t + 1, 1 - b)
                        act.wait_ge(up_ready, l * T + (t + 1))
                        for h in range(2):
                            last = S.activation(GT[:, h * MF // 2:(h + 1) * MF // 2, :], psU[:, h * MF // 2:(h + 1) * MF // 2, :], ACT.Gelu)
                        last.then_inc(gelu_ready, 1)
                    ht(0, 0)
                    tiles(act, step)

                @block.tensor
                def _(pe):
                    def turn(t, b):
                        pe.wait_ge(xn2_ready, l * T + (t + 1))
                        e.transpose_tile(psT[:, 0:D], XS[:, b, :]).then_inc(tp2_ready, 1)

                    def step(t, b, n, j):
                        pe.wait_ge(ht2_ready, l * T + (t + 1))
                        if n == P:
                            turn(t + 1, 1 - b)
                        for m in range(MF):
                            nc.tensor.matmul(psU[:, m, :], b1[:, m * P:(m + 1) * P], ones[0:1, :], start=True, stop=False)
                            for c in range(HALF):
                                last = nc.tensor.matmul(psU[:, m, :], W1[:, c, m * P:(m + 1) * P], HT[:, b, c * P:(c + 1) * P],
                                                        start=False, stop=(c == HALF - 1))
                        last.then_inc(up_ready, 1)
                        if n == P:
                            G.add_up(pe, block_q(l, 3, t), b, block_j(l, 3, j), psG)
                        pe.wait_ge(down_added, l * (T + 1) + (t + 1))
                        nc.tensor.matmul(psF[:, 0:D], ones[0:1, :], b2, start=True, stop=False)
                        pe.wait_ge(gelu_ready, l * T + (t + 1))
                        for m in range(MF):
                            last = nc.tensor.matmul(psF[:, 0:D], GT[:, m, :], W2[:, m, :], start=False, stop=(m == MF - 1))
                        last.then_inc(down_ready, 1)
                    turn(0, 0)
                    tiles(pe, step)
    layer.close()
    e.G.append(G)
    e.G.append(psG)


def sum_phase(nc, A, e):
    X, Y, ones, tiles, hold = e.X, e.Y, e.ones, e.tiles, e.hold
    V = nc.vector
    G, psG = e.G
    left = GNN_BLOCKS - MIXED
    assert left % 2 == 0 and left > 2 and MIXED % 2 == 0
    with nc.Block() as block:
        def blocks(eng, step):
            with eng.Fori(0, left // 2 - 1) as j:
                for b in range(2):
                    step(j * 2 + (MIXED + b), b, j + MIXED // 2, True)
            for b in range(2):
                step(GNN_BLOCKS - 2 + b, b, GNN_BLOCKS // 2 - 1, b == 0)

        @block.gpsimd
        def _(pool):
            blocks(pool, lambda q, b, j, more: G.gather(pool, q, b))

        @block.tensor
        def _(pe):
            blocks(pe, lambda q, b, j, more: G.add_up(pe, q, b, j, psG))

        @block.vector
        def _(v):
            def step(q, b, j, more):
                if more:
                    G.stage(q + 1, 1 - b)
                G.accumulate(v, q, b, psG, Y)
            blocks(v, step)

    with ExitStack() as own:
        bn = e.sb("bn", [P, 4, D], f32, own)
        neg_mean, scale, shift, work = (bn[:, i, :] for i in range(4))
        gb = e.sb("gb", [1, 2 * D], f32, own)
        SQ, XI = e.sb("SQ", [P, 2, D], f32, own), e.sb("XI", [P, 2, D], f32, own)
        ps = e.pb("psBN", [P, 2, BANK], own)
        gb_in, sums_ready, centred, sq_ready, sq_used = e.sem("gb_in"), e.sem("sums_ready"), e.sem("centred"), e.sem("sq_ready"), e.sem("sq_used")
        gb_ready, v_ready, sd_ready, x_used, xi_in = e.sem("gb_ready"), e.sem("bn_v_ready"), e.sem("bn_sd_ready"), e.sem("x_used"), e.sem2("xi_in")
        with nc.Block() as block:
            @block.sync
            def _(sp):
                sp.dma_start(gb[:, 0:D], A["L0_gnn_gamma"].rearrange("(a n) -> a n", a=1)).then_inc(gb_in, 16)
                sp.dma_start(gb[:, D:2 * D], A["L0_gnn_beta"].rearrange("(a n) -> a n", a=1)).then_inc(gb_in, 16)
                sp.wait_ge(gb_in, 32)

            @block.tensor
            def _(pe):
                nc.tensor.matmul(ps[:, 0, 0:D], e.zeros[0:1, 0:P], e.zeros[0:1, 0:D], start=True, stop=False)
                tiles(pe, lambda t, b, n, j: nc.tensor.matmul(ps[:, 0, 0:D], ones[0:n, :], Y[0:n, t, :], start=False, stop=(n != P)))

        with nc.Block() as block:
            @block.vector
            def _(v):
                V.tensor_scalar(neg_mean, ps[:, 0, 0:D], -1.0 / N, None, ALU.mult)
                v.drain()
                tiles(v, lambda t, b, n, j: V.tensor_tensor(Y[:, t, :], Y[:, t, :], neg_mean, ALU.add).then_inc(centred, 1))

            @block.scalar
            def _(act):
                def step(t, b, n, j):
                    hold(act, sq_used, t + 1)
                    act.wait_ge(centred, t + 1)
                    nc.scalar.activation(SQ[:, b, :], Y[:, t, :], ACT.Square).then_inc(sq_ready, 1)
                tiles(act, step)

            @block.tensor
            def _(pe):
                pe.sem_inc(sq_used, 2)

                def step(t, b, n, j):
                    pe.wait_ge(sq_ready, t + 1)
                    nc.tensor.matmul(ps[:, 1, 0:D], ones[0:n, :], SQ[0:n, b, :], start=False, stop=(n != P)).then_inc(sq_used, 1)
                nc.tensor.matmul(ps[:, 1, 0:D], e.zeros[0:1, 0:P], e.zeros[0:1, 0:D], start=True, stop=False)
                tiles(pe, step)

        with nc.Block() as block:
            @block.tensor
            def _(pe):
                nc.tensor.matmul(ps[:, 0, :], ones[0:1, :], gb[:, :], start=True, stop=True).then_inc(gb_ready, 1)

            @block.scalar
            def _(act):
                act.wait_ge(v_ready, 1)
                nc.scalar.activation(scale, work, ACT.Sqrt).then_inc(sd_ready, 1)

            @block.vector
            def _(v):
                V.tensor_scalar(work, ps[:, 1, 0:D], 1.0 / N, EPS, ALU.mult, ALU.add).then_inc(v_ready, 1)
                v.wait_ge(sd_ready, 1)
                V.reciprocal(scale, scale)
                v.drain()
                V.tensor_tensor(neg_mean, scale, scale, ALU.mult)
                v.drain()
                V.tensor_tensor(neg_mean, neg_mean, work, ALU.mult)
                v.drain()
                V.tensor_scalar(neg_mean, neg_mean, -0.5, 1.5, ALU.mult, ALU.add)
                v.drain()
                V.tensor_tensor(scale, scale, neg_mean, ALU.mult)
                v.wait_ge(gb_ready, 1)
                V.tensor_copy(shift, ps[:, 0, D:2 * D])
                v.drain()
                V.tensor_tensor(scale, scale, ps[:, 0, 0:D], ALU.mult)

        with nc.Block() as block:
            @block.sync
            def _(sp):
                def step(t, b, n, j):
                    hold(sp, x_used, t + 1)
                    sp.dma_start(XI[0:n, b, :], A["x"][bass.ds(t * P, n), :] if n == P else A["x"][N - n:N, :]).then_inc(xi_in[b], 16)
                tiles(sp, step)

            @block.vector
            def _(v):
                v.sem_inc(x_used, 2)

                def step(t, b, n, j):
                    V.tensor_tensor(Y[:, t, :], Y[:, t, :], scale, ALU.mult)
                    v.drain()
                    V.tensor_tensor(Y[:, t, :], Y[:, t, :], shift, ALU.add)
                    v.drain()
                    V.scalar_tensor_tensor(X[:, t, :], Y[:, t, :], 0.0, X[:, t, :], ALU.max, ALU.add)
                    v.drain()
                    hold(v, xi_in[b], j * 16 + 16)
                    V.tensor_tensor(X[0:n, t, :], X[0:n, t, :], XI[0:n, b, :], ALU.add).then_inc(x_used, 1)
                    v.drain()
                    e.row_stats(v, t)
                tiles(v, step)


def expert_phase(nc, A, out, e):
    X, ident, ones, tiles, hold = e.X, e.ident, e.ones, e.tiles, e.hold
    V, S = nc.vector, nc.scalar
    phase = e.ctx.enter_context(ExitStack())
    e.rstd_block(2 * LAYERS + 1)
    gate = e.sb("gate", [P, T, NE], f32, phase)

    with ExitStack() as own:
        att = e.sb("att", [P, 5 * HE], f32, own)
        att_row = e.sb("att_row", [1, 5 * HE], f32, own)
        Wg = e.sb("Wg", [P, HALF, HE], f32, own)
        tab = e.sb("tab", [P, T, TAB], f32, own)
        am = e.sb("am", [P, T, 2 * GH], f32, own)
        best = e.sb("best", [P, T, GH], f32, own)
        acc = e.sb("acc", [P, T, MSG], f32, own)
        wk = e.sb("wk", [P, T, HE], f32, own)
        wk4, wk4b = e.sb("wk4", [P, T, GH], f32, own), e.sb("wk4b", [P, T, GH], f32, own)
        up = e.sb("up", [P, 2, GH], f32, own)
        att_rows = ["L0_ffn_att_src", "L0_ffn_att_dst", "L0_ffn_b_gat", "L0_ffn_ln_gamma", "L0_ffn_ln_beta"]

        def over_tiles(i):
            return att[:, i * HE:(i + 1) * HE].unsqueeze(1).to_broadcast([P, T, HE])

        def by_head(ap):
            return ap.rearrange("p t (h x) -> p t h x", h=GH)

        def each_head(ap, n):
            return ap.unsqueeze(3).to_broadcast([P, T, GH, n])

        with ExitStack() as own2:
            XS, HT = e.sb("XS4", [P, 2, D], f32, own2), e.sb("HT4", [P, 2, D], f32, own2)
            psT, psH, psR = e.pb("psT4", [P, BANK], own2), e.pb("psH", [P, 2, BANK], own2), e.pb("psR", [P, BANK], own2)
            g_in, row_ready, xn_ready, tp_ready, ht_ready = e.sem("g_in"), e.sem("row_ready"), e.sem("xn4_ready"), e.sem("tp4_ready"), e.sem("ht4_ready")
            h_ready, max_ready, all_ready, tab_ready, tab_out = e.sem("h_ready"), e.sem("max_ready"), e.sem("all_ready"), e.sem("tab_ready"), e.sem("tab_out")
            with nc.Block() as block:
                @block.sync
                def _(sp):
                    sp.dma_start(Wg[:, :, :], A["L0_ffn_W_gat"].rearrange("(c p) n -> p c n", p=P)).then_inc(g_in, 16)
                    for i, name in enumerate(att_rows):
                        a = A[name]
                        a = a.rearrange("(a h) e -> a (h e)", a=1) if i < 2 else a.rearrange("(a n) -> a n", a=1)
                        sp.dma_start(att_row[:, i * HE:(i + 1) * HE], a).then_inc(g_in, 16)
                    sp.wait_ge(tab_ready, 1)
                    sp.dma_start(e.tab_d.rearrange("(t p) c -> p t c", p=P), tab[:, :, :]).then_inc(tab_out, 16)
                    sp.wait_ge(tab_out, 16)

                @block.tensor
                def _(pe):
                    pe.wait_ge(g_in, 96)
                    nc.tensor.matmul(psR[:, 0:5 * HE], ones[0:1, :], att_row[:, :], start=True, stop=True).then_inc(row_ready, 1)

                    def turn(t, b):
                        pe.wait_ge(xn_ready, t + 1)
                        e.transpose_tile(psT[:, 0:D], XS[:, b, :]).then_inc(tp_ready, 1)

                    def step(t, b, n, j):
                        pe.wait_ge(ht_ready, t + 1)
                        if n == P:
                            turn(t + 1, 1 - b)
                        for c in range(HALF):
                            last = nc.tensor.matmul(psH[:, b, 0:HE], HT[:, b, c * P:(c + 1) * P], Wg[:, c, :], start=(c == 0), stop=(c == HALF - 1))
                        last.then_inc(h_ready, 1)
                    turn(0, 0)
                    tiles(pe, step)

                @block.scalar
                def _(act):
                    def step(t, b, n, j):
                        act.wait_ge(tp_ready, t + 1)
                        S.activation(HT[:, b, :], psT[:, 0:D], ACT.Copy).then_inc(ht_ready, 1)
                    tiles(act, step)

                @block.gpsimd
                def _(pool):
                    pool.wait_ge(max_ready, 1)
                    nc.gpsimd.partition_all_reduce(up[:, 1, :], up[:, 0, :], P, bass.bass_isa.ReduceOp.max).then_inc(all_ready, 1)

                @block.vector
                def _(v):
                    def xn(t, b):
                        e.normalise(t, XS[:, b, :]).then_inc(xn_ready, 1)

                    def step(t, b, n, j):
                        if n == P:
                            xn(t + 1, 1 - b)
                        hold(v, h_ready, t + 1)
                        V.tensor_copy(tab[:, t, 0:HE], psH[:, b, 0:HE])
                    xn(0, 0)
                    tiles(v, step)
                    v.wait_ge(row_ready, 1)
                    V.tensor_copy(att[:, :], psR[:, 0:5 * HE])
                    v.drain()
                    for i, dst in enumerate((tab[:, :, HE:HE + GH], am[:, :, 0:GH])):
                        V.tensor_tensor(wk[:, :, :], tab[:, :, 0:HE], over_tiles(i), ALU.mult)
                        v.drain()
                        V.tensor_reduce(dst, by_head(wk[:, :, :]), AX.X, ALU.add)
                        v.drain()
                    V.tensor_scalar(wk4[:, :, :], tab[:, :, HE:HE + GH], -1.0, None, ALU.mult)
                    v.drain()
                    V.tensor_reduce(up[:, 0, :], wk4[:, :, :].rearrange("p t h -> p h t"), AX.X, ALU.max).then_inc(max_ready, 1)
                    v.wait_ge(all_ready, 1)
                    V.tensor_tensor(tab[:, :, HE + GH:TAB], tab[:, :, HE:HE + GH], up[:, 1, :].unsqueeze(1).to_broadcast([P, T, GH]), ALU.add).then_inc(tab_ready, 1)
                    v.drain()
                    V.tensor_copy(best[:, :, :], tab[:, :, HE + GH:TAB])

        kept = own.enter_context(ExitStack())
        tile_row = e.sb("gat_tile_row", [1, GAT_G * GAT_Q], i16, kept)
        rows_all = e.sb("rows_all", [P, GAT_G * GAT_Q, MSG], f32, kept)
        BLOCKS = GAT_BLOCKS
        assert BLOCKS % 2 == 0

        def onehots(dst, q):
            for s in range(UB):
                last = V.tensor_scalar(dst[:, s, :], e.node_no[:, :], e.gat_node[:, bass.ds(q * UB + s, 1)], None, ALU.is_equal)
            return last

        with ExitStack() as own2:
            numbers = e.sb("gat_numbers", [P, 2, UB], i32, own2)
            oh = e.sb("gat_onehot", [P, 2, UB, P], f32, own2)
            rows = e.sb("gat_rows", [P, 2, UB, TAB], f32, own2)
            diag = e.sb("gat_diag", [P, 2, UB, GH, P], f32, own2)
            most = e.sb("gat_most", [P, UB, GH], f32, own2)
            psM = e.pb("psM", [P, 2, UB, GH * P], own2)
            row_in, num_ready, oh_ready, diag_ready, masked = e.sem("gat_row_in"), e.sem("gat_num_ready"), e.sem("gat_oh_ready"), e.sem("gat_diag_ready"), e.sem("gat_masked")
            gathered = [e.sem(f"gat_gathered{i}") for i in range(2 * UB)]

            def blocks(eng, step):
                with eng.Fori(0, BLOCKS // 2 - 1) as j:
                    step(j * 2 + 1, 1, j, True)
                    step(j * 2 + 2, 0, j + 1, True)
                step(BLOCKS - 1, 1, BLOCKS // 2 - 1, False)

            with nc.Block() as block:
                @block.sync
                def _(sp):
                    sp.dma_start(tile_row[:, :], e.gat_tile_d.rearrange("(a g) q -> a (g q)", a=1)).then_inc(row_in, 16)

                @block.gpsimd
                def _(pool):
                    def step(q, b, j, more):
                        hold(pool, num_ready, q + 1)
                        for s in range(UB):
                            nc.gpsimd.indirect_dma_start(out=rows[:, b, s, :], out_offset=None, in_=e.tab_d,
                                                         in_offset=bass.IndirectOffsetOnAxis(ap=numbers[:, b, s:s + 1], axis=0)).then_inc(gathered[b * UB + s], 16)
                    step(0, 0, 0, True)
                    blocks(pool, step)

                @block.tensor
                def _(pe):
                    def step(q, b, j, more):
                        pe.wait_ge(oh_ready, q + 1)
                        pe.wait_ge(diag_ready, q + 1)
                        for s in range(UB):
                            last = nc.tensor.matmul(psM[:, b, s, :], oh[:, b, s, :], diag[:, b, s, :, :].rearrange("p h n -> p (h n)"), start=True, stop=True)
                        last.then_inc(masked, 1)
                    step(0, 0, 0, True)
                    blocks(pe, step)

                @block.vector
                def _(v):
                    def number(q, b):
                        V.tensor_copy(numbers[:, b, :], e.gat_src[:, bass.ds(q * UB, UB)]).then_inc(num_ready, 1)

                    def spread(q, b, j):
                        for s in range(UB):
                            hold(v, gathered[b * UB + s], j * 16 + 16)
                        V.tensor_copy(rows_all[:, bass.ds(q * UB, UB), :], rows[:, b, :, 0:MSG])
                        for s in range(UB):
                            last = V.tensor_tensor(diag[:, b, s, :, :], ident[:, :].unsqueeze(1).to_broadcast([P, GH, P]),
                                                   rows[:, b, s, HE + GH:TAB].unsqueeze(2).to_broadcast([P, GH, P]), ALU.mult)
                        last.then_inc(diag_ready, 1)

                    def largest(q, b):
                        hold(v, masked, q + 1)
                        V.tensor_reduce(most[:, :, :].rearrange("p s h -> p (s h)"), psM[:, b, :, :].rearrange("p s (h n) -> p (s h) n", h=GH), AX.X, ALU.max)
                        v.drain()
                        for s in range(UB):
                            t = v.value_load(tile_row[0:1, bass.ds(q * UB + s, 1)], min_val=0, max_val=T - 1)
                            V.tensor_tensor(best[:, t, :], best[:, t, :], most[:, s, :], ALU.max)
                            v.drain()

                    def step(q, b, j, more):
                        if more:
                            number(q + 1, 1 - b)
                        spread(q, b, j)
                        largest(q - 1, 1 - b)
                        if more:
                            onehots(oh[:, 1 - b, :, :], q + 1).then_inc(oh_ready, 1)
                    hold(v, row_in, 16)
                    number(0, 0)
                    number(1, 1)
                    onehots(oh[:, 0, :, :], 0).then_inc(oh_ready, 1)
                    onehots(oh[:, 1, :, :], 1).then_inc(oh_ready, 1)
                    spread(0, 0, 0)
                    blocks(v, step)
                    largest(BLOCKS - 1, 1)

        own_ready, own_exp = e.sem("own_ready"), e.sem("own_exp")
        with nc.Block() as block:
            @block.vector
            def _(v):
                V.tensor_tensor(wk4[:, :, :], best[:, :, :], up[:, 1, :].unsqueeze(1).to_broadcast([P, T, GH]), ALU.subtract)
                v.drain()
                V.tensor_tensor(wk4[:, :, :], wk4[:, :, :], am[:, :, 0:GH], ALU.add)
                v.drain()
                V.scalar_tensor_tensor(am[:, :, GH:2 * GH], wk4[:, :, :], 0.2, wk4[:, :, :], ALU.mult, ALU.max)
                V.tensor_tensor(wk4b[:, :, :], tab[:, :, HE:HE + GH], am[:, :, 0:GH], ALU.add)
                v.drain()
                V.scalar_tensor_tensor(wk4[:, :, :], wk4b[:, :, :], 0.2, wk4b[:, :, :], ALU.mult, ALU.max)
                v.drain()
                V.tensor_tensor(wk4[:, :, :], wk4[:, :, :], am[:, :, GH:2 * GH], ALU.subtract).then_inc(own_ready, 1)
                v.wait_ge(own_exp, 1)
                V.tensor_tensor(by_head(acc[:, :, 0:HE]), by_head(tab[:, :, 0:HE]), each_head(acc[:, :, HE:MSG], NE), ALU.mult)

            @block.scalar
            def _(act):
                act.wait_ge(own_ready, 1)
                S.activation(acc[:, :, HE:MSG], wk4[:, :, :], ACT.Exp).then_inc(own_exp, 1)

        with ExitStack() as own2:
            oh = e.sb("sum_onehot", [P, 2, UB, P], f32, own2)
            oht = e.sb("sum_onehot_t", [P, 2, UB, P], f32, own2)
            ea, eb, ex = (e.sb("edge_" + x, [P, 2, UB, GH], f32, own2) for x in "abc")
            msg = e.sb("msg", [P, 2, UB, MSG], f32, own2)
            psO, psE, psS = e.pb("psO", [P, 2, BANK], own2), e.pb("psE", [P, 2, BANK], own2), e.pb("psS", [P, 2, BANK], own2)
            oh_ready, turned, oht_ready, ends_ready = e.sem("sum_oh_ready"), e.sem("sum_turned"), e.sem("sum_oht_ready"), e.sem("sum_ends_ready")
            e_ready, ex_ready, msg_ready, sum_ready = e.sem("sum_e_ready"), e.sem("sum_ex_ready"), e.sem("sum_msg_ready"), e.sem("sum_ready")

            def blocks(eng, step):
                with eng.Fori(0, BLOCKS // 2 - 1) as j:
                    for b in range(2):
                        step(j * 2 + b, b, True)
                step(BLOCKS - 2, 0, True)
                step(BLOCKS - 1, 1, False)

            with nc.Block() as block:
                @block.vector
                def _(v):
                    def step(q, b, more):
                        if more:
                            onehots(oh[:, 1 - b, :, :], q + 1).then_inc(oh_ready, 1)
                        here = rows_all[:, bass.ds(q * UB, UB), :]
                        ends = psE[:, b, 0:UB * 2 * GH].rearrange("p (s x) -> p s x", s=UB)
                        hold(v, ends_ready, q + 1)
                        V.tensor_tensor(ea[:, b, :, :], here[:, :, HE:MSG], ends[:, :, 0:GH], ALU.add)
                        v.drain()
                        V.scalar_tensor_tensor(eb[:, b, :, :], ea[:, b, :, :], 0.2, ea[:, b, :, :], ALU.mult, ALU.max)
                        v.drain()
                        V.tensor_tensor(ea[:, b, :, :], eb[:, b, :, :], ends[:, :, GH:2 * GH], ALU.subtract).then_inc(e_ready, 1)
                        hold(v, ex_ready, q + 1)
                        V.tensor_copy(msg[:, b, :, HE:MSG], ex[:, b, :, :])
                        V.tensor_tensor(msg[:, b, :, 0:HE].rearrange("p s (h x) -> p s h x", h=GH), here[:, :, 0:HE].rearrange("p s (h x) -> p s h x", h=GH),
                                        ex[:, b, :, :].unsqueeze(3).to_broadcast([P, UB, GH, NE]), ALU.mult).then_inc(msg_ready, 1)
                        hold(v, sum_ready, q + 1)
                        for s in range(UB):
                            t = v.value_load(tile_row[0:1, bass.ds(q * UB + s, 1)], min_val=0, max_val=T - 1)
                            V.tensor_tensor(acc[:, t, :], acc[:, t, :], psS[:, b, s * MSG:(s + 1) * MSG], ALU.add)
                            v.drain()
                    onehots(oh[:, 0, :, :], 0).then_inc(oh_ready, 1)
                    blocks(v, step)

                @block.scalar
                def _(act):
                    def ready(q, b):
                        act.wait_ge(turned, q + 1)
                        S.activation(oht[:, b, :, :].rearrange("p s n -> p (s n)"), psO[:, b, :], ACT.Copy).then_inc(oht_ready, 1)

                    def step(q, b, more):
                        if more:
                            ready(q + 1, 1 - b)
                        act.wait_ge(e_ready, q + 1)
                        S.activation(ex[:, b, :, :], ea[:, b, :, :], ACT.Exp).then_inc(ex_ready, 1)
                    ready(0, 0)
                    blocks(act, step)

                @block.tensor
                def _(pe):
                    def turn(q, b):
                        pe.wait_ge(oh_ready, q + 1)
                        for s in range(UB):
                            last = nc.tensor.transpose(psO[:, b, s * P:(s + 1) * P], oh[:, b, s, :], ident[:, :])
                        last.then_inc(turned, 1)

                    def step(q, b, more):
                        if more:
                            turn(q + 1, 1 - b)
                        hold(pe, oht_ready, q + 1)
                        for s in range(UB):
                            t = pe.value_load(tile_row[0:1, bass.ds(q * UB + s, 1)], min_val=0, max_val=T - 1)
                            last = nc.tensor.matmul(psE[:, b, s * 2 * GH:(s + 1) * 2 * GH], oht[:, b, s, :], am[:, t, :], start=True, stop=True)
                        last.then_inc(ends_ready, 1)
                        pe.wait_ge(msg_ready, q + 1)
                        for s in range(UB):
                            last = nc.tensor.matmul(psS[:, b, s * MSG:(s + 1) * MSG], oh[:, b, s, :], msg[:, b, s, :], start=True, stop=True)
                        last.then_inc(sum_ready, 1)
                    turn(0, 0)
                    blocks(pe, step)
        kept.close()

        gv_ready, gsd_ready, sx_ready, se_ready = e.sem("gv_ready"), e.sem("gsd_ready"), e.sem("sx_ready"), e.sem("se_ready")
        with ExitStack() as own2:
            one = [e.sb(f"one{i}", [P, T], f32, own2) for i in range(4)]
            score = e.sb("score", [P, T, NE], f32, own2)
            rank = e.sb("rank", [P, T, NE], f32, own2)

            def over(ap, n):
                return ap.unsqueeze(2).to_broadcast([P, T, n])

            with nc.Block() as block:
                @block.scalar
                def _(act):
                    act.wait_ge(gv_ready, 1)
                    S.activation(one[1][:, :], one[0][:, :], ACT.Sqrt).then_inc(gsd_ready, 1)
                    act.wait_ge(sx_ready, 1)
                    S.activation(gate[:, :, :], gate[:, :, :], ACT.Exp).then_inc(se_ready, 1)

                @block.vector
                def _(v):
                    def do(ins):
                        v.drain()
                        return ins
                    W = wk[:, :, :]
                    do(V.tensor_scalar(wk4[:, :, :], acc[:, :, HE:MSG], 1e-16, None, ALU.add))
                    do(V.reciprocal(wk4[:, :, :], wk4[:, :, :]))
                    do(V.tensor_tensor(by_head(W), by_head(acc[:, :, 0:HE]), each_head(wk4[:, :, :], NE), ALU.mult))
                    do(V.tensor_tensor(W, W, over_tiles(2), ALU.add))
                    do(V.tensor_reduce(one[0][:, :], W, AX.X, ALU.add))
                    do(V.tensor_scalar(one[0][:, :], one[0][:, :], 1.0 / HE, None, ALU.mult))
                    do(V.tensor_tensor(W, W, over(one[0][:, :], HE), ALU.subtract))
                    do(V.tensor_tensor(acc[:, :, 0:HE], W, W, ALU.mult))
                    do(V.tensor_reduce(one[0][:, :], acc[:, :, 0:HE], AX.X, ALU.add))
                    V.tensor_scalar(one[0][:, :], one[0][:, :], 1.0 / HE, EPS, ALU.mult, ALU.add).then_inc(gv_ready, 1)
                    v.wait_ge(gsd_ready, 1)
                    do(V.reciprocal(one[1][:, :], one[1][:, :]))
                    do(V.tensor_tensor(one[2][:, :], one[1][:, :], one[1][:, :], ALU.mult))
                    do(V.tensor_tensor(one[2][:, :], one[2][:, :], one[0][:, :], ALU.mult))
                    do(V.tensor_scalar(one[2][:, :], one[2][:, :], -0.5, 1.5, ALU.mult, ALU.add))
                    do(V.tensor_tensor(one[1][:, :], one[1][:, :], one[2][:, :], ALU.mult))
                    do(V.tensor_tensor(W, W, over(one[1][:, :], HE), ALU.mult))
                    do(V.tensor_tensor(W, W, over_tiles(3), ALU.mult))
                    do(V.tensor_tensor(W, W, over_tiles(4), ALU.add))
                    do(V.tensor_reduce(score[:, :, :], W.rearrange("p t (h x) -> p t x h", h=GH), AX.X, ALU.add))
                    do(V.tensor_scalar(score[:, :, :], score[:, :, :], 1.0 / GH, None, ALU.mult))
                    for i in range(NE):
                        do(V.memset(rank[:, :, i:i + 1], float(i)))
                    for i in range(NE):
                        for k in range(i + 1, NE):
                            do(V.tensor_tensor(one[2][:, :], score[:, :, k], score[:, :, i], ALU.is_gt))
                            do(V.tensor_tensor(rank[:, :, i], rank[:, :, i], one[2][:, :], ALU.add))
                            do(V.tensor_tensor(rank[:, :, k], rank[:, :, k], one[2][:, :], ALU.subtract))
                    do(V.tensor_scalar(rank[:, :, :], rank[:, :, :], 2.0, None, ALU.is_lt))
                    do(V.tensor_reduce(one[2][:, :], score[:, :, :], AX.X, ALU.max))
                    V.tensor_tensor(gate[:, :, :], score[:, :, :], over(one[2][:, :], NE), ALU.subtract).then_inc(sx_ready, 1)
                    v.wait_ge(se_ready, 1)
                    do(V.tensor_tensor(gate[:, :, :], gate[:, :, :], rank[:, :, :], ALU.mult))
                    do(V.tensor_reduce(one[3][:, :], gate[:, :, :], AX.X, ALU.add))
                    do(V.reciprocal(one[3][:, :], one[3][:, :]))
                    do(V.tensor_tensor(gate[:, :, :], gate[:, :, :], over(one[3][:, :], NE), ALU.mult))

    with ExitStack() as own:
        W1, W2 = e.sb("EW1", [P, HALF, NE, EF], f32, own), e.sb("EW2", [P, ME, NE, D], f32, own)
        b1, b2 = e.sb("Eb1", [1, NE * EF], f32, own), e.sb("Eb2", [1, NE * D], f32, own)
        XS, HT = e.sb("XS5", [P, 2, D], f32, own), e.sb("HT5", [P, 2, D], f32, own)
        GT = e.sb("EGT", [P, 2, EF], f32, own)
        psT, psU, psD = e.pb("psT5", [P, BANK], own), e.pb("psU5", [P, 2, BANK], own), e.pb("psD5", [P, 2, BANK], own)
        w_in, xn_ready, tp_ready, ht_ready = e.sem("ew_in"), e.sem("xn5_ready"), e.sem("tp5_ready"), e.sem("ht5_ready")
        up_ready, gelu_ready, down_ready, down_added, rows_out = e.sem("eup_ready"), e.sem("egelu_ready"), e.sem("edown_ready"), e.sem("edown_added"), e.sem("rows_out")
        with nc.Block() as block:
            @block.sync
            def _(sp):
                for x in range(NE):
                    sp.dma_start(W1[:, :, x, :], A["L0_ffn_W1"][x, :, :].rearrange("(c p) n -> p c n", p=P)).then_inc(w_in, 16)
                    sp.dma_start(W2[:, :, x, :], A["L0_ffn_W2"][x, :, :].rearrange("(c p) n -> p c n", p=P)).then_inc(w_in, 16)
                sp.dma_start(b1[:, :], A["L0_ffn_b1"].rearrange("(a e) n -> a (e n)", a=1)).then_inc(w_in, 16)
                sp.dma_start(b2[:, :], A["L0_ffn_b2"].rearrange("(a e) n -> a (e n)", a=1)).then_inc(w_in, 16)

                def step(t, b, n, j):
                    hold(sp, down_added, t * NE + (NE + 2))
                    sp.dma_start(out[bass.ds(t * P, P), :] if n == P else out[N - n:N, :], X[0:n, t, :]).then_inc(rows_out, 16)
                tiles(sp, step)
                sp.wait_ge(rows_out, T * 16)

            @block.vector
            def _(v):
                v.sem_inc(down_added, 2)

                def xn(t, b):
                    e.normalise(t, XS[:, b, :]).then_inc(xn_ready, 1)

                def step(t, b, n, j):
                    if n == P:
                        xn(t + 1, 1 - b)
                    for x in range(NE):
                        hold(v, down_ready, t * NE + (x + 1))
                        V.scalar_tensor_tensor(X[:, t, :], psD[:, x % 2, 0:D], gate[:, t, x:x + 1], X[:, t, :], ALU.mult, ALU.add).then_inc(down_added, 1)
                        v.drain()
                xn(0, 0)
                tiles(v, step)

            @block.scalar
            def _(act):
                def ht(t, b):
                    act.wait_ge(tp_ready, t + 1)
                    S.activation(HT[:, b, :], psT[:, 0:D], ACT.Copy).then_inc(ht_ready, 1)

                def step(t, b, n, j):
                    for x in range(NE):
                        act.wait_ge(up_ready, t * NE + (x + 1))
                        S.activation(GT[:, x % 2, :], psU[:, x % 2, :], ACT.Gelu).then_inc(gelu_ready, 1)
                        if x == 0 and n == P:
                            ht(t + 1, 1 - b)
                ht(0, 0)
                tiles(act, step)

            @block.tensor
            def _(pe):
                def turn(t, b):
                    pe.wait_ge(xn_ready, t + 1)
                    e.transpose_tile(psT[:, 0:D], XS[:, b, :]).then_inc(tp_ready, 1)

                def raise_up(t, b, x):
                    for m in range(ME):
                        at = psU[:, x % 2, m * P:(m + 1) * P]
                        nc.tensor.matmul(at, b1[:, x * EF + m * P:x * EF + (m + 1) * P], ones[0:1, :], start=True, stop=False)
                        for c in range(HALF):
                            last = nc.tensor.matmul(at, W1[:, c, x, m * P:(m + 1) * P], HT[:, b, c * P:(c + 1) * P], start=False, stop=(c == HALF - 1))
                    last.then_inc(up_ready, 1)

                def bring_down(t, x):
                    pe.wait_ge(down_added, t * NE + (x + 1))
                    nc.tensor.matmul(psD[:, x % 2, 0:D], ones[0:1, :], b2[:, x * D:(x + 1) * D], start=True, stop=False)
                    pe.wait_ge(gelu_ready, t * NE + (x + 1))
                    for m in range(ME):
                        last = nc.tensor.matmul(psD[:, x % 2, 0:D], GT[:, x % 2, m * P:(m + 1) * P], W2[:, m, x, :], start=False, stop=(m == ME - 1))
                    last.then_inc(down_ready, 1)

                def step(t, b, n, j):
                    for x in range(NE):
                        if x + 1 < NE:
                            raise_up(t, b, x + 1)
                        elif n == P:
                            pe.wait_ge(ht_ready, t + 2)
                            raise_up(t + 1, 1 - b, 0)
                        if x == 0 and n == P:
                            turn(t + 1, 1 - b)
                        bring_down(t, x)
                pe.wait_ge(w_in, 160)
                turn(0, 0)
                pe.wait_ge(ht_ready, 1)
                raise_up(0, 0, 0)
                tiles(pe, step)


_INS = ["x", "src", "dst", "L0_gnn_W0", "L0_gnn_b0", "L0_gnn_W1", "L0_gnn_b1", "L0_gnn_gamma", "L0_gnn_beta",
        "L0_mix_Wq", "L0_mix_Wk", "L0_mix_Wv", "L0_mix_Wo", "L0_mix_bo", "L0_mix_ln1_g", "L0_mix_ln1_b",
        "L0_mix_W1", "L0_mix_b1", "L0_mix_W2", "L0_mix_b2", "L0_mix_ln2_g", "L0_mix_ln2_b",
        "L0_ffn_W_gat", "L0_ffn_att_src", "L0_ffn_att_dst", "L0_ffn_b_gat", "L0_ffn_ln_gamma", "L0_ffn_ln_beta",
        "L0_ffn_W1", "L0_ffn_b1", "L0_ffn_W2", "L0_ffn_b2", "L0_ffn_edge_index"]
NOWHERE = -128


def kernel(**inputs):
    import numpy as np
    import concourse.bacc as bacc
    from concourse.bass_utils import run_bass_kernel_spmd

    def grouped(flat, groups, columns, fill):
        room = np.full((groups * P * columns,), fill, np.int32)
        room[:flat.shape[0]] = flat
        return room.reshape(groups, P, columns)

    arrays = {k: np.ascontiguousarray(inputs[k]) for k in _INS}
    src, dst = arrays.pop("src"), arrays.pop("dst")
    ei = arrays.pop("L0_ffn_edge_index")
    arrays["gnn_end"] = np.concatenate([grouped(dst, GNN_G // 2, GNN_C, NOWHERE), grouped(src, GNN_G // 2, GNN_C, NOWHERE)])
    arrays["gnn_start"] = np.concatenate([grouped(src, GNN_G // 2, GNN_C, 0), grouped(dst, GNN_G // 2, GNN_C, 0)])
    arrays["gat_end"] = grouped(ei[1], GAT_G, GAT_C, NOWHERE)
    arrays["gat_start"] = grouped(ei[0], GAT_G, GAT_C, 0)

    nc = bacc.Bacc("TRN2", target_bir_lowering=False, num_devices=1)
    A = {k: nc.dram_tensor(k, a.shape, mybir.dt.from_np(a.dtype), kind="ExternalInput").ap() for k, a in arrays.items()}
    out = nc.dram_tensor("out", (N, D), f32, kind="ExternalOutput").ap()
    build(nc, A, out)
    r = run_bass_kernel_spmd(nc, [arrays], core_ids=[0])
    return r.results[0]["out"]
```

```python
from contextlib import ExitStack

import concourse.bass as bass
from concourse import mybir

f32, f16, bf16, i32, i16 = mybir.dt.float32, mybir.dt.float16, mybir.dt.bfloat16, mybir.dt.int32, mybir.dt.int16
ALU, ACT, AX = mybir.AluOpType, mybir.ActivationFunctionType, mybir.AxisListType

P = 128
N, D = 6250, 256
BANK = 512
T = -(-N // P)
LAST = N - (T - 1) * P
EVEN, ODD = (T + 1) // 2, T // 2
HALF = D // P
EPS = 1e-5
LAYERS, HEADS, FF = 4, 8, 1024
DH = D // HEADS
MF = FF // P
QK_SCALE = float(DH) ** -0.25
LOWEST = -3.0e38
FIRST = object()
UB = 4
GNN_E, GAT_E = 206250, 131072
GNN_G, GNN_C = 8, -(-GNN_E // (4 * P))
GAT_G, GAT_C = 3, -(-GAT_E // (3 * P))
GNN_Q = -(-(GNN_C + T) // UB) * UB
GAT_Q = -(-(GAT_C + T) // UB) * UB
MAXC, MAXQ = max(GNN_C, GAT_C), max(GNN_Q, GAT_Q)
GNN_BLOCKS = GNN_G * GNN_Q // UB
GAT_BLOCKS = GAT_G * GAT_Q // UB
UC, SETS = 9, 3
TOGETHER = 7
BESIDE = ((0, 1), (2, 3), (4,), (5, 6), (7, 8), (9,))
SIX = len(BESIDE)
WITH_SIX = sum(len(x) for x in BESIDE)
WITH_LAYER = 3 * (T - 1) + WITH_SIX * (T - 1) // SIX
MIXED = LAYERS * WITH_LAYER
GH, NE = 4, 4
EF = 512
ME = EF // P
HE = GH * NE
TAB = HE + 2 * GH
MSG = HE + GH


class Shared:
    pass


def build(nc, A, out):
    ctx = ExitStack()

    def sb(name, shape, dt, where=ctx):
        return where.enter_context(nc.sbuf_tensor(name, shape, dt))

    def pb(name, shape, where, dt=f32):
        return where.enter_context(nc.psum_tensor(name, shape, dt))

    def sem(name):
        return ctx.enter_context(nc.semaphore(name))

    def sem2(name):
        return [sem(name + "0"), sem(name + "1")]

    def dram(name, shape, dt):
        return nc.dram_tensor(name, shape, dt, kind="Internal").ap()

    def tiles(eng, step):
        with eng.Fori(0, (T - 1) // 2) as j:
            for b in range(2):
                step(j * 2 + b, b, P, j)
        step(T - 1, 0, LAST, EVEN - 1)

    def tiles4(eng, step):
        with eng.Fori(0, (T - 1) // 4) as j:
            for b in range(4):
                step(j * 4 + b, b, P, j)
        step(T - 1, 0, LAST, (T - 1) // 4)

    def one(t, w=1):
        return bass.ds(t * w, w)

    with ctx:
        hn_d = dram("hn_d", (T * P, D), f32)
        k_d = dram("k_d", (T * P, D), f32)
        v_d = dram("v_d", (T * P, D), f32)
        q_d = dram("q_d", (T * P, D), f32)
        gnn_tile_d = dram("gnn_tile_d", (GNN_G, GNN_Q), i16)
        gat_tile_d = dram("gat_tile_d", (GAT_G, GAT_Q), i16)
        tab_d = dram("tab_d", (T * P, TAB), f32)

        X = sb("X", [P, T, D], f32)
        ident = sb("ident", [P, P], f32)
        ones = sb("ones", [P, P], f32)
        zeros = sb("zeros", [1, D], f32)
        G = []
        node_no = sb("node_no", [P, P], f32)
        MV = sb("MV", [P, T, 2], f32)
        RS = sb("RS", [P, T], f32)
        NM = sb("NM", [P, T], f32)
        sd = sb("sd", [P, 2, T], f32)
        bst = sb("bst", [P, 6], f32)
        bag = sb("bag", [P, 2], f32)
        bst4 = sb("bst4", [P, 4, 6], f32)
        bag4 = sb("bag4", [P, 4, 2], f32)
        gat_src = sb("gat_src", [P, GAT_G * GAT_Q], i32)
        gat_node = sb("gat_node", [P, GAT_G * GAT_Q], f16)

        idle = sem("idle")
        var_ready, sd_ready = sem("var_ready"), sem("sd_ready")

        def hold(eng, s, value):
            eng.wait_ge(s, value)
            eng.sem_inc(idle, 1)

        def chunk_tiles(eng, tile_row, q):
            return nc.values_load_multi_w_load_instructions(
                tile_row[0:1, bass.ds(q * UB, UB)], engines=[eng.engine], min_val=0, max_val=T - 1,
                skip_runtime_bounds_check_because="the sort keeps them from 0 (a count) to T - 1 (a minimum)")[1]

        def row_stats(v, t):
            nc.vector.bn_stats(bst[:, :], X[:, t, :])
            v.drain()
            nc.vector.bn_aggr(bag[:, :], bst[:, :])
            v.drain()
            nc.vector.tensor_copy(MV[:, t, :], bag[:, :])

        def all_stats(v, before=None):
            def step(t, b, j, w):
                if before:
                    before(t, b, j, w)
                for i in range(w):
                    nc.vector.bn_stats(bst4[:, i, :], X[:, t + i, :])
                v.drain()
                for i in range(w):
                    nc.vector.bn_aggr(bag4[:, i, :], bst4[:, i, :])
                v.drain()
                nc.vector.tensor_copy(MV[:, bass.ds(t, w), :], bag4[:, 0:w, :])
            with v.Fori(0, T // 8) as j:
                for b in range(2):
                    step(j * 8 + b * 4, b, j, 4)
            assert T % 8 == 1
            v.drain()
            step(T - 1, 0, T // 8, 1)

        def rstd_block(k):
            with nc.Block() as block:
                @block.vector
                def _(v):
                    nc.vector.tensor_scalar(sd[:, 0, :], MV[:, :, 1], EPS, None, ALU.add).then_inc(var_ready, 1)
                    hold(v, sd_ready, k + 1)
                    nc.vector.reciprocal(RS[:, :], sd[:, 1, :])
                    v.drain()
                    nc.vector.tensor_tensor(NM[:, :], RS[:, :], RS[:, :], ALU.mult)
                    v.drain()
                    nc.vector.tensor_tensor(NM[:, :], NM[:, :], sd[:, 0, :], ALU.mult)
                    v.drain()
                    nc.vector.tensor_scalar(NM[:, :], NM[:, :], -0.5, 1.5, ALU.mult, ALU.add)
                    v.drain()
                    nc.vector.tensor_tensor(RS[:, :], RS[:, :], NM[:, :], ALU.mult)
                    v.drain()
                    nc.vector.scalar_tensor_tensor(NM[:, :], MV[:, :, 0], -1.0, RS[:, :], ALU.mult, ALU.mult)

                @block.scalar
                def _(act):
                    act.wait_ge(var_ready, k + 1)
                    nc.scalar.activation(sd[:, 1, :], sd[:, 0, :], ACT.Sqrt).then_inc(sd_ready, 1)

        def normalise(t, dst):
            return nc.vector.tensor_scalar(dst, X[:, t, :], RS[:, one(t)], NM[:, one(t)], ALU.mult, ALU.add)

        def transpose_tile(dst, src):
            for c in range(HALF):
                last = nc.tensor.transpose(dst[:, c * P:(c + 1) * P], src[:, c * P:(c + 1) * P], ident[:, :])
            return last

        graph = ctx.enter_context(ExitStack())
        Y = sb("Y", [P, T, D], f32, graph)
        gnn_src = sb("gnn_src", [P, GNN_G * GNN_Q], i32, graph)
        gnn_node = sb("gnn_node", [P, GNN_G * GNN_Q], f16, graph)

        e = Shared()
        e.G, e.X, e.Y, e.ctx = G, X, Y, ctx
        e.gat_node, e.gat_src, e.gat_tile_d, e.gnn_node = gat_node, gat_src, gat_tile_d, gnn_node
        e.gnn_src, e.gnn_tile_d, e.graph, e.hn_d = gnn_src, gnn_tile_d, graph, hn_d
        e.hold, e.ident, e.k_d, e.node_no = hold, ident, k_d, node_no
        e.normalise, e.ones, e.pb, e.q_d = normalise, ones, pb, q_d
        e.row_stats, e.rstd_block, e.sb, e.sem = row_stats, rstd_block, sb, sem
        e.sem2, e.tab_d, e.tiles, e.transpose_tile = sem2, tab_d, tiles, transpose_tile
        e.v_d, e.zeros, e.tiles4, e.chunk_tiles, e.all_stats = v_d, zeros, tiles4, chunk_tiles, all_stats
        first_phase(nc, A, e)
        sort_phase(nc, A, e)
        mix_phase(nc, A, e)
        sum_phase(nc, A, e)
        graph.close()
        expert_phase(nc, A, out, e)


def first_phase(nc, A, e):
    sb, pb, sem, X, Y, ident, ones = e.sb, e.pb, e.sem, e.X, e.Y, e.ident, e.ones
    x_in, zeroed = sem("x_in"), sem("zeroed")
    wt_ready, wt_copied = sem("wt_ready"), sem("wt_copied")
    xn_ready, tp_ready, ht_ready = sem("xn0_ready"), sem("tp0_ready"), sem("ht0_ready")
    mm_ready, hn_ready, hn_out, hn_stored = sem("mm0_ready"), sem("hn_ready"), e.sem2("hn_out"), sem("hn_stored")
    with ExitStack() as own:
        W01 = sb("W01", [P, 2, HALF, D], f32, own)
        WT = sb("WT", [P, HALF, 2 * D], f32, own)
        b01 = sb("b01", [P, 2, D], f32, own)
        XS = sb("XS0", [P, 2, D], f32, own)
        HT = sb("HT0", [P, 2, D], f32, own)
        HN = sb("HN", [P, 2, D], f32, own)
        psT = pb("psT0", [P, 2, BANK], own)
        psY = pb("psY0", [P, 2, BANK], own)
        psN = pb("psN0", [P, 2, BANK], own)
        with nc.Block() as block:
            @block.sync
            def _(sp):
                sp.dma_start(X[:, 0:T - 1, :], A["x"][0:(T - 1) * P, :].rearrange("(t p) d -> p t d", p=P)).then_inc(x_in, 16)
                sp.wait_ge(zeroed, 1)
                sp.dma_start(X[0:LAST, T - 1, :], A["x"][(T - 1) * P:N, :]).then_inc(x_in, 16)
                sp.dma_start(W01[:, 0, :, :], A["L0_gnn_W0"].rearrange("(c p) d -> p c d", p=P)).then_inc(x_in, 16)
                sp.dma_start(W01[:, 1, :, :], A["L0_gnn_W1"].rearrange("(c p) d -> p c d", p=P)).then_inc(x_in, 16)
                sp.dma_start(b01[:, 0, :], A["L0_gnn_b0"].rearrange("(a n) -> a n", a=1).to_broadcast([P, D])).then_inc(x_in, 16)
                sp.dma_start(b01[:, 1, :], A["L0_gnn_b1"].rearrange("(a n) -> a n", a=1).to_broadcast([P, D])).then_inc(x_in, 16)
                sp.wait_ge(x_in, 96)

            @block.gpsimd
            def _(pool):
                nc.gpsimd.memset(ident[:, :], 0.0)
                nc.gpsimd.iota(e.node_no[:, :], pattern=[[1, P]], base=1, channel_multiplier=0,
                               allow_small_or_imprecise_dtypes=True)
                pool.drain()
                nc.gpsimd.affine_select(out=ident[:, :], in_=ident[:, :], compare_op=ALU.not_equal, fill=1.0,
                                        base=0, pattern=[[-1, P]], channel_multiplier=1)

            @block.vector
            def _(v):
                nc.vector.memset(X[:, T - 1, :], 0.0).then_inc(zeroed, 1)
                nc.vector.memset(ones[:, :], 1.0)
                nc.vector.memset(e.zeros[:, :], 0.0)
                e.hold(v, x_in, 96)
                e.all_stats(v)
        e.rstd_block(0)

        with nc.Block() as block:
            @block.tensor
            def _(pe):
                for k in range(4):
                    w, c = divmod(k, HALF)
                    if k >= 2:
                        pe.wait_ge(wt_copied, k - 1)
                    for o in range(HALF):
                        last = nc.tensor.transpose(psY[:, k % 2, o * P:(o + 1) * P],
                                                   W01[:, w, o, c * P:(c + 1) * P], ident[:, :])
                    last.then_inc(wt_ready, 1)
                pe.wait_ge(wt_copied, 4)

                def turn(t, b):
                    pe.wait_ge(xn_ready, t + 1)
                    e.transpose_tile(psT[:, b, 0:D], XS[:, b, :]).then_inc(tp_ready, 1)

                def products(t, b, n, j):
                    pe.wait_ge(ht_ready, t + 1)
                    for w, ps in enumerate((psY, psN)):
                        cols = slice(w * D, (w + 1) * D)
                        for c in range(HALF):
                            last = nc.tensor.matmul(ps[:, b, 0:D], HT[:, b, c * P:(c + 1) * P], WT[:, c, cols],
                                                    start=(c == 0), stop=(c == HALF - 1))
                        if w == 1:
                            last.then_inc(mm_ready, 1)
                        elif n == P:
                            turn(t + 1, 1 - b)
                turn(0, 0)
                e.tiles(pe, products)

            @block.vector
            def _(v):
                for k in range(4):
                    w, c = divmod(k, HALF)
                    v.wait_ge(wt_ready, k + 1)
                    nc.vector.tensor_copy(WT[:, c, w * D:(w + 1) * D], psY[:, k % 2, 0:D]).then_inc(wt_copied, 1)

                def xn(t, b):
                    e.normalise(t, XS[:, b, :]).then_inc(xn_ready, 1)
                    e.normalise(t, X[:, t, :])

                def own_part(t, b, n, j):
                    if n == P:
                        xn(t + 1, 1 - b)
                    v.wait_ge(mm_ready, t + 1)
                    nc.vector.tensor_tensor(Y[:, t, :], psY[:, b, 0:D], b01[:, 0, :], ALU.add)
                    e.hold(v, hn_stored, t + 1)
                    nc.vector.tensor_tensor(HN[:, b, :], psN[:, b, 0:D], b01[:, 1, :], ALU.add).then_inc(hn_ready, 1)
                xn(0, 0)
                e.tiles(v, own_part)

            @block.scalar
            def _(act):
                def ht(t, b):
                    act.wait_ge(tp_ready, t + 1)
                    nc.scalar.activation(HT[:, b, :], psT[:, b, 0:D], ACT.Copy).then_inc(ht_ready, 1)

                e.tiles(act, lambda t, b, n, j: ht(t, b))

            @block.sync
            def _(sp):
                def store(t, b, n, j):
                    sp.wait_ge(hn_ready, t + 1)
                    sp.dma_start(e.hn_d[bass.ds(t * P, P), :], HN[:, b, :]).then_inc(hn_out[b], 16)
                    sp.wait_ge(hn_out[b], j * 16 + 16)
                    sp.sem_inc(hn_stored, 1)
                sp.sem_inc(hn_stored, 2)
                e.tiles(sp, store)


def sort_phase(nc, A, e):
    with ExitStack() as own:
        w = Shared()
        w.lane = e.sb("lane", [P, P], f16, own)
        w.chunk_no = e.sb("chunk_no", [P, MAXQ], f16, own)
        w.tile_no = e.sb("tile_no", [P, T], f32, own)
        w.chunk_at = e.sb("chunk_at", [P, -(-MAXQ // P)], f32, own)
        w.before = e.sb("before", [P, P], f32, own)
        w.blank = e.sb("blank", [P, MAXQ], f16, own)
        w.end, w.start, w.t_a, w.t_b = (e.sb(x, [P, MAXQ], i32, own) for x in ("end", "start", "t_a", "t_b"))
        w.lane_of, w.chunk_of, w.pay_hi, w.pay_lo = (e.sb(x, [P, MAXC], f32, own) for x in ("lane_of", "chunk_of", "pay_hi", "pay_lo"))
        w.minus_lane, w.minus_hi, w.minus_lo = (e.sb(x, [P, MAXC], f32, own) for x in ("minus_lane", "minus_hi", "minus_lo"))
        w.tile_of = e.sb("tile_of", [P, MAXC], f16, own)
        w.tot, w.chunks, w.upto, w.base = (e.sb(x, [P, T], f32, own) for x in ("tot", "chunks", "upto", "base"))
        w.nothing = e.sb("nothing", [1, MAXC], f32, own)
        w.tot_i = e.sb("tot_i", [P, T], i32, own)
        w.hits = e.sb("hits", [P, T], f32, own)
        w.tile_f = e.sb("tile_f", [P, -(-MAXQ // P)], f32, own)
        w.tile_i = e.sb("tile_i", [P, -(-MAXQ // P)], i16, own)
        w.psP = e.pb("psP", [P, 2, BANK], own)
        w.psL = e.pb("psL", [P, 2, BANK], own)
        w.psR = e.pb("psR1", [P, BANK], own)
        with nc.Block() as block:
            @block.gpsimd
            def _(pool):
                small = dict(allow_small_or_imprecise_dtypes=True)
                nc.gpsimd.iota(w.lane[:, :], pattern=[[1, P]], base=0, channel_multiplier=0, **small)
                nc.gpsimd.iota(w.chunk_no[:, :], pattern=[[1, MAXQ]], base=0, channel_multiplier=0, **small)
                nc.gpsimd.iota(w.tile_no[:, :], pattern=[[1, T]], base=0, channel_multiplier=0, **small)
                nc.gpsimd.iota(w.chunk_at[:, :], pattern=[[P, -(-MAXQ // P)]], base=0, channel_multiplier=1, **small)
                nc.gpsimd.memset(w.blank[:, :], 0.0)
                nc.gpsimd.memset(w.nothing[:, :], 0.0)
                nc.gpsimd.memset(w.before[:, :], 1.0)
                pool.drain()
                nc.gpsimd.affine_select(out=w.before[:, :], in_=w.before[:, :], compare_op=ALU.is_ge, fill=0.0,
                                        base=-1, pattern=[[1, P]], channel_multiplier=-1)
        sort_groups(nc, e, w, "gnn", GNN_G, GNN_C, GNN_Q, A["gnn_end"], A["gnn_start"], e.gnn_src, e.gnn_node, e.gnn_tile_d)
        sort_groups(nc, e, w, "gat", GAT_G, GAT_C, GAT_Q, A["gat_end"], A["gat_start"], e.gat_src, e.gat_node, e.gat_tile_d)


def sort_groups(nc, e, w, kind, G, C, Q, end_d, start_d, src_list, node_list, tile_d):
    edges_in, tot_ready, prefix_ready = e.sem(kind + "_edges_in"), e.sem(kind + "_tot_ready"), e.sem(kind + "_prefix_ready")
    tile_ready, tile_out = e.sem(kind + "_tile_ready"), e.sem(kind + "_tile_out")
    onehot_ready, onehot_used, list_ready = e.sem(kind + "_onehot_ready"), e.sem(kind + "_onehot_used"), e.sem(kind + "_list_ready")
    lane_ready, counted, count_used, place_ready = (e.sem(kind + x) for x in ("_lane_ready", "_counted", "_count_used", "_place_ready"))
    V, hold = nc.vector, e.hold
    QK = -(-Q // P)

    STEPS = -(-C // UC)
    PARTS = (range(0, TOGETHER // 2 + 1), range(TOGETHER // 2 + 1, TOGETHER))
    NP = T // TOGETHER * len(PARTS)
    assert T % TOGETHER == 0 and C % UC != 1

    def columns(eng, step):
        with eng.Fori(0, C // (SETS * UC)) as j:
            for b in range(SETS):
                step(j * SETS + b, j * (SETS * UC) + b * UC, b * UC, UC)
        for b, i in enumerate(range(C // (SETS * UC) * SETS, STEPS)):
            step(i, i * UC, b * UC, min(UC, C - i * UC))

    def counts(eng, step):
        with eng.Fori(0, T // TOGETHER) as j:
            for x, ks in enumerate(PARTS):
                step(j * len(PARTS) + x, j * TOGETHER, ks)

    with nc.Fori(0, G) as g:
        counting = ExitStack()
        scan = e.sb(kind + "_scan", [P, TOGETHER, C], f32, counting)
        mask = e.sb(kind + "_mask", [P, T, C], f16, counting)
        with nc.Block() as block:
            @block.sync
            def _(sp):
                sp.dma_start(w.end[:, 0:C], end_d[g, :, :]).then_inc(edges_in, 16)
                sp.dma_start(w.start[:, 0:C], start_d[g, :, :]).then_inc(edges_in, 16)
                sp.wait_ge(tile_ready, g + 1)
                for k in range(QK):
                    n = min(P, Q - k * P)
                    sp.dma_start(tile_d[g, k * P:k * P + n].rearrange("(p a) -> p a", a=1), w.tile_i[0:n, k:k + 1]).then_inc(tile_out, 16)
                e.hold(sp, tile_out, g * (16 * QK) + 16 * QK)

            @block.tensor
            def _(pe):
                pe.wait_ge(tot_ready, g + 1)
                nc.tensor.matmul(w.psP[:, 0, 0:T], w.before[:, :], w.tot[:, :], start=True, stop=True)
                nc.tensor.matmul(w.psP[:, 0, T:2 * T], e.ones[:, :], w.tot[:, :], start=True, stop=True).then_inc(prefix_ready, 1)

                def add(i, c, ks):
                    pe.wait_ge(counted, g * NP + (i + 1))
                    for k in ks:
                        last = nc.tensor.matmul(w.psR[:, 0:C], e.ident[:, :], scan[:, k, :], start=False, stop=False)
                    last.then_inc(count_used, 1)
                nc.tensor.matmul(w.psR[:, 0:C], e.zeros[0:1, 0:P], w.nothing[0:1, 0:C], start=True, stop=False)
                counts(pe, add)
                nc.tensor.matmul(w.psR[:, 0:C], e.zeros[0:1, 0:P], w.nothing[0:1, 0:C], start=False, stop=True).then_inc(place_ready, 1)

            @block.vector
            def _(v):
                end, start, t_a, t_b = w.end[:, 0:C], w.start[:, 0:C], w.t_a[:, 0:C], w.t_b[:, 0:C]
                tile_of = w.tile_of[:, 0:C]
                v.wait_ge(edges_in, g * 32 + 32)
                V.tensor_scalar(t_a, end, 7, None, ALU.arith_shift_right)
                V.tensor_scalar(t_b, end, 127, None, ALU.bitwise_and)
                V.tensor_scalar(start, start, float(N - 1), None, ALU.min)
                v.drain()
                V.tensor_copy(tile_of, t_a)
                V.tensor_scalar(w.pay_lo[:, 0:C], t_b, 1.0, None, ALU.add)
                v.drain()
                V.tensor_scalar(t_a, start, 3, None, ALU.bitwise_and)
                V.tensor_scalar(t_b, start, 2, None, ALU.arith_shift_right)
                v.drain()
                V.scalar_tensor_tensor(w.pay_lo[:, 0:C], t_a, 256.0, w.pay_lo[:, 0:C], ALU.mult, ALU.add)
                V.tensor_copy(w.pay_hi[:, 0:C], t_b)
                with v.Fori(0, T // TOGETHER) as i:
                    for k in range(TOGETHER):
                        t = i * TOGETHER + k
                        V.tensor_scalar(mask[:, t, :], tile_of, w.tile_no[:, bass.ds(t, 1)], None, ALU.is_equal, ALU.add,
                                        accum_out=w.tot[:, bass.ds(t, 1)])
                v.drain()
                V.tensor_copy(w.tot[:, 0:1], w.tot[:, 0:1]).then_inc(tot_ready, 1)
                v.wait_ge(prefix_ready, g + 1)
                V.tensor_scalar(w.tot_i[:, :], w.psP[:, 0, T:2 * T], float(P - 1), None, ALU.add)
                v.drain()
                V.tensor_scalar(w.tot_i[:, :], w.tot_i[:, :], 7, None, ALU.arith_shift_right)
                v.drain()
                V.tensor_copy(w.chunks[:, :], w.tot_i[:, :])
                v.drain()
                V.tensor_tensor_scan(w.upto[:, :], w.chunks[:, :], w.blank[:, 0:T], 0.0, ALU.add, ALU.add)
                v.drain()
                V.tensor_tensor(w.base[:, :], w.upto[:, :], w.chunks[:, :], ALU.subtract)
                v.drain()
                V.scalar_tensor_tensor(w.base[:, :], w.base[:, :], float(P), w.psP[:, 0, 0:T], ALU.mult, ALU.add)
                for k in range(QK):
                    V.tensor_scalar(w.hits[:, :], w.upto[:, :], w.chunk_at[:, k:k + 1], None, ALU.is_le, ALU.add,
                                    accum_out=w.tile_f[:, k:k + 1])
                    v.drain()
                V.tensor_scalar(w.tile_i[:, 0:QK], w.tile_f[:, 0:QK], float(T - 1), None, ALU.min).then_inc(tile_ready, 1)
                def count(i, c, ks):
                    hold(v, count_used, g * (NP + 2) + (i + 1))
                    for k in ks:
                        t = c + k
                        V.tensor_tensor_scan(scan[:, k, :], mask[:, t, :], w.blank[:, 0:C], w.base[:, bass.ds(t, 1)], ALU.add, ALU.add)
                    v.drain()
                    for k in ks:
                        last = V.tensor_tensor(scan[:, k, :], scan[:, k, :], mask[:, c + k, :], ALU.mult)
                    last.then_inc(counted, 1)
                v.sem_inc(count_used, 2)
                counts(v, count)
                hold(v, place_ready, g + 1)
                V.tensor_scalar(t_a, w.psR[:, 0:C], -1.0, None, ALU.add)
                v.drain()
                V.tensor_scalar(t_b, t_a, 7, None, ALU.arith_shift_right)
                V.tensor_scalar(t_a, t_a, 127, None, ALU.bitwise_and)
                v.drain()
                V.tensor_copy(w.chunk_of[:, 0:C], t_b)
                V.tensor_copy(w.lane_of[:, 0:C], t_a)
                V.tensor_scalar(w.minus_lane[:, 0:C], t_a, -1.0, None, ALU.mult)
                V.tensor_scalar(w.minus_hi[:, 0:C], w.pay_hi[:, 0:C], -1.0, None, ALU.mult)
                V.tensor_scalar(w.minus_lo[:, 0:C], w.pay_lo[:, 0:C], -1.0, None, ALU.mult)
        counting.close()

        moving = ExitStack()
        L = e.sb(kind + "_L", [P, SETS * UC, 2, P], f16, moving)
        off = e.sb(kind + "_off", [P, SETS * UC, P], f16, moving)
        R = e.sb(kind + "_R", [P, SETS * UC, Q], f16, moving)
        with nc.Block() as block:
            @block.vector
            def _(v):
                def onehots(i, c, b, n):
                    hold(v, onehot_used, g * (STEPS + SETS) + (i + 1))
                    for k in range(n):
                        at = bass.ds(c + k, 1)
                        if k % 2 == 0:
                            V.tensor_scalar(L[:, b + k, 0, :], w.lane[:, :], w.lane_of[:, at], w.pay_hi[:, at], ALU.is_equal, ALU.mult)
                            V.tensor_scalar(L[:, b + k, 1, :], w.lane[:, :], w.lane_of[:, at], w.pay_lo[:, at], ALU.is_equal, ALU.mult)
                        last = V.tensor_scalar(R[:, b + k, :], w.chunk_no[:, 0:Q], w.chunk_of[:, at], None, ALU.is_equal)
                    last.then_inc(onehot_ready, 1)
                columns(v, onehots)
                v.wait_ge(list_ready, g + 1)
                t_a, t_b = w.t_a[:, 0:Q], w.t_b[:, 0:Q]
                V.tensor_copy(t_a, w.psL[:, 1, 0:Q])
                v.drain()
                V.tensor_scalar(t_b, t_a, 8, None, ALU.arith_shift_right)
                V.tensor_scalar(t_a, t_a, 255, None, ALU.bitwise_and)
                v.drain()
                V.tensor_copy(node_list[:, bass.ds(g * Q, Q)], t_a)
                V.scalar_tensor_tensor(src_list[:, bass.ds(g * Q, Q)], w.psL[:, 0, 0:Q], 4.0, t_b, ALU.mult, ALU.add)

            @block.scalar
            def _(act):
                def lanes(i, c, b, n):
                    hold(act, onehot_used, g * (STEPS + SETS) + (i + 1))
                    for k in range(1, n, 2):
                        nc.scalar.activation(off[:, b + k, :], w.lane[:, :], ACT.Abs, bias=w.minus_lane[:, bass.ds(c + k, 1)])
                    act.drain()
                    for k in range(1, n, 2):
                        at = bass.ds(c + k, 1)
                        for h, (what, minus) in enumerate(((w.pay_hi, w.minus_hi), (w.pay_lo, w.minus_lo))):
                            last = nc.scalar.activation(L[:, b + k, h, :], off[:, b + k, :], ACT.Relu, bias=what[:, at], scale=minus[:, at])
                    last.then_inc(lane_ready, 1)
                columns(act, lanes)

            @block.tensor
            def _(pe):
                pe.sem_inc(onehot_used, SETS)

                def move(i, c, b, n):
                    hold(pe, lane_ready, g * STEPS + (i + 1))
                    pe.wait_ge(onehot_ready, g * STEPS + (i + 1))
                    for k in range(n):
                        for h in range(2):
                            last = nc.tensor.matmul(w.psL[:, h, 0:Q], L[:, b + k, h, :], R[:, b + k, :], start=False, stop=False)
                    last.then_inc(onehot_used, 1)
                for h in range(2):
                    nc.tensor.matmul(w.psL[:, h, 0:Q], w.blank[:, 0:P], w.blank[:, 0:Q], start=True, stop=False)
                columns(pe, move)
                for h in range(2):
                    last = nc.tensor.matmul(w.psL[:, h, 0:Q], w.blank[:, 0:P], w.blank[:, 0:Q], start=False, stop=True)
                last.then_inc(list_ready, 1)
        moving.close()


class Gathers:

    def __init__(self, nc, e, kind, width, rows_d, src_list, node_list, tile_d, blocks, own):
        self.nc, self.e, self.width, self.rows_d, self.blocks = nc, e, width, rows_d, blocks
        self.src_list, self.node_list, self.tile_d = src_list, node_list, tile_d
        self.numbers = e.sb(kind + "_numbers", [P, 2 * UB], i32, own)
        self.onehot = e.sb(kind + "_onehot", [P, 2 * UB, P], f32, own)
        self.rows = e.sb(kind + "_rows", [P, 2 * UB, width], f32, own)
        self.tile_row = e.sb(kind + "_tile_row", [1, blocks * UB], i16, own)
        self.staged, self.summed = e.sem(kind + "_staged"), e.sem(kind + "_summed")
        self.gathered = [e.sem(f"{kind}_gathered{i}") for i in range(2 * UB)]

    def stage(self, q, b):
        for s in range(UB):
            last = self.nc.vector.tensor_scalar(self.onehot[:, UB * b + s, :], self.e.node_no[:, :],
                                                self.node_list[:, bass.ds(q * UB + s, 1)], None, ALU.is_equal)
        last.then_inc(self.staged, 1)

    def gather(self, pool, q, b):
        self.e.hold(pool, self.summed, q + 1)
        self.nc.gpsimd.tensor_copy(self.numbers[:, UB * b:UB * b + UB], self.src_list[:, bass.ds(q * UB, UB)])
        pool.drain()
        for i in range(UB * b, UB * b + UB):
            self.nc.gpsimd.indirect_dma_start(
                out=self.rows[:, i, :], out_offset=None, in_=self.rows_d,
                in_offset=bass.IndirectOffsetOnAxis(ap=self.numbers[:, i:i + 1], axis=0)).then_inc(self.gathered[i], 16)

    def add_up(self, pe, q, b, j, psG):
        pe.wait_ge(self.staged, q + 1)
        for i in range(UB * b, UB * b + UB):
            pe.wait_ge(self.gathered[i], j * 16 + 16)
            last = self.nc.tensor.matmul(psG[:, i, :], self.onehot[:, i, :], self.rows[:, i, :], start=True, stop=True)
        last.then_inc(self.summed, 1)

    def accumulate(self, v, q, b, psG, Y):
        tiles = self.e.chunk_tiles(v, self.tile_row, q)
        self.e.hold(v, self.summed, q + 3)
        for s, t in enumerate(tiles):
            self.nc.vector.tensor_tensor(Y[:, t, :], Y[:, t, :], psG[:, UB * b + s, :], ALU.add)
            v.drain()


def mix_phase(nc, A, e):
    X, Y, ident, ones, tiles, hold = e.X, e.Y, e.ident, e.ones, e.tiles, e.hold
    V, S = nc.vector, nc.scalar
    own = e.graph
    G = Gathers(nc, e, "gnn", D, e.hn_d, e.gnn_src, e.gnn_node, e.gnn_tile_d, GNN_BLOCKS, own)
    psG = e.pb("psG", [P, 2 * UB, D], own)
    head_block = e.sb("head_block", [P, P], f32, own)
    w_in = e.sem("mix_w_in")
    xn_ready, tp_ready, ht_ready = e.sem("xn_ready"), e.sem("tp_ready"), e.sem("ht_ready")
    qkv_ready, kv_ready, qsub_ready, qexp_ready = e.sem("qkv_ready"), e.sem("kv_ready"), e.sem("qsub_ready"), e.sem("qexp_ready")
    qn_ready, qt_ready, qts_ready = e.sem("qn_ready"), e.sem("qt_ready"), e.sem("qts_ready")
    kv_stored, q_stored = e.sem("kv_stored"), e.sem("q_stored")
    kv_out, q_out, kv_in, q_in = e.sem2("kv_out"), e.sem2("q_out"), [e.sem(f"kv_in{i}") for i in range(4)], [e.sem(f"q_in{i}") for i in range(4)]
    kmt_ready, diag_ready, kmb_ready = e.sem("kmt_ready"), e.sem("diag_ready"), e.sem("kmb_ready")
    ks_ready, ke_ready, ctx_done = e.sem("ks_ready"), e.sem("ke_ready"), e.sem("ctx_done")
    cn_ready, cnt_ready, cnt_copied, mx_ready = e.sem("cn_ready"), e.sem("cnt_ready"), e.sem("cnt_copied"), e.sem("mx_ready")
    att_ready, att_added, q_used = e.sem("att_ready"), e.sem("att_added"), e.sem("q_used")
    xn2_ready, tp2_ready, ht2_ready = e.sem("xn2_ready"), e.sem("tp2_ready"), e.sem("ht2_ready")
    up_ready, gelu_ready, down_ready, down_added = e.sem("up_ready"), e.sem("gelu_ready"), e.sem("down_ready"), e.sem("down_added")

    with nc.Block() as block:
        @block.sync
        def _(sp):
            sp.dma_start(G.tile_row[:, :], e.gnn_tile_d.rearrange("(a g) q -> a (g q)", a=1)).then_inc(w_in, 16)
            sp.wait_ge(w_in, 16)

        @block.vector
        def _(v):
            V.memset(head_block[:, :], 0.0)
            v.drain()
            for h in range(P // DH):
                V.memset(head_block[h * DH:(h + 1) * DH, h * DH:(h + 1) * DH], 1.0)
            v.sem_inc(G.summed, 2)
            G.stage(0, 0)
            e.all_stats(v)

    layer = own.enter_context(ExitStack())
    Wqkv = e.sb("Wqkv", [P, HALF, 3 * D], f32, layer)
    Wo = e.sb("Wo", [P, HALF, D], f32, layer)
    W1 = e.sb("W1", [P, HALF, FF], f32, layer)
    W2 = e.sb("W2", [P, MF, D], f32, layer)
    out_bias = e.sb("out_bias", [P, 2, D], f32, layer)
    b1 = e.sb("b1", [P, MF], f32, layer)
    ln = e.sb("ln", [P, 4, HALF], f32, layer)
    KM = e.sb("KM", [P, D], f32, layer)
    MX = e.sb("MX", [P, HALF, D], f32, layer)

    def tiles_from_first(eng, step):
        step(0, 0, P, FIRST)
        step(1, 1, P, 0)
        with eng.Fori(1, (T - 1) // 2) as j:
            for b in range(2):
                step(j * 2 + b, b, P, j)
        step(T - 1, 0, LAST, EVEN - 1)

    def tiles_to_last(eng, step, first):
        with eng.Fori(first, (T - 1) // 2 - 1) as j:
            for b in range(2):
                step(j * 2 + b, b, P, j)
        step(T - 3, 0, P, (T - 1) // 2 - 1)
        step(T - 2, 1, P, (T - 1) // 2 - 1)
        step(T - 1, 0, LAST, EVEN - 1)

    def tiles_by_six(eng, step, to_last=False):
        with eng.Fori(0, (T - 1) // SIX - to_last) as j:
            for b in range(SIX):
                step(j * SIX + b, b, P, j)
        if to_last:
            for b in range(SIX):
                step(T - 1 - SIX + b, b, P, (T - 1) // SIX - 1)
        step(T - 1, 0, LAST, (T - 1) // SIX)

    def ahead(t, w):
        return not isinstance(t, int) or t + w < T

    def block_q(l, p, t):
        return l * WITH_LAYER + (t + p * (T - 1))

    def block_j(l, p, j):
        return l * (WITH_LAYER // 2) + (j + p * (T - 1) // 2)

    def beside(l, b, j):
        return [(l * WITH_LAYER + (j * WITH_SIX + (3 * (T - 1) + i)), i % 2,
                 l * (WITH_LAYER // 2) + (j * (WITH_SIX // 2) + (3 * (T - 1) + i) // 2)) for i in BESIDE[b]]

    def uses4(b):
        return (T - 1) // 4 + (b == 0)

    def gathers(pool, l, p):
        def step(t, b, n, j):
            if n == P:
                G.gather(pool, block_q(l, p, t), b)
        tiles(pool, step)

    with nc.Fori(0, LAYERS) as l:
        with nc.Block() as block:
            @block.sync
            def _(sp):
                loads = [(Wqkv[:, :, i * D:(i + 1) * D], A["L0_mix_W" + x][l, :, :].rearrange("(c p) n -> p c n", p=P)) for i, x in enumerate("qkv")]
                loads += [(Wo[:, :, :], A["L0_mix_Wo"][l, :, :].rearrange("(c p) n -> p c n", p=P)),
                          (W1[:, :, :], A["L0_mix_W1"][l, :, :].rearrange("(c p) n -> p c n", p=P)),
                          (W2[:, :, :], A["L0_mix_W2"][l, :, :].rearrange("(c p) n -> p c n", p=P)),
                          (out_bias[:, 0, :], A["L0_mix_bo"][bass.ds(l, 1), :].to_broadcast([P, D])),
                          (out_bias[:, 1, :], A["L0_mix_b2"][bass.ds(l, 1), :].to_broadcast([P, D])),
                          (b1[:, :], A["L0_mix_b1"][l, :].rearrange("(m p) -> p m", p=P))]
                for i, x in enumerate(("ln1_g", "ln1_b", "ln2_g", "ln2_b")):
                    loads.append((ln[:, i, :], A["L0_mix_" + x][l, :].rearrange("(c p) -> p c", p=P)))
                for dst, src in loads:
                    sp.dma_start(dst, src, allow_slow_non_contiguous=True).then_inc(w_in, 16)
                n = 16 * len(loads)
                hold(sp, w_in, l * n + (n + 16))

            @block.vector
            def _(v):
                V.memset(KM[:, :], LOWEST)

        e.rstd_block(l * 2 + 1)

        with ExitStack() as own:
            XS, HT = e.sb("XS", [P, 2, D], f32, own), e.sb("HT", [P, 2, D], f32, own)
            KV, QS = e.sb("KV", [P, 2, 2 * D], f32, own), e.sb("QS", [P, 2, D], f32, own)
            QE, QT = e.sb("QE", [P, 2, D], f32, own), e.sb("QT", [P, 2, D], f32, own)
            QM = e.sb("QM", [P, 2, 2, HEADS], f32, own)
            psT, psQ = e.pb("psT", [P, BANK], own), e.pb("psQ", [P, BANK], own)
            psKV, psQT = e.pb("psKV", [P, BANK], own), e.pb("psQT", [P, BANK], own)

            def heads(ap):
                return ap.rearrange("p (h d) -> p h d", h=HEADS)

            with nc.Block() as block:
                @block.gpsimd
                def _(pool):
                    gathers(pool, l, 0)

                @block.vector
                def _(v):
                    def xn(t, b):
                        e.normalise(t, XS[:, b, :]).then_inc(xn_ready, 1)

                    def step(t, b, n, j):
                        if j is not FIRST:
                            shares(t - 1, 1 - b)
                        mx = QM[:, b, 0, :]
                        v.wait_ge(qkv_ready, l * T + (t + 1))
                        V.tensor_reduce(mx, heads(psQ[:, 0:D]), AX.X, ALU.max)
                        v.drain()
                        V.tensor_tensor(heads(QS[:, b, :]), heads(psQ[:, 0:D]), mx.unsqueeze(2).to_broadcast([P, HEADS, DH]),
                                        ALU.subtract).then_inc(qsub_ready, 1)
                        hold(v, kv_ready, l * (T + 1) + (t + 2))
                        V.tensor_tensor(KM[0:n, :], KM[0:n, :], KV[0:n, b, 0:D], ALU.max)
                        if ahead(t, 2):
                            xn(t + 2, b)
                        if n == P:
                            G.stage(block_q(l, 0, t) + 1, 1 - b)
                            G.accumulate(v, block_q(l, 0, t), b, psG, Y)

                    def shares(t, b):
                        sm = QM[:, b, 1, :]
                        v.wait_ge(qexp_ready, l * T + (t + 1))
                        V.tensor_reduce(sm, heads(QE[:, b, :]), AX.X, ALU.add)
                        v.drain()
                        V.reciprocal(sm, sm)
                        v.drain()
                        V.tensor_tensor(heads(QE[:, b, :]), heads(QE[:, b, :]), sm.unsqueeze(2).to_broadcast([P, HEADS, DH]),
                                        ALU.mult).then_inc(qn_ready, 1)
                    xn(0, 0)
                    xn(1, 1)
                    step(0, 0, P, FIRST)
                    step(1, 1, P, 0)
                    tiles_to_last(v, step, 1)
                    shares(T - 1, 0)

                @block.tensor
                def _(pe):
                    def turn(t, b):
                        pe.wait_ge(xn_ready, l * T + (t + 1))
                        e.transpose_tile(psT[:, 0:D], XS[:, b, :]).then_inc(tp_ready, 1)

                    def step(t, b, n, j):
                        pe.wait_ge(ht_ready, l * T + (t + 1))
                        if n == P:
                            turn(t + 1, 1 - b)
                        if j is not FIRST:
                            pe.wait_ge(qsub_ready, l * T + t)
                        pe.wait_ge(kv_ready, l * (T + 1) + (t + 1))
                        for ps, lo, hi in ((psQ, 0, D), (psKV, D, 3 * D)):
                            for c in range(HALF):
                                last = nc.tensor.matmul(ps[:, 0:hi - lo], HT[:, b, c * P:(c + 1) * P], Wqkv[:, c, lo:hi],
                                                        start=(c == 0), stop=(c == HALF - 1))
                        last.then_inc(qkv_ready, 1)
                        if n == P:
                            G.add_up(pe, block_q(l, 0, t), b, block_j(l, 0, 0 if j is FIRST else j), psG)
                        if j is not FIRST:
                            turn_q(t - 1, 1 - b)

                    def turn_q(t, b):
                        pe.wait_ge(qn_ready, l * T + (t + 1))
                        e.transpose_tile(psQT[:, 0:D], QE[:, b, :]).then_inc(qt_ready, 1)
                    turn(0, 0)
                    tiles_from_first(pe, step)
                    turn_q(T - 1, 0)

                @block.scalar
                def _(act):
                    def ht(t, b):
                        act.wait_ge(tp_ready, l * T + (t + 1))
                        for c in range(HALF):
                            last = S.activation(HT[:, b, c * P:(c + 1) * P], psT[:, c * P:(c + 1) * P], ACT.Identity,
                                                bias=ln[:, 1, c:c + 1], scale=ln[:, 0, c:c + 1])
                        last.then_inc(ht_ready, 1)

                    def step(t, b, n, j):
                        if n == P:
                            ht(t + 1, 1 - b)
                        hold(act, kv_stored, l * (T + 2) + (t + 1))
                        act.wait_ge(qkv_ready, l * T + (t + 1))
                        S.activation(KV[:, b, :], psKV[:, :], ACT.Copy).then_inc(kv_ready, 1)
                        if j is not FIRST:
                            copy_q(t - 1, 1 - b)
                        act.wait_ge(qsub_ready, l * T + (t + 1))
                        S.activation(QE[:, b, :], QS[:, b, :], ACT.Exp, scale=QK_SCALE).then_inc(qexp_ready, 1)

                    def copy_q(t, b):
                        hold(act, q_stored, l * (T + 2) + (t + 1))
                        act.wait_ge(qt_ready, l * T + (t + 1))
                        S.activation(QT[:, b, :], psQT[:, 0:D], ACT.Copy).then_inc(qts_ready, 1)
                    act.sem_inc(kv_ready, 1)
                    ht(0, 0)
                    tiles_from_first(act, step)
                    copy_q(T - 1, 0)

                @block.sync
                def _(sp):
                    for stored in (kv_stored, q_stored):
                        sp.sem_inc(stored, 2)

                    def step(t, b, n, j):
                        uses = l * (ODD if b else EVEN) + (0 if j is FIRST else j)
                        sp.wait_ge(kv_ready, l * (T + 1) + (t + 2))
                        sp.dma_start(e.k_d[bass.ds(t * P, P), :], KV[:, b, 0:D]).then_inc(kv_out[b], 16)
                        sp.dma_start(e.v_d[bass.ds(t * P, P), :], KV[:, b, D:2 * D]).then_inc(kv_out[b], 16)
                        if j is not FIRST:
                            store_q(t - 1, 1 - b, l * (EVEN if b else ODD) + (j if b else j - 1))
                        sp.wait_ge(kv_out[b], uses * 32 + 32)
                        sp.sem_inc(kv_stored, 1)

                    def store_q(t, b, uses):
                        sp.wait_ge(qts_ready, l * T + (t + 1))
                        sp.dma_start(e.q_d[bass.ds(t * P, P), :], QT[:, b, :]).then_inc(q_out[b], 16)
                        sp.wait_ge(q_out[b], uses * 16 + 16)
                        sp.sem_inc(q_stored, 1)
                    tiles_from_first(sp, step)
                    store_q(T - 1, 0, l * EVEN + (EVEN - 1))

        with ExitStack() as own:
            KIN, KE = e.sb("KIN", [P, 4, D], f32, own), e.sb("KE", [P, 4, D], f32, own)
            VIN = e.sb("VIN", [P, 4, HALF, P + 1], f32, own)
            diag, km2 = e.sb("diag", [P, HALF, P], f32, own), e.sb("km2", [P, HALF], f32, own)
            CN, CNT = e.sb("CN", [P, HALF, P], f32, own), e.sb("CNT", [P, HALF, P], f32, own)
            psC = e.pb("psC", [P, HALF, BANK], own)
            psA, psB = e.pb("psA", [P, BANK], own), e.pb("psB", [P, BANK], own)
            with nc.Block() as block:
                @block.tensor
                def _(pe):
                    e.transpose_tile(psA[:, 0:D], KM[:, :]).then_inc(kmt_ready, 1)
                    pe.wait_ge(diag_ready, l + 1)
                    for c in range(HALF):
                        last = nc.tensor.matmul(psB[:, c * P:(c + 1) * P], ones[:, :], diag[:, c, :], start=True, stop=True)
                    last.then_inc(kmb_ready, 1)

                @block.vector
                def _(v):
                    V.memset(VIN[:, :, :, P:P + 1], 1.0)
                    v.wait_ge(kmt_ready, l + 1)
                    V.tensor_reduce(km2[:, :], psA[:, 0:D].rearrange("p (c n) -> p c n", c=HALF), AX.X, ALU.max)
                    v.drain()
                    for c in range(HALF):
                        last = V.tensor_scalar(diag[:, c, :], ident[:, :], km2[:, c:c + 1], None, ALU.mult)
                    last.then_inc(diag_ready, 1)
                    v.wait_ge(kmb_ready, l + 1)
                    V.tensor_copy(KM[:, :], psB[:, 0:D])

            with nc.Block() as block:
                @block.gpsimd
                def _(pool):
                    gathers(pool, l, 1)

                @block.sync
                def _(sp):
                    def step(t, b, n, j):
                        hold(sp, ctx_done, l * (T + 4) + (t + 1))
                        sp.dma_start(KIN[:, b, :], e.k_d[bass.ds(t * P, P), :]).then_inc(kv_in[b], 16)
                        sp.dma_start(VIN[:, b, :, 0:P], e.v_d[bass.ds(t * P, P), :].rearrange("p (c n) -> p c n", c=HALF)).then_inc(kv_in[b], 16)
                    e.tiles4(sp, step)

                @block.vector
                def _(v):
                    def less_most(t, b, j):
                        v.wait_ge(kv_in[b], (l * uses4(b) + j) * 32 + 32)
                        V.tensor_tensor(KIN[:, b, :], KIN[:, b, :], KM[:, :], ALU.subtract).then_inc(ks_ready, 1)

                    def step(t, b, n, j):
                        if n == P:
                            less_most(t + 1, (b + 1) % 4, j + (b + 1) // 4)
                            G.stage(block_q(l, 1, t) + 1, 1 - b % 2)
                            G.accumulate(v, block_q(l, 1, t), b % 2, psG, Y)
                    less_most(0, 0, 0)
                    e.tiles4(v, step)

                @block.scalar
                def _(act):
                    def step(t, b, n, j):
                        act.wait_ge(ks_ready, l * T + (t + 1))
                        S.activation(KE[:, b, :], KIN[:, b, :], ACT.Exp, scale=QK_SCALE).then_inc(ke_ready, 1)
                    e.tiles4(act, step)

                @block.tensor
                def _(pe):
                    pe.sem_inc(ctx_done, 4)

                    def step(t, b, n, j):
                        if n == P:
                            G.add_up(pe, block_q(l, 1, t), b % 2, block_j(l, 1, j * 2 + b // 2), psG)
                        pe.wait_ge(ke_ready, l * T + (t + 1))
                        for c in range(HALF):
                            last = nc.tensor.matmul(psC[:, c, 0:P + 1], KE[0:n, b, c * P:(c + 1) * P], VIN[0:n, b, c, :],
                                                    start=False, stop=(n != P))
                        last.then_inc(ctx_done, 1)
                    for c in range(HALF):
                        nc.tensor.matmul(psC[:, c, 0:P + 1], e.zeros[0:1, 0:P], e.zeros[0:1, 0:P + 1], start=True, stop=False)
                    e.tiles4(pe, step)

            with nc.Block() as block:
                @block.vector
                def _(v):
                    for c in range(HALF):
                        V.reciprocal(km2[:, c:c + 1], psC[:, c, P:P + 1])
                    v.drain()
                    for c in range(HALF):
                        last = V.scalar_tensor_tensor(CN[:, c, :], psC[:, c, 0:P], km2[:, c:c + 1], head_block[:, :], ALU.mult, ALU.mult)
                    last.then_inc(cn_ready, 1)
                    v.wait_ge(cnt_ready, l + 1)
                    V.tensor_copy(CNT[:, :, :], psA[:, 0:D].rearrange("p (c n) -> p c n", c=HALF)).then_inc(cnt_copied, 1)
                    v.wait_ge(mx_ready, l + 1)
                    V.tensor_copy(MX[:, :, :], psB[:, :].rearrange("p (c n) -> p c n", c=HALF))

                @block.tensor
                def _(pe):
                    pe.wait_ge(cn_ready, l + 1)
                    for c in range(HALF):
                        last = nc.tensor.transpose(psA[:, c * P:(c + 1) * P], CN[:, c, :], ident[:, :])
                    last.then_inc(cnt_ready, 1)
                    pe.wait_ge(cnt_copied, l + 1)
                    for c in range(HALF):
                        last = nc.tensor.matmul(psB[:, c * D:(c + 1) * D], CNT[:, c, :], Wo[:, c, :], start=True, stop=True)
                    last.then_inc(mx_ready, 1)

        with ExitStack() as own:
            QIN = e.sb("QIN", [P, 4, D], f32, own)
            psF = e.pb("psF", [P, 2, BANK], own)
            with nc.Block() as block:
                @block.gpsimd
                def _(pool):
                    gathers(pool, l, 2)

                @block.sync
                def _(sp):
                    def step(t, b, n, j):
                        hold(sp, q_used, l * (T + 4) + (t + 1))
                        sp.dma_start(QIN[:, b, :], e.q_d[bass.ds(t * P, P), :]).then_inc(q_in[b], 16)
                    e.tiles4(sp, step)

                @block.tensor
                def _(pe):
                    pe.sem_inc(q_used, 4)

                    def step(t, b, n, j):
                        pe.wait_ge(att_added, l * (T + 2) + (t + 1))
                        pe.wait_ge(q_in[b], (l * uses4(b) + j) * 16 + 16)
                        for c in range(HALF):
                            last = nc.tensor.matmul(psF[:, b % 2, 0:D], QIN[:, b, c * P:(c + 1) * P], MX[:, c, :],
                                                    start=(c == 0), stop=(c == HALF - 1))
                        last.then_inc(q_used, 1)
                        if n == P:
                            G.add_up(pe, block_q(l, 2, t), b % 2, block_j(l, 2, j * 2 + b // 2), psG)
                    e.tiles4(pe, step)

                @block.vector
                def _(v):
                    v.sem_inc(att_added, 2)

                    def step(t, b, n, j):
                        if n == P:
                            G.stage(block_q(l, 2, t) + 1, 1 - b % 2)
                        V.tensor_tensor(X[:, t, :], X[:, t, :], out_bias[:, 0, :], ALU.add)
                        v.drain()
                        hold(v, q_used, l * (T + 4) + (t + 5))
                        V.tensor_tensor(X[:, t, :], X[:, t, :], psF[:, b % 2, 0:D], ALU.add).then_inc(att_added, 1)
                        v.drain()
                        e.row_stats(v, t)
                        if n == P:
                            G.accumulate(v, block_q(l, 2, t), b % 2, psG, Y)
                    e.tiles4(v, step)

        e.rstd_block(l * 2 + 2)

        with ExitStack() as own:
            XS, HT = e.sb("XS3", [P, 2, D], f32, own), e.sb("HT3", [P, 2, D], f32, own)
            GT = e.sb("GT", [P, MF, P], f32, own)
            psT, psF = e.pb("psT3", [P, BANK], own), e.pb("psF3", [P, BANK], own)
            psU = e.pb("psU", [P, MF, P], own)
            with nc.Block() as block:
                @block.gpsimd
                def _(pool):
                    def step(t, b, n, j):
                        if n == P:
                            for q, parity, _ in beside(l, b, j):
                                G.gather(pool, q, parity)
                    tiles_by_six(pool, step)

                @block.vector
                def _(v):
                    v.sem_inc(down_added, 1)

                    def xn(t, b):
                        e.normalise(t, XS[:, b, :]).then_inc(xn2_ready, 1)

                    def step(t, b, n, j):
                        V.tensor_tensor(X[:, t, :], X[:, t, :], out_bias[:, 1, :], ALU.add)
                        if n == P:
                            for q, parity, _ in beside(l, b, j):
                                G.stage(q + 1, 1 - parity)
                                G.accumulate(v, q, parity, psG, Y)
                        else:
                            v.drain()
                        if ahead(t, 2):
                            xn(t + 2, b % 2)
                        hold(v, down_ready, l * T + (t + 1))
                        V.tensor_tensor(X[:, t, :], X[:, t, :], psF[:, 0:D], ALU.add).then_inc(down_added, 1)
                        v.drain()
                        e.row_stats(v, t)
                    xn(0, 0)
                    xn(1, 1)
                    tiles_by_six(v, step, to_last=True)

                @block.scalar
                def _(act):
                    def ht(t, b):
                        act.wait_ge(tp2_ready, l * T + (t + 1))
                        for c in range(HALF):
                            last = S.activation(HT[:, b, c * P:(c + 1) * P], psT[:, c * P:(c + 1) * P], ACT.Identity,
                                                bias=ln[:, 3, c:c + 1], scale=ln[:, 2, c:c + 1])
                        last.then_inc(ht2_ready, 1)

                    def step(t, b, n, j):
                        if n == P:
                            ht(t + 1, 1 - b)
                        for x in range(2):
                            act.wait_ge(up_ready, l * (2 * T) + (t * 2 + (x + 1)))
                            for m in range(x * MF // 2, (x + 1) * MF // 2):
                                last = S.activation(GT[:, m, :], psU[:, m, :], ACT.Gelu, bias=b1[:, m:m + 1])
                            last.then_inc(gelu_ready, 1)
                    ht(0, 0)
                    tiles(act, step)

                @block.tensor
                def _(pe):
                    def turn(t, b):
                        pe.wait_ge(xn2_ready, l * T + (t + 1))
                        e.transpose_tile(psT[:, 0:D], XS[:, b, :]).then_inc(tp2_ready, 1)

                    def step(t, b, n, j):
                        pe.wait_ge(ht2_ready, l * T + (t + 1))
                        if n == P:
                            turn(t + 1, 1 - b % 2)
                        blocks = beside(l, b, j) if n == P else []
                        for q, parity, earlier in blocks[:1]:
                            G.add_up(pe, q, parity, earlier, psG)
                        for m in range(MF):
                            for c in range(HALF):
                                last = nc.tensor.matmul(psU[:, m, :], W1[:, c, m * P:(m + 1) * P], HT[:, b % 2, c * P:(c + 1) * P],
                                                        start=(c == 0), stop=(c == HALF - 1))
                            if m % (MF // 2) == MF // 2 - 1:
                                last.then_inc(up_ready, 1)
                        for q, parity, earlier in blocks[1:]:
                            G.add_up(pe, q, parity, earlier, psG)
                        pe.wait_ge(down_added, l * (T + 1) + (t + 1))
                        for m in range(MF):
                            if m % (MF // 2) == 0:
                                pe.wait_ge(gelu_ready, l * (2 * T) + (t * 2 + (m // (MF // 2) + 1)))
                            last = nc.tensor.matmul(psF[:, 0:D], GT[:, m, :], W2[:, m, :], start=(m == 0), stop=(m == MF - 1))
                        last.then_inc(down_ready, 1)
                    turn(0, 0)
                    tiles_by_six(pe, step)
    layer.close()
    e.G.append(G)
    e.G.append(psG)


def sum_phase(nc, A, e):
    X, Y, ones, tiles, hold = e.X, e.Y, e.ones, e.tiles, e.hold
    V = nc.vector
    G, psG = e.G
    left = GNN_BLOCKS - MIXED
    assert left % 2 == 0 and left > 2 and MIXED % 2 == 0 and (T - 1) % SIX == 0 and SIX % 2 == 0 and WITH_SIX % 2 == 0
    with nc.Block() as block:
        def blocks(eng, step):
            with eng.Fori(0, left // 2 - 1) as j:
                for b in range(2):
                    step(j * 2 + (MIXED + b), b, j + MIXED // 2, True)
            for b in range(2):
                step(GNN_BLOCKS - 2 + b, b, GNN_BLOCKS // 2 - 1, b == 0)

        @block.gpsimd
        def _(pool):
            blocks(pool, lambda q, b, j, more: G.gather(pool, q, b))

        @block.tensor
        def _(pe):
            blocks(pe, lambda q, b, j, more: G.add_up(pe, q, b, j, psG))

        @block.vector
        def _(v):
            def step(q, b, j, more):
                if more:
                    G.stage(q + 1, 1 - b)
                G.accumulate(v, q, b, psG, Y)
            blocks(v, step)

    with ExitStack() as own:
        bn = e.sb("bn", [P, 4, D], f32, own)
        neg_mean, scale, shift, work = (bn[:, i, :] for i in range(4))
        gb = e.sb("gb", [1, 2 * D], f32, own)
        SQ, XI = e.sb("SQ", [P, 2, D], f32, own), e.sb("XI", [P, 2, 4, D], f32, own)
        ps = e.pb("psBN", [P, 2, BANK], own)
        gb_in, sums_ready, centred, sq_ready, sq_used = e.sem("gb_in"), e.sem("sums_ready"), e.sem("centred"), e.sem("sq_ready"), e.sem("sq_used")
        gb_ready, v_ready, sd_ready, x_used, xi_in = e.sem("gb_ready"), e.sem("bn_v_ready"), e.sem("bn_sd_ready"), e.sem("x_used"), e.sem2("xi_in")
        with nc.Block() as block:
            @block.sync
            def _(sp):
                sp.dma_start(gb[:, 0:D], A["L0_gnn_gamma"].rearrange("(a n) -> a n", a=1)).then_inc(gb_in, 16)
                sp.dma_start(gb[:, D:2 * D], A["L0_gnn_beta"].rearrange("(a n) -> a n", a=1)).then_inc(gb_in, 16)
                sp.wait_ge(gb_in, 32)

            @block.tensor
            def _(pe):
                nc.tensor.matmul(ps[:, 0, 0:D], e.zeros[0:1, 0:P], e.zeros[0:1, 0:D], start=True, stop=False)
                tiles(pe, lambda t, b, n, j: nc.tensor.matmul(ps[:, 0, 0:D], ones[0:n, :], Y[0:n, t, :], start=False, stop=(n != P)))

        with nc.Block() as block:
            @block.vector
            def _(v):
                V.tensor_scalar(neg_mean, ps[:, 0, 0:D], -1.0 / N, None, ALU.mult)
                v.drain()
                tiles(v, lambda t, b, n, j: V.tensor_tensor(Y[:, t, :], Y[:, t, :], neg_mean, ALU.add).then_inc(centred, 1))

            @block.scalar
            def _(act):
                def step(t, b, n, j):
                    hold(act, sq_used, t + 1)
                    act.wait_ge(centred, t + 1)
                    nc.scalar.activation(SQ[:, b, :], Y[:, t, :], ACT.Square).then_inc(sq_ready, 1)
                tiles(act, step)

            @block.tensor
            def _(pe):
                pe.sem_inc(sq_used, 2)

                def step(t, b, n, j):
                    pe.wait_ge(sq_ready, t + 1)
                    nc.tensor.matmul(ps[:, 1, 0:D], ones[0:n, :], SQ[0:n, b, :], start=False, stop=(n != P)).then_inc(sq_used, 1)
                nc.tensor.matmul(ps[:, 1, 0:D], e.zeros[0:1, 0:P], e.zeros[0:1, 0:D], start=True, stop=False)
                tiles(pe, step)

        with nc.Block() as block:
            @block.tensor
            def _(pe):
                nc.tensor.matmul(ps[:, 0, :], ones[0:1, :], gb[:, :], start=True, stop=True).then_inc(gb_ready, 1)

            @block.scalar
            def _(act):
                act.wait_ge(v_ready, 1)
                nc.scalar.activation(scale, work, ACT.Sqrt).then_inc(sd_ready, 1)

            @block.vector
            def _(v):
                V.tensor_scalar(work, ps[:, 1, 0:D], 1.0 / N, EPS, ALU.mult, ALU.add).then_inc(v_ready, 1)
                v.wait_ge(sd_ready, 1)
                V.reciprocal(scale, scale)
                v.drain()
                V.tensor_tensor(neg_mean, scale, scale, ALU.mult)
                v.drain()
                V.tensor_tensor(neg_mean, neg_mean, work, ALU.mult)
                v.drain()
                V.tensor_scalar(neg_mean, neg_mean, -0.5, 1.5, ALU.mult, ALU.add)
                v.drain()
                V.tensor_tensor(scale, scale, neg_mean, ALU.mult)
                v.wait_ge(gb_ready, 1)
                V.tensor_copy(shift, ps[:, 0, D:2 * D])
                v.drain()
                V.tensor_tensor(scale, scale, ps[:, 0, 0:D], ALU.mult)

        with nc.Block() as block:
            @block.sync
            def _(sp):
                def step(i, b):
                    hold(sp, x_used, i + 1)
                    sp.dma_start(XI[:, b, :, :], A["x"][bass.ds(i * (4 * P), 4 * P), :].rearrange("(t p) d -> p t d", p=P)).then_inc(xi_in[b], 16)
                with sp.Fori(0, T // 8) as j:
                    for b in range(2):
                        step(j * 2 + b, b)
                hold(sp, x_used, T // 4 + 1)
                sp.dma_start(XI[0:LAST, 0, 0, :], A["x"][N - LAST:N, :]).then_inc(xi_in[0], 16)

            @block.vector
            def _(v):
                v.sem_inc(x_used, 2)

                def add(t, b, j, w):
                    y, x, n = Y[:, bass.ds(t, w), :], X[:, bass.ds(t, w), :], P if w > 1 else LAST

                    def over(row):
                        return row.unsqueeze(1).to_broadcast([P, w, D])
                    V.tensor_tensor(y, y, over(scale), ALU.mult)
                    v.drain()
                    V.tensor_tensor(y, y, over(shift), ALU.add)
                    v.drain()
                    V.scalar_tensor_tensor(x, y, 0.0, x, ALU.max, ALU.add)
                    v.drain()
                    hold(v, xi_in[b], j * 16 + 16)
                    V.tensor_tensor(X[0:n, bass.ds(t, w), :], X[0:n, bass.ds(t, w), :], XI[0:n, b, 0:w, :], ALU.add).then_inc(x_used, 1)
                    v.drain()
                e.all_stats(v, add)


def expert_phase(nc, A, out, e):
    X, ident, ones, tiles, hold = e.X, e.ident, e.ones, e.tiles, e.hold
    V, S = nc.vector, nc.scalar
    phase = e.ctx.enter_context(ExitStack())
    e.rstd_block(2 * LAYERS + 1)
    gate = e.sb("gate", [P, T, NE], f32, phase)

    with ExitStack() as own:
        att = e.sb("att", [P, 5 * HE], f32, own)
        att_row = e.sb("att_row", [1, 5 * HE], f32, own)
        Wg = e.sb("Wg", [P, HALF, HE], f32, own)
        tab = e.sb("tab", [P, T, TAB], f32, own)
        am = e.sb("am", [P, T, 2 * GH], f32, own)
        best = e.sb("best", [P, T, GH], f32, own)
        acc = e.sb("acc", [P, T, MSG], f32, own)
        wk = e.sb("wk", [P, T, HE], f32, own)
        wk4, wk4b = e.sb("wk4", [P, T, GH], f32, own), e.sb("wk4b", [P, T, GH], f32, own)
        up = e.sb("up", [P, 2, GH], f32, own)
        att_rows = ["L0_ffn_att_src", "L0_ffn_att_dst", "L0_ffn_b_gat", "L0_ffn_ln_gamma", "L0_ffn_ln_beta"]

        def over_tiles(i):
            return att[:, i * HE:(i + 1) * HE].unsqueeze(1).to_broadcast([P, T, HE])

        def by_head(ap):
            return ap.rearrange("p t (h x) -> p t h x", h=GH)

        def each_head(ap, n):
            return ap.unsqueeze(3).to_broadcast([P, T, GH, n])

        with ExitStack() as own2:
            XS, HT = e.sb("XS4", [P, 2, D], f32, own2), e.sb("HT4", [P, 2, D], f32, own2)
            psT, psH, psR = e.pb("psT4", [P, BANK], own2), e.pb("psH", [P, 2, BANK], own2), e.pb("psR", [P, BANK], own2)
            g_in, row_ready, xn_ready, tp_ready, ht_ready = e.sem("g_in"), e.sem("row_ready"), e.sem("xn4_ready"), e.sem("tp4_ready"), e.sem("ht4_ready")
            h_ready, max_ready, all_ready, tab_ready, tab_out = e.sem("h_ready"), e.sem("max_ready"), e.sem("all_ready"), e.sem("tab_ready"), e.sem("tab_out")
            with nc.Block() as block:
                @block.sync
                def _(sp):
                    sp.dma_start(Wg[:, :, :], A["L0_ffn_W_gat"].rearrange("(c p) n -> p c n", p=P)).then_inc(g_in, 16)
                    for i, name in enumerate(att_rows):
                        a = A[name]
                        a = a.rearrange("(a h) e -> a (h e)", a=1) if i < 2 else a.rearrange("(a n) -> a n", a=1)
                        sp.dma_start(att_row[:, i * HE:(i + 1) * HE], a).then_inc(g_in, 16)
                    sp.wait_ge(tab_ready, 1)
                    sp.dma_start(e.tab_d.rearrange("(t p) c -> p t c", p=P), tab[:, :, :]).then_inc(tab_out, 16)
                    sp.wait_ge(tab_out, 16)

                @block.tensor
                def _(pe):
                    pe.wait_ge(g_in, 96)
                    nc.tensor.matmul(psR[:, 0:5 * HE], ones[0:1, :], att_row[:, :], start=True, stop=True).then_inc(row_ready, 1)

                    def turn(t, b):
                        pe.wait_ge(xn_ready, t + 1)
                        e.transpose_tile(psT[:, 0:D], XS[:, b, :]).then_inc(tp_ready, 1)

                    def step(t, b, n, j):
                        pe.wait_ge(ht_ready, t + 1)
                        if n == P:
                            turn(t + 1, 1 - b)
                        for c in range(HALF):
                            last = nc.tensor.matmul(psH[:, b, 0:HE], HT[:, b, c * P:(c + 1) * P], Wg[:, c, :], start=(c == 0), stop=(c == HALF - 1))
                        last.then_inc(h_ready, 1)
                    turn(0, 0)
                    tiles(pe, step)

                @block.scalar
                def _(act):
                    def step(t, b, n, j):
                        act.wait_ge(tp_ready, t + 1)
                        S.activation(HT[:, b, :], psT[:, 0:D], ACT.Copy).then_inc(ht_ready, 1)
                    tiles(act, step)

                @block.gpsimd
                def _(pool):
                    pool.wait_ge(max_ready, 1)
                    nc.gpsimd.partition_all_reduce(up[:, 1, :], up[:, 0, :], P, bass.bass_isa.ReduceOp.max).then_inc(all_ready, 1)

                @block.vector
                def _(v):
                    def xn(t, b):
                        e.normalise(t, XS[:, b, :]).then_inc(xn_ready, 1)

                    def step(t, b, n, j):
                        if n == P:
                            xn(t + 1, 1 - b)
                        hold(v, h_ready, t + 1)
                        V.tensor_copy(tab[:, t, 0:HE], psH[:, b, 0:HE])
                    xn(0, 0)
                    tiles(v, step)
                    v.wait_ge(row_ready, 1)
                    V.tensor_copy(att[:, :], psR[:, 0:5 * HE])
                    v.drain()
                    for i, dst in enumerate((tab[:, :, HE:HE + GH], am[:, :, 0:GH])):
                        V.tensor_tensor(wk[:, :, :], tab[:, :, 0:HE], over_tiles(i), ALU.mult)
                        v.drain()
                        V.tensor_reduce(dst, by_head(wk[:, :, :]), AX.X, ALU.add)
                        v.drain()
                    V.tensor_scalar(wk4[:, :, :], tab[:, :, HE:HE + GH], -1.0, None, ALU.mult)
                    v.drain()
                    V.tensor_reduce(up[:, 0, :], wk4[:, :, :].rearrange("p t h -> p h t"), AX.X, ALU.max).then_inc(max_ready, 1)
                    v.wait_ge(all_ready, 1)
                    V.tensor_tensor(tab[:, :, HE + GH:TAB], tab[:, :, HE:HE + GH], up[:, 1, :].unsqueeze(1).to_broadcast([P, T, GH]), ALU.add).then_inc(tab_ready, 1)
                    v.drain()
                    V.tensor_copy(best[:, :, :], tab[:, :, HE + GH:TAB])

        kept = own.enter_context(ExitStack())
        tile_row = e.sb("gat_tile_row", [1, GAT_G * GAT_Q], i16, kept)
        node = e.sb("gat_node_f32", [P, GAT_G * GAT_Q], f32, kept)
        am_parts = e.sb("am_parts", [P, T, 3, 2 * GH], bf16, kept)
        rows_all = e.sb("rows_all", [P, GAT_G * GAT_Q, MSG], f32, kept)
        BLOCKS = GAT_BLOCKS
        assert BLOCKS % 2 == 0

        def onehots(act, dst, off, q):
            for s in range(UB):
                S.activation(off[:, s, :], e.node_no[:, :], ACT.Abs, bias=node[:, bass.ds(q * UB + s, 1)], scale=-1.0)
            act.drain()
            return S.activation(dst, off, ACT.Relu, bias=ones[:, 0:1], scale=-1.0)

        with ExitStack() as own2:
            numbers = e.sb("gat_numbers", [P, 2, UB], i32, own2)
            oh = e.sb("gat_onehot", [P, 2, UB, P], f32, own2)
            off = e.sb("gat_distance", [P, 2, UB, P], f32, own2)
            rows = e.sb("gat_rows", [P, 2, UB, TAB], f32, own2)
            diag = e.sb("gat_diag", [P, 2, UB, GH, P], f32, own2)
            most = e.sb("gat_most", [P, UB, GH], f32, own2)
            psM = e.pb("psM", [P, 2, UB, GH * P], own2)
            BY_DVE = UB // 2
            nil = e.sb("nil", [P, 1], f32, own2)
            rest_diag_ready = e.sem("gat_rest_diag_ready")
            row_in, node_ready, oh_ready, diag_ready, masked = e.sem("gat_row_in"), e.sem("gat_node_ready"), e.sem("gat_oh_ready"), e.sem("gat_diag_ready"), e.sem("gat_masked")
            gathered = [e.sem(f"gat_gathered{i}") for i in range(2 * UB)]

            def blocks(eng, step):
                with eng.Fori(0, BLOCKS // 2 - 1) as j:
                    step(j * 2 + 1, 1, j, True)
                    step(j * 2 + 2, 0, j + 1, True)
                step(BLOCKS - 1, 1, BLOCKS // 2 - 1, False)

            with nc.Block() as block:
                @block.sync
                def _(sp):
                    sp.dma_start(tile_row[:, :], e.gat_tile_d.rearrange("(a g) q -> a (g q)", a=1)).then_inc(row_in, 16)

                @block.gpsimd
                def _(pool):
                    def step(q, b, j, more):
                        hold(pool, diag_ready, q + 1)
                        hold(pool, rest_diag_ready, q + 1)
                        nc.gpsimd.tensor_copy(numbers[:, b, :], e.gat_src[:, bass.ds(q * UB, UB)])
                        pool.drain()
                        for s in range(UB):
                            nc.gpsimd.indirect_dma_start(out=rows[:, b, s, :], out_offset=None, in_=e.tab_d,
                                                         in_offset=bass.IndirectOffsetOnAxis(ap=numbers[:, b, s:s + 1], axis=0)).then_inc(gathered[b * UB + s], 16)
                    step(0, 0, 0, True)
                    blocks(pool, step)

                @block.tensor
                def _(pe):
                    def step(q, b, j, more):
                        pe.wait_ge(oh_ready, q + 1)
                        pe.wait_ge(diag_ready, q + 3)
                        pe.wait_ge(rest_diag_ready, q + 3)
                        for s in range(UB):
                            last = nc.tensor.matmul(psM[:, b, s, :], oh[:, b, s, :], diag[:, b, s, :, :].rearrange("p h n -> p (h n)"), start=True, stop=True)
                        last.then_inc(masked, 1)
                    pe.sem_inc(masked, 2)
                    step(0, 0, 0, True)
                    blocks(pe, step)

                @block.scalar
                def _(act):
                    def step(q, b, j, more):
                        hold(act, masked, q + 1)
                        onehots(act, oh[:, b, :, :], off[:, b, :, :], q).then_inc(oh_ready, 1)
                        for s in range(BY_DVE, UB):
                            hold(act, gathered[b * UB + s], j * 16 + 16)
                            for h in range(GH):
                                last = S.activation(diag[:, b, s, h, :], ident[:, :], ACT.Identity, bias=nil[:, :], scale=rows[:, b, s, HE + GH + h:HE + GH + h + 1])
                        last.then_inc(rest_diag_ready, 1)
                    act.sem_inc(rest_diag_ready, 2)
                    hold(act, node_ready, 1)
                    step(0, 0, 0, True)
                    blocks(act, step)

                @block.vector
                def _(v):
                    def spread(q, b, j):
                        for s in range(UB):
                            hold(v, gathered[b * UB + s], j * 16 + 16)
                        V.tensor_copy(rows_all[:, bass.ds(q * UB, UB), :], rows[:, b, :, 0:MSG])
                        for s in range(BY_DVE):
                            last = V.tensor_tensor(diag[:, b, s, :, :], ident[:, :].unsqueeze(1).to_broadcast([P, GH, P]),
                                                   rows[:, b, s, HE + GH:TAB].unsqueeze(2).to_broadcast([P, GH, P]), ALU.mult)
                        last.then_inc(diag_ready, 1)

                    def largest(q, b):
                        tiles = e.chunk_tiles(v, tile_row, q)
                        hold(v, masked, q + 3)
                        V.tensor_reduce(most[:, :, :].rearrange("p s h -> p (s h)"), psM[:, b, :, :].rearrange("p s (h n) -> p (s h) n", h=GH), AX.X, ALU.max)
                        v.drain()
                        for s, t in enumerate(tiles):
                            V.tensor_tensor(best[:, t, :], best[:, t, :], most[:, s, :], ALU.max)
                            v.drain()

                    def step(q, b, j, more):
                        spread(q, b, j)
                        largest(q - 1, 1 - b)
                    v.sem_inc(diag_ready, 2)
                    V.memset(nil[:, :], 0.0)
                    V.tensor_copy(node[:, :], e.gat_node[:, :]).then_inc(node_ready, 1)
                    hold(v, row_in, 16)
                    spread(0, 0, 0)
                    blocks(v, step)
                    largest(BLOCKS - 1, 1)

        own_ready, own_exp = e.sem("own_ready"), e.sem("own_exp")
        with nc.Block() as block:
            @block.vector
            def _(v):
                V.tensor_tensor(wk4[:, :, :], best[:, :, :], up[:, 1, :].unsqueeze(1).to_broadcast([P, T, GH]), ALU.subtract)
                v.drain()
                V.tensor_tensor(wk4[:, :, :], wk4[:, :, :], am[:, :, 0:GH], ALU.add)
                v.drain()
                V.scalar_tensor_tensor(am[:, :, GH:2 * GH], wk4[:, :, :], 0.2, wk4[:, :, :], ALU.mult, ALU.max)
                V.tensor_tensor(wk4b[:, :, :], tab[:, :, HE:HE + GH], am[:, :, 0:GH], ALU.add)
                v.drain()
                V.scalar_tensor_tensor(wk4[:, :, :], wk4b[:, :, :], 0.2, wk4b[:, :, :], ALU.mult, ALU.max)
                v.drain()
                V.tensor_tensor(wk4[:, :, :], wk4[:, :, :], am[:, :, GH:2 * GH], ALU.subtract).then_inc(own_ready, 1)
                v.wait_ge(own_exp, 1)
                V.tensor_tensor(by_head(acc[:, :, 0:HE]), by_head(tab[:, :, 0:HE]), each_head(acc[:, :, HE:MSG], NE), ALU.mult)
                rest = wk[:, :, 0:2 * GH]
                V.tensor_copy(rest, am[:, :, :])
                v.drain()
                for i in range(3):
                    V.tensor_copy(am_parts[:, :, i, :], rest)
                    v.drain()
                    if i < 2:
                        V.tensor_tensor(rest, rest, am_parts[:, :, i, :], ALU.subtract)
                        v.drain()

            @block.scalar
            def _(act):
                act.wait_ge(own_ready, 1)
                S.activation(acc[:, :, HE:MSG], wk4[:, :, :], ACT.Exp).then_inc(own_exp, 1)

        with ExitStack() as own2:
            oh = e.sb("sum_onehot", [P, 6, UB, P], f32, own2)
            off = e.sb("sum_distance", [P, 2, UB, P], f32, own2)
            oht = e.sb("sum_onehot_t", [P, 3, UB, P], bf16, own2)
            ea, eb, ex = (e.sb("edge_" + x, [P, 3, UB, GH], f32, own2) for x in "abc")
            msg = e.sb("msg", [P, 3, UB, MSG], f32, own2)
            psO, psE, psS = e.pb("psO", [P, BANK], own2), e.pb("psE", [P, 3, BANK], own2), e.pb("psS", [P, 3, BANK], own2)
            oh_ready, turned, oht_ready, ends_ready = e.sem("sum_oh_ready"), e.sem("sum_turned"), e.sem("sum_oht_ready"), e.sem("sum_ends_ready")
            e_ready, ex_ready, msg_ready, sum_ready = e.sem("sum_e_ready"), e.sem("sum_ex_ready"), e.sem("sum_msg_ready"), e.sem("sum_ready")
            assert BLOCKS % 6 == 0

            def steps(eng, step):
                for k in range(6):
                    step(k, k, k)
                with eng.Fori(1, BLOCKS // 6 - 1) as j:
                    for b in range(6):
                        step(j * 6 + b, b, 6)
                for k in range(BLOCKS - 6, BLOCKS + 2):
                    step(k, k % 6, k)

            with nc.Block() as block:
                @block.vector
                def _(v):
                    def add(q, b, tiles):
                        for s, t in enumerate(tiles):
                            V.tensor_tensor(acc[:, t, :], acc[:, t, :], psS[:, b, s * MSG:(s + 1) * MSG], ALU.add)
                            v.drain()

                    def exponents(q, b):
                        ends = psE[:, b, 0:UB * 2 * GH].rearrange("p (s x) -> p s x", s=UB)
                        hold(v, ends_ready, q + 1)
                        V.tensor_tensor(ea[:, b, :, :], rows_all[:, bass.ds(q * UB, UB), HE:MSG], ends[:, :, 0:GH], ALU.add)
                        v.drain()
                        V.scalar_tensor_tensor(eb[:, b, :, :], ea[:, b, :, :], 0.2, ea[:, b, :, :], ALU.mult, ALU.max)
                        v.drain()
                        V.tensor_tensor(ea[:, b, :, :], eb[:, b, :, :], ends[:, :, GH:2 * GH], ALU.subtract).then_inc(e_ready, 1)

                    def messages(q, b):
                        hold(v, ex_ready, q + 1)
                        V.tensor_copy(msg[:, b, :, HE:MSG], ex[:, b, :, :])
                        V.tensor_tensor(msg[:, b, :, 0:HE].rearrange("p s (h x) -> p s h x", h=GH),
                                        rows_all[:, bass.ds(q * UB, UB), 0:HE].rearrange("p s (h x) -> p s h x", h=GH),
                                        ex[:, b, :, :].unsqueeze(3).to_broadcast([P, UB, GH, NE]), ALU.mult).then_inc(msg_ready, 1)

                    def step(k, b, at):
                        if at >= 2:
                            tiles = e.chunk_tiles(v, tile_row, k - 2)
                            hold(v, sum_ready, k + 5)
                        if 1 <= at <= BLOCKS:
                            messages(k - 1, (b - 1) % 3)
                        if at < BLOCKS:
                            exponents(k, b % 3)
                        if at >= 2:
                            add(k - 2, (b - 2) % 3, tiles)
                    steps(v, step)

                @block.scalar
                def _(act):
                    def one_turned(q, b):
                        act.wait_ge(turned, q + 1)
                        S.activation(oht[:, b, :, :].rearrange("p s n -> p (s n)"), psO[:, :], ACT.Copy).then_inc(oht_ready, 1)

                    def ones_of(q, b):
                        hold(act, sum_ready, q + 1)
                        onehots(act, oh[:, b, :, :], off[:, b % 2, :, :], q).then_inc(oh_ready, 1)

                    def step(k, b, at):
                        if at + 1 < BLOCKS:
                            one_turned(k + 1, (b + 1) % 3)
                        if at < BLOCKS:
                            act.wait_ge(e_ready, k + 1)
                            S.activation(ex[:, b % 3, :, :], ea[:, b % 3, :, :], ACT.Exp).then_inc(ex_ready, 1)
                        if at + 3 < BLOCKS:
                            ones_of(k + 3, (b + 3) % 6)
                    for q in range(3):
                        ones_of(q, q)
                    one_turned(0, 0)
                    steps(act, step)

                @block.tensor
                def _(pe):
                    def turn(q, b):
                        pe.wait_ge(oh_ready, q + 1)
                        for s in range(UB):
                            last = nc.tensor.transpose(psO[:, s * P:(s + 1) * P], oh[:, b, s, :], ident[:, :])
                        last.then_inc(turned, 1)

                    def ends(q, b):
                        tiles = e.chunk_tiles(pe, tile_row, q)
                        hold(pe, oht_ready, q + 1)
                        for s, t in enumerate(tiles):
                            for i in range(3):
                                last = nc.tensor.matmul(psE[:, b % 3, s * 2 * GH:(s + 1) * 2 * GH], oht[:, b % 3, s, :], am_parts[:, t, i, :], start=(i == 0), stop=(i == 2))
                        last.then_inc(ends_ready, 1)

                    def sums(q, b):
                        pe.wait_ge(msg_ready, q + 1)
                        for s in range(UB):
                            last = nc.tensor.matmul(psS[:, b % 3, s * MSG:(s + 1) * MSG], oh[:, b, s, :], msg[:, b % 3, s, :], start=True, stop=True)
                        last.then_inc(sum_ready, 1)

                    def step(k, b, at):
                        if at < BLOCKS:
                            ends(k, b)
                        if at + 1 < BLOCKS:
                            turn(k + 1, (b + 1) % 6)
                        if 1 <= at <= BLOCKS:
                            sums(k - 1, (b - 1) % 6)
                    pe.sem_inc(sum_ready, 6)
                    turn(0, 0)
                    steps(pe, step)
        kept.close()

        gv_ready, gsd_ready, sx_ready, se_ready = e.sem("gv_ready"), e.sem("gsd_ready"), e.sem("sx_ready"), e.sem("se_ready")
        with ExitStack() as own2:
            one = [e.sb(f"one{i}", [P, T], f32, own2) for i in range(4)]
            score = e.sb("score", [P, T, NE], f32, own2)
            rank = e.sb("rank", [P, T, NE], f32, own2)

            def over(ap, n):
                return ap.unsqueeze(2).to_broadcast([P, T, n])

            with nc.Block() as block:
                @block.scalar
                def _(act):
                    act.wait_ge(gv_ready, 1)
                    S.activation(one[1][:, :], one[0][:, :], ACT.Sqrt).then_inc(gsd_ready, 1)
                    act.wait_ge(sx_ready, 1)
                    S.activation(gate[:, :, :], gate[:, :, :], ACT.Exp).then_inc(se_ready, 1)

                @block.vector
                def _(v):
                    def do(ins):
                        v.drain()
                        return ins
                    W = wk[:, :, :]
                    do(V.tensor_scalar(wk4[:, :, :], acc[:, :, HE:MSG], 1e-16, None, ALU.add))
                    do(V.reciprocal(wk4[:, :, :], wk4[:, :, :]))
                    do(V.tensor_tensor(by_head(W), by_head(acc[:, :, 0:HE]), each_head(wk4[:, :, :], NE), ALU.mult))
                    do(V.tensor_tensor(W, W, over_tiles(2), ALU.add))
                    do(V.tensor_reduce(one[0][:, :], W, AX.X, ALU.add))
                    do(V.tensor_scalar(one[0][:, :], one[0][:, :], 1.0 / HE, None, ALU.mult))
                    do(V.tensor_tensor(W, W, over(one[0][:, :], HE), ALU.subtract))
                    do(V.tensor_tensor(acc[:, :, 0:HE], W, W, ALU.mult))
                    do(V.tensor_reduce(one[0][:, :], acc[:, :, 0:HE], AX.X, ALU.add))
                    V.tensor_scalar(one[0][:, :], one[0][:, :], 1.0 / HE, EPS, ALU.mult, ALU.add).then_inc(gv_ready, 1)
                    v.wait_ge(gsd_ready, 1)
                    do(V.reciprocal(one[1][:, :], one[1][:, :]))
                    do(V.tensor_tensor(one[2][:, :], one[1][:, :], one[1][:, :], ALU.mult))
                    do(V.tensor_tensor(one[2][:, :], one[2][:, :], one[0][:, :], ALU.mult))
                    do(V.tensor_scalar(one[2][:, :], one[2][:, :], -0.5, 1.5, ALU.mult, ALU.add))
                    do(V.tensor_tensor(one[1][:, :], one[1][:, :], one[2][:, :], ALU.mult))
                    do(V.tensor_tensor(W, W, over(one[1][:, :], HE), ALU.mult))
                    do(V.tensor_tensor(W, W, over_tiles(3), ALU.mult))
                    do(V.tensor_tensor(W, W, over_tiles(4), ALU.add))
                    do(V.tensor_reduce(score[:, :, :], W.rearrange("p t (h x) -> p t x h", h=GH), AX.X, ALU.add))
                    do(V.tensor_scalar(score[:, :, :], score[:, :, :], 1.0 / GH, None, ALU.mult))
                    for i in range(NE):
                        do(V.memset(rank[:, :, i:i + 1], float(i)))
                    for i in range(NE):
                        for k in range(i + 1, NE):
                            do(V.tensor_tensor(one[2][:, :], score[:, :, k], score[:, :, i], ALU.is_gt))
                            do(V.tensor_tensor(rank[:, :, i], rank[:, :, i], one[2][:, :], ALU.add))
                            do(V.tensor_tensor(rank[:, :, k], rank[:, :, k], one[2][:, :], ALU.subtract))
                    do(V.tensor_scalar(rank[:, :, :], rank[:, :, :], 2.0, None, ALU.is_lt))
                    do(V.tensor_reduce(one[2][:, :], score[:, :, :], AX.X, ALU.max))
                    V.tensor_tensor(gate[:, :, :], score[:, :, :], over(one[2][:, :], NE), ALU.subtract).then_inc(sx_ready, 1)
                    v.wait_ge(se_ready, 1)
                    do(V.tensor_tensor(gate[:, :, :], gate[:, :, :], rank[:, :, :], ALU.mult))
                    do(V.tensor_reduce(one[3][:, :], gate[:, :, :], AX.X, ALU.add))
                    do(V.reciprocal(one[3][:, :], one[3][:, :]))
                    do(V.tensor_tensor(gate[:, :, :], gate[:, :, :], over(one[3][:, :], NE), ALU.mult))

    with ExitStack() as own:
        W1, W2 = e.sb("EW1", [P, HALF, NE, EF], f32, own), e.sb("EW2", [P, ME, NE, D], f32, own)
        b1, b2 = e.sb("Eb1", [P, NE, ME], f32, own), e.sb("Eb2", [P, NE, D], f32, own)
        XS, HT = e.sb("XS5", [P, 2, D], f32, own), e.sb("HT5", [P, 2, D], f32, own)
        GT = e.sb("EGT", [P, 2, EF], f32, own)
        psT, psU, psD = e.pb("psT5", [P, BANK], own), e.pb("psU5", [P, 2, BANK], own), e.pb("psD5", [P, 2, BANK], own)
        w_in, xn_ready, tp_ready, ht_ready = e.sem("ew_in"), e.sem("xn5_ready"), e.sem("tp5_ready"), e.sem("ht5_ready")
        up_ready, gelu_ready, down_ready, down_added, rows_out = e.sem("eup_ready"), e.sem("egelu_ready"), e.sem("edown_ready"), e.sem("edown_added"), e.sem("rows_out")
        with nc.Block() as block:
            @block.sync
            def _(sp):
                for x in range(NE):
                    sp.dma_start(W1[:, :, x, :], A["L0_ffn_W1"][x, :, :].rearrange("(c p) n -> p c n", p=P)).then_inc(w_in, 16)
                    sp.dma_start(W2[:, :, x, :], A["L0_ffn_W2"][x, :, :].rearrange("(c p) n -> p c n", p=P)).then_inc(w_in, 16)
                    sp.dma_start(b1[:, x, :], A["L0_ffn_b1"][x, :].rearrange("(m p) -> p m", p=P), allow_slow_non_contiguous=True).then_inc(w_in, 16)
                    sp.dma_start(b2[:, x, :], A["L0_ffn_b2"][x:x + 1, :].to_broadcast([P, D])).then_inc(w_in, 16)

                def step(t, b, n, j):
                    hold(sp, down_added, t * NE + (NE + 2))
                    sp.dma_start(out[bass.ds(t * P, P), :] if n == P else out[N - n:N, :], X[0:n, t, :]).then_inc(rows_out, 16)
                tiles(sp, step)
                sp.wait_ge(rows_out, T * 16)

            @block.vector
            def _(v):
                v.sem_inc(down_added, 2)

                def xn(t, b):
                    e.normalise(t, XS[:, b, :]).then_inc(xn_ready, 1)

                def step(t, b, n, j):
                    if n == P:
                        xn(t + 1, 1 - b)
                    for x in range(NE):
                        V.scalar_tensor_tensor(X[:, t, :], b2[:, x, :], gate[:, t, x:x + 1], X[:, t, :], ALU.mult, ALU.add)
                        v.drain()
                        hold(v, down_ready, t * NE + (x + 1))
                        V.scalar_tensor_tensor(X[:, t, :], psD[:, x % 2, 0:D], gate[:, t, x:x + 1], X[:, t, :], ALU.mult, ALU.add).then_inc(down_added, 1)
                        v.drain()
                xn(0, 0)
                hold(v, w_in, 16 * 4 * NE)
                tiles(v, step)

            @block.scalar
            def _(act):
                def ht(t, b):
                    act.wait_ge(tp_ready, t + 1)
                    S.activation(HT[:, b, :], psT[:, 0:D], ACT.Copy).then_inc(ht_ready, 1)

                def step(t, b, n, j):
                    for x in range(NE):
                        act.wait_ge(up_ready, t * NE + (x + 1))
                        for m in range(ME):
                            last = S.activation(GT[:, x % 2, m * P:(m + 1) * P], psU[:, x % 2, m * P:(m + 1) * P], ACT.Gelu, bias=b1[:, x, m:m + 1])
                        last.then_inc(gelu_ready, 1)
                        if x == 0 and n == P:
                            ht(t + 1, 1 - b)
                ht(0, 0)
                tiles(act, step)

            @block.tensor
            def _(pe):
                def turn(t, b):
                    pe.wait_ge(xn_ready, t + 1)
                    e.transpose_tile(psT[:, 0:D], XS[:, b, :]).then_inc(tp_ready, 1)

                def raise_up(t, b, x):
                    for m in range(ME):
                        at = psU[:, x % 2, m * P:(m + 1) * P]
                        for c in range(HALF):
                            last = nc.tensor.matmul(at, W1[:, c, x, m * P:(m + 1) * P], HT[:, b, c * P:(c + 1) * P], start=(c == 0), stop=(c == HALF - 1))
                    last.then_inc(up_ready, 1)

                def bring_down(t, x):
                    pe.wait_ge(down_added, t * NE + (x + 1))
                    pe.wait_ge(gelu_ready, t * NE + (x + 1))
                    for m in range(ME):
                        last = nc.tensor.matmul(psD[:, x % 2, 0:D], GT[:, x % 2, m * P:(m + 1) * P], W2[:, m, x, :], start=(m == 0), stop=(m == ME - 1))
                    last.then_inc(down_ready, 1)

                def step(t, b, n, j):
                    for x in range(NE):
                        if x + 1 < NE:
                            raise_up(t, b, x + 1)
                        elif n == P:
                            pe.wait_ge(ht_ready, t + 2)
                            raise_up(t + 1, 1 - b, 0)
                        if x == 0 and n == P:
                            turn(t + 1, 1 - b)
                        bring_down(t, x)
                pe.wait_ge(w_in, 16 * 4 * NE)
                turn(0, 0)
                pe.wait_ge(ht_ready, 1)
                raise_up(0, 0, 0)
                tiles(pe, step)


_INS = ["x", "src", "dst", "L0_gnn_W0", "L0_gnn_b0", "L0_gnn_W1", "L0_gnn_b1", "L0_gnn_gamma", "L0_gnn_beta",
        "L0_mix_Wq", "L0_mix_Wk", "L0_mix_Wv", "L0_mix_Wo", "L0_mix_bo", "L0_mix_ln1_g", "L0_mix_ln1_b",
        "L0_mix_W1", "L0_mix_b1", "L0_mix_W2", "L0_mix_b2", "L0_mix_ln2_g", "L0_mix_ln2_b",
        "L0_ffn_W_gat", "L0_ffn_att_src", "L0_ffn_att_dst", "L0_ffn_b_gat", "L0_ffn_ln_gamma", "L0_ffn_ln_beta",
        "L0_ffn_W1", "L0_ffn_b1", "L0_ffn_W2", "L0_ffn_b2", "L0_ffn_edge_index"]
NOWHERE = -128


def kernel(**inputs):
    import numpy as np
    import concourse.bacc as bacc
    from concourse.bass_utils import run_bass_kernel_spmd

    def grouped(flat, groups, columns, fill):
        room = np.full((groups * P * columns,), fill, np.int32)
        room[:flat.shape[0]] = flat
        return room.reshape(groups, P, columns)

    arrays = {k: np.ascontiguousarray(inputs[k]) for k in _INS}
    src, dst = arrays.pop("src"), arrays.pop("dst")
    ei = arrays.pop("L0_ffn_edge_index")
    arrays["gnn_end"] = np.concatenate([grouped(dst, GNN_G // 2, GNN_C, NOWHERE), grouped(src, GNN_G // 2, GNN_C, NOWHERE)])
    arrays["gnn_start"] = np.concatenate([grouped(src, GNN_G // 2, GNN_C, 0), grouped(dst, GNN_G // 2, GNN_C, 0)])
    arrays["gat_end"] = grouped(ei[1], GAT_G, GAT_C, NOWHERE)
    arrays["gat_start"] = grouped(ei[0], GAT_G, GAT_C, 0)

    nc = bacc.Bacc("TRN2", target_bir_lowering=False, num_devices=1)
    A = {k: nc.dram_tensor(k, a.shape, mybir.dt.from_np(a.dtype), kind="ExternalInput").ap() for k, a in arrays.items()}
    out = nc.dram_tensor("out", (N, D), f32, kind="ExternalOutput").ap()
    build(nc, A, out)
    r = run_bass_kernel_spmd(nc, [arrays], core_ids=[0])
    return r.results[0]["out"]
```
